# Optimizing a Trainium2 kernel written in Bass

```python
import numpy as np
import jax
import jax.numpy as jnp

def _softmax(x, axis=-1):
    return jax.nn.softmax(x, axis=axis)

def _gelu(x):
    return jax.nn.gelu(x, approximate=True)

def _silu(x):
    return jax.nn.silu(x)

def _sigmoid(x):
    return jax.nn.sigmoid(x)

def _layernorm(x, axis=-1, eps=1e-05):
    m = jnp.mean(x, axis=axis, keepdims=True)
    v = jnp.var(x, axis=axis, keepdims=True)
    return (x - m) / jnp.sqrt(v + eps)

def _scatter_add(tgt, idx, src, axis=0):
    return tgt.at[idx].add(src)

def _segment_sum(src, seg, n):
    return jax.ops.segment_sum(src, seg, n)
kernel_name = 'mk_audio_tower_d4_tok_audfeat256_r4_b6a925'

def setup_inputs(seed: int=0):
    np.random.seed(seed)
    _w = jnp.asarray

    def _rec_inputs():
        import jax
        import jax.numpy as jnp
        _rk = jax.random.key(seed)
        x = -0.00154741 + 1.00114 * jax.random.normal(jax.random.fold_in(_rk, 1), (64, 125, 32), jnp.float32)
        return x
    x = _rec_inputs()

    def _L0_tok_setup():
        import jax, jax.numpy as jnp
        import numpy as np
        import math
        D_LAT, D_MODEL, N_LAYERS, N_HEADS, D_FF, K = (32, 64, 2, 4, 256, 10)
        LN_EPS = 1e-05

        def _sinusoidal_pe(length, d):
            pos = jnp.arange(length, dtype=jnp.float32)[:, None]
            div = jnp.exp(jnp.arange(0, d, 2, dtype=jnp.float32) * (-math.log(10000.0) / d))
            ang = pos * div
            return jnp.stack([jnp.sin(ang), jnp.cos(ang)], axis=-1).reshape(length, d)

        def _layernorm(x, g, b):
            mu = jnp.mean(x, axis=-1, keepdims=True)
            var = jnp.mean(jnp.square(x - mu), axis=-1, keepdims=True)
            return (x - mu) * jax.lax.rsqrt(var + LN_EPS) * g + b
        key = jax.random.key(seed)
        ks = jax.random.split(key, 8)
        B, S = (16, 128)
        sc = 0.02
        inp = {}
        inp['x_clean'] = jax.random.normal(ks[0], (B, S, D_LAT), jnp.float32)
        inp['w_in'] = jax.random.normal(ks[1], (D_LAT, D_MODEL), jnp.float32) * sc
        inp['b_in'] = jnp.zeros((D_MODEL,), jnp.float32)
        inp['wqkv'] = jax.random.normal(ks[2], (N_LAYERS, D_MODEL, 3 * D_MODEL), jnp.float32) * sc
        inp['bqkv'] = jnp.zeros((N_LAYERS, 3 * D_MODEL), jnp.float32)
        inp['wo'] = jax.random.normal(ks[3], (N_LAYERS, D_MODEL, D_MODEL), jnp.float32) * sc
        inp['bo'] = jnp.zeros((N_LAYERS, D_MODEL), jnp.float32)
        inp['w1'] = jax.random.normal(ks[4], (N_LAYERS, D_MODEL, D_FF), jnp.float32) * sc
        inp['b1'] = jnp.zeros((N_LAYERS, D_FF), jnp.float32)
        inp['w2'] = jax.random.normal(ks[5], (N_LAYERS, D_FF, D_MODEL), jnp.float32) * sc
        inp['b2'] = jnp.zeros((N_LAYERS, D_MODEL), jnp.float32)
        inp['ln1_g'] = jnp.ones((N_LAYERS, D_MODEL), jnp.float32)
        inp['ln1_b'] = jnp.zeros((N_LAYERS, D_MODEL), jnp.float32)
        inp['ln2_g'] = jnp.ones((N_LAYERS, D_MODEL), jnp.float32)
        inp['ln2_b'] = jnp.zeros((N_LAYERS, D_MODEL), jnp.float32)
        inp['w_out'] = jax.random.normal(ks[6], (D_MODEL, D_MODEL), jnp.float32) * sc
        inp['b_out'] = jnp.zeros((D_MODEL,), jnp.float32)
        return inp
    _L0_tok_all = _L0_tok_setup()
    _L0_tok_in = {k: v for k, v in _L0_tok_all.items() if k in ('w_in', 'b_in', 'wqkv', 'bqkv', 'wo', 'bo', 'w1', 'b1', 'w2', 'b2', 'ln1_g', 'ln1_b', 'ln2_g', 'ln2_b', 'w_out', 'b_out')}
    del _L0_tok_all

    def _L0_attn_setup():
        import jax, jax.numpy as jnp
        import numpy as np
        DIM = 64
        NUM_HEADS = 8
        WINDOW = 7

        def _rel_bias(bias_table, seq_len):
            w = WINDOW
            coords = jnp.arange(w)
            idx = coords[:, None] - coords[None, :] + (w - 1)
            bias = bias_table[idx]
            if seq_len <= w:
                return bias[:seq_len, :seq_len]
            repeats = (seq_len + w - 1) // w
            bias = jnp.tile(bias, (repeats, repeats))[:seq_len, :seq_len]
            return bias
        key = jax.random.key(seed)
        ks = jax.random.split(key, 6)
        B, N, C = (4, 512, DIM)
        x = jax.random.normal(ks[0], (B, N, C), dtype=jnp.float32)
        qkv_w = jax.random.normal(ks[1], (3 * C, C), dtype=jnp.float32) * 0.02
        qkv_b = jax.random.normal(ks[2], (3 * C,), dtype=jnp.float32) * 0.02
        proj_w = jax.random.normal(ks[3], (C, C), dtype=jnp.float32) * 0.02
        proj_b = jax.random.normal(ks[4], (C,), dtype=jnp.float32) * 0.02
        bias_table = jax.random.normal(ks[5], ((2 * WINDOW - 1) * NUM_HEADS,), dtype=jnp.float32) * 0.02
        return {'x': x, 'qkv_w': qkv_w, 'qkv_b': qkv_b, 'proj_w': proj_w, 'proj_b': proj_b, 'bias_table': bias_table}
    _L0_attn_all = _L0_attn_setup()
    _L0_attn_in = {k: v for k, v in _L0_attn_all.items() if k in ('qkv_w', 'qkv_b', 'proj_w', 'proj_b', 'bias_table')}
    del _L0_attn_all

    def _L0_ffn_setup():
        import jax, jax.numpy as jnp
        import numpy as np
        B, S, H, F, E, K = (8, 1024, 64, 128, 16, 2)
        EPS = 1e-05
        key = jax.random.key(seed)
        ks = jax.random.split(key, 9)
        sc = 0.02
        return {'x': jax.random.normal(ks[0], (B, S, H), dtype=jnp.float32), 'gate_w': jax.random.normal(ks[1], (H, E), dtype=jnp.float32) * sc, 'gate_b': jnp.zeros((E,), dtype=jnp.float32), 'w1': jax.random.normal(ks[2], (E, H, F), dtype=jnp.float32) * sc, 'b1': jnp.zeros((E, F), dtype=jnp.float32), 'w2': jax.random.normal(ks[3], (E, F, H), dtype=jnp.float32) * sc, 'b2': jnp.zeros((E, H), dtype=jnp.float32), 'gamma': jnp.ones((H,), dtype=jnp.float32), 'beta': jnp.zeros((H,), dtype=jnp.float32)}
    _L0_ffn_all = _L0_ffn_setup()
    _L0_ffn_in = {k: v for k, v in _L0_ffn_all.items() if k in ('gate_w', 'gate_b', 'w1', 'b1', 'w2', 'b2', 'gamma', 'beta')}
    del _L0_ffn_all

    def _L1_attn_setup():
        import jax, jax.numpy as jnp
        import numpy as np
        B, N, C, H = (64, 75, 64, 8)
        STD = 0.02

        def _rel_indices(n):
            d = (jnp.arange(n)[None, :] - jnp.arange(n)[:, None]).astype(jnp.float32)
            return jnp.stack([d, jnp.zeros_like(d), d * d], axis=-1)
        key = jax.random.key(seed)
        ks = jax.random.split(key, 6)
        return {'x': jax.random.normal(ks[0], (B, N, C), jnp.float32), 'Wqk': jax.random.normal(ks[1], (2 * C, C), jnp.float32) * STD, 'Wv': jax.random.normal(ks[2], (C, C), jnp.float32) * STD, 'Wpos': jax.random.normal(ks[3], (H, 3), jnp.float32) * STD, 'bpos': jnp.zeros((H,), jnp.float32), 'Wproj': jax.random.normal(ks[4], (C, C), jnp.float32) * STD, 'bproj': jnp.zeros((C,), jnp.float32), 'gating': jnp.ones((H,), jnp.float32)}
    _L1_attn_all = _L1_attn_setup()
    _L1_attn_in = {k: v for k, v in _L1_attn_all.items() if k in ('Wqk', 'Wv', 'Wpos', 'bpos', 'Wproj', 'bproj', 'gating')}
    del _L1_attn_all

    def _L1_ffn_setup():
        import jax, jax.numpy as jnp
        import numpy as np
        D_IN, D_HID, D_OUT = (64, 128, 64)
        N_EXPERTS, TOP_K = (64, 2)
        B, S = (8, 1024)
        key = jax.random.key(seed)
        ks = jax.random.split(key, 8)
        scale_in = 1.0 / np.sqrt(D_IN)
        scale_hid = 1.0 / np.sqrt(D_HID)
        return {'x': jax.random.normal(ks[0], (B, S, D_IN), dtype=jnp.float32), 'Wr': jax.random.uniform(ks[1], (D_IN, N_EXPERTS), jnp.float32, -scale_in, scale_in), 'br': jax.random.uniform(ks[2], (N_EXPERTS,), jnp.float32, -scale_in, scale_in), 'W1': jax.random.uniform(ks[3], (N_EXPERTS, D_IN, D_HID), jnp.float32, -scale_in, scale_in), 'b1': jax.random.uniform(ks[4], (N_EXPERTS, D_HID), jnp.float32, -scale_in, scale_in), 'W2': jax.random.uniform(ks[5], (N_EXPERTS, D_HID, D_OUT), jnp.float32, -scale_hid, scale_hid), 'b2': jax.random.uniform(ks[6], (N_EXPERTS, D_OUT), jnp.float32, -scale_hid, scale_hid)}
    _L1_ffn_all = _L1_ffn_setup()
    _L1_ffn_in = {k: v for k, v in _L1_ffn_all.items() if k in ('Wr', 'br', 'W1', 'b1', 'W2', 'b2')}
    del _L1_ffn_all

    def _L2_attn_setup():
        import jax, jax.numpy as jnp
        import numpy as np
        import math
        D = 64
        K = 32
        B = 2
        L = 512
        MAX_SEQ = 2048
        PI = math.pi

        def _content_stream(x, Wk1, bk1, Wk2, bk2, Wq1, bq1, Wq2, bq2, Wvc, bvc):
            Bc, Lc, Dc = x.shape
            key_phase = jnp.tanh(jnp.tanh(x @ Wk1 + bk1) @ Wk2 + bk2) * PI
            query_phase = jnp.tanh(jnp.tanh(x @ Wq1 + bq1) @ Wq2 + bq2) * PI
            value = x @ Wvc + bvc
            cos_k = jnp.cos(key_phase)[..., None]
            sin_k = jnp.sin(key_phase)[..., None]
            v_e = value[:, :, None, :]
            mem_real = jnp.cumsum(cos_k * v_e, axis=1)
            mem_imag = jnp.cumsum(sin_k * v_e, axis=1)
            cos_q = jnp.cos(query_phase)[..., None]
            sin_q = jnp.sin(query_phase)[..., None]
            retrieved = (mem_real * cos_q + mem_imag * sin_q).sum(axis=2)
            positions = jnp.arange(1, Lc + 1, dtype=jnp.float32)
            norm = jnp.sqrt(positions * K)[None, :, None]
            return retrieved / norm

        def _pos_stream(x, base_phases, Wvp, bvp):
            Bc, Lc, Dc = x.shape
            phases = base_phases[:Lc][None]
            value = x @ Wvp + bvp
            cos_p = jnp.cos(phases)
            sin_p = jnp.sin(phases)
            mem_real = jnp.cumsum(value * cos_p, axis=1)
            mem_imag = jnp.cumsum(value * sin_p, axis=1)
            retrieved = mem_real * cos_p + mem_imag * sin_p
            positions = jnp.arange(1, Lc + 1, dtype=jnp.float32)
            return retrieved / jnp.sqrt(positions)[None, :, None]
        key = jax.random.key(seed)
        ks = jax.random.split(key, 24)
        s = 0.02
        inp = {}
        inp['x'] = jax.random.normal(ks[0], (B, L, D), dtype=jnp.float32)
        inp['base_phases'] = jax.random.normal(ks[1], (MAX_SEQ, D), dtype=jnp.float32) * PI
        inp['Wk1'] = jax.random.normal(ks[2], (D, D), dtype=jnp.float32) * s
        inp['bk1'] = jnp.zeros((D,), jnp.float32)
        inp['Wk2'] = jax.random.normal(ks[3], (D, K), dtype=jnp.float32) * s
        inp['bk2'] = jnp.zeros((K,), jnp.float32)
        inp['Wq1'] = jax.random.normal(ks[4], (D, D), dtype=jnp.float32) * s
        inp['bq1'] = jnp.zeros((D,), jnp.float32)
        inp['Wq2'] = jax.random.normal(ks[5], (D, K), dtype=jnp.float32) * s
        inp['bq2'] = jnp.zeros((K,), jnp.float32)
        inp['Wvc'] = jax.random.normal(ks[6], (D, D), dtype=jnp.float32) * s
        inp['bvc'] = jnp.zeros((D,), jnp.float32)
        inp['Wvp'] = jax.random.normal(ks[7], (D, D), dtype=jnp.float32) * s
        inp['bvp'] = jnp.zeros((D,), jnp.float32)
        inp['Wg1'] = jax.random.normal(ks[8], (D, D // 4), dtype=jnp.float32) * s
        inp['bg1'] = jnp.zeros((D // 4,), jnp.float32)
        inp['Wg2'] = jax.random.normal(ks[9], (D // 4, 2), dtype=jnp.float32) * s
        inp['bg2'] = jnp.zeros((2,), jnp.float32)
        inp['ln_g'] = jnp.ones((D,), jnp.float32)
        inp['ln_b'] = jnp.zeros((D,), jnp.float32)
        inp['Wo'] = jax.random.normal(ks[10], (D, D), dtype=jnp.float32) * s
        inp['bo'] = jnp.zeros((D,), jnp.float32)
        return inp
    _L2_attn_all = _L2_attn_setup()
    _L2_attn_in = {k: v for k, v in _L2_attn_all.items() if k in ('base_phases', 'Wk1', 'bk1', 'Wk2', 'bk2', 'Wq1', 'bq1', 'Wq2', 'bq2', 'Wvc', 'bvc', 'Wvp', 'bvp', 'Wg1', 'bg1', 'Wg2', 'bg2', 'ln_g', 'ln_b', 'Wo', 'bo')}
    del _L2_attn_all

    def _L2_ffn_setup():
        import jax, jax.numpy as jnp
        import numpy as np
        B, S, H, NH, NE = (4, 256, 64, 4, 4)
        D = H // NH
        EPS = 1e-08

        def layernorm(x, g, b):
            m = jnp.mean(x, axis=-1, keepdims=True)
            v = jnp.mean((x - m) ** 2, axis=-1, keepdims=True)
            return (x - m) / jnp.sqrt(v + EPS) * g + b
        key = jax.random.key(seed)
        ks = jax.random.split(key, 18)
        sc = 0.05
        return {'x': jax.random.normal(ks[0], (B, S, H), jnp.float32), 'hl_w': jax.random.normal(ks[1], (NH, D, H), jnp.float32) * sc, 'hl_b': jax.random.normal(ks[2], (NH, D), jnp.float32) * sc, 'wq': jax.random.normal(ks[3], (NH, NE, D, D), jnp.float32) * sc, 'wk': jax.random.normal(ks[4], (NH, D, D), jnp.float32) * sc, 'wv': jax.random.normal(ks[5], (NH, D, D), jnp.float32) * sc, 'gate_w': jax.random.normal(ks[6], (NH, NE, NE * D), jnp.float32) * sc, 'gate_b': jax.random.normal(ks[7], (NH, NE), jnp.float32) * sc, 'ln_g': jnp.ones((D,), jnp.float32), 'ln_b': jnp.zeros((D,), jnp.float32), 'fc1_w': jax.random.normal(ks[8], (D, D), jnp.float32) * sc, 'fc1_b': jax.random.normal(ks[9], (D,), jnp.float32) * sc, 'fc2_w': jax.random.normal(ks[10], (D, D), jnp.float32) * sc, 'fc2_b': jax.random.normal(ks[11], (D,), jnp.float32) * sc, 'fnorm_g': jnp.ones((D,), jnp.float32), 'fnorm_b': jnp.zeros((D,), jnp.float32), 'fgate_w': jax.random.normal(ks[12], (NH, H), jnp.float32) * sc}
    _L2_ffn_all = _L2_ffn_setup()
    _L2_ffn_in = {k: v for k, v in _L2_ffn_all.items() if k in ('hl_w', 'hl_b', 'wq', 'wk', 'wv', 'gate_w', 'gate_b', 'ln_g', 'ln_b', 'fc1_w', 'fc1_b', 'fc2_w', 'fc2_b', 'fnorm_g', 'fnorm_b', 'fgate_w')}
    del _L2_ffn_all

    def _L3_attn_setup():
        import jax, jax.numpy as jnp
        import numpy as np
        import math
        D_MODEL = 64
        NHEAD = 8
        D_LATTICE = 512
        D_K = D_LATTICE // NHEAD
        PHI = (1.0 + math.sqrt(5.0)) / 2.0
        PHI_INV = 1.0 / PHI
        PHI_INT = 1618.0
        C1 = PHI * math.sqrt(2.0) * 51.85
        C2 = math.pi / PHI

        def qrt_damping(x):
            return jnp.sin(C1 * x) * jnp.exp(-(x * x) / PHI) + jnp.cos(C2 * x)

        def ttt_filter(scores):
            int_scores = (jnp.abs(scores) * PHI_INT).astype(jnp.int32)
            mod9 = int_scores % 9
            chaos = (mod9 == 0) | (mod9 == 3) | (mod9 == 6)
            penalty = jnp.where(chaos, jnp.float32(PHI_INV), jnp.float32(1.0))
            return scores * penalty
        key = jax.random.key(seed)
        ks = jax.random.split(key, 9)
        B, S = (2, 512)
        s_in = 1.0 / math.sqrt(D_MODEL)
        s_lat = 1.0 / math.sqrt(D_LATTICE)
        return {'x': jax.random.normal(ks[0], (B, S, D_MODEL), dtype=jnp.float32), 'Wq': jax.random.normal(ks[1], (D_MODEL, D_LATTICE), dtype=jnp.float32) * s_in, 'bq': jax.random.normal(ks[2], (D_LATTICE,), dtype=jnp.float32) * 0.01, 'Wk': jax.random.normal(ks[3], (D_MODEL, D_LATTICE), dtype=jnp.float32) * s_in, 'bk': jax.random.normal(ks[4], (D_LATTICE,), dtype=jnp.float32) * 0.01, 'Wv': jax.random.normal(ks[5], (D_MODEL, D_LATTICE), dtype=jnp.float32) * s_in, 'bv': jax.random.normal(ks[6], (D_LATTICE,), dtype=jnp.float32) * 0.01, 'Wo': jax.random.normal(ks[7], (D_LATTICE, D_MODEL), dtype=jnp.float32) * s_lat, 'bo': jax.random.normal(ks[8], (D_MODEL,), dtype=jnp.float32) * 0.01}
    _L3_attn_all = _L3_attn_setup()
    _L3_attn_in = {k: v for k, v in _L3_attn_all.items() if k in ('Wq', 'bq', 'Wk', 'bk', 'Wv', 'bv', 'Wo', 'bo')}
    del _L3_attn_all

    def _L3_ffn_setup():
        import jax, jax.numpy as jnp
        import numpy as np
        INPUT_WIDTH = 64
        DEPTH = 7
        OUTPUT_WIDTH = 64
        N_NODES = 2 ** (DEPTH + 1) - 1
        key = jax.random.key(seed)
        k_x, k_w1, k_w2 = jax.random.split(key, 3)
        init1 = 1.0 / np.sqrt(INPUT_WIDTH)
        x = jax.random.normal(k_x, (2, 256, INPUT_WIDTH), dtype=jnp.float32)
        w1s = jax.random.uniform(k_w1, (N_NODES, INPUT_WIDTH), jnp.float32, -init1, init1)
        b1s = jnp.zeros((N_NODES,), jnp.float32)
        w2s = jax.random.uniform(k_w2, (N_NODES, INPUT_WIDTH, OUTPUT_WIDTH), jnp.float32, -init1, init1)
        b2s = jnp.zeros((N_NODES, OUTPUT_WIDTH), jnp.float32)
        return {'x': x, 'w1s': w1s, 'b1s': b1s, 'w2s': w2s, 'b2s': b2s}
    _L3_ffn_all = _L3_ffn_setup()
    _L3_ffn_in = {k: v for k, v in _L3_ffn_all.items() if k in ('w1s', 'b1s', 'w2s', 'b2s')}
    del _L3_ffn_all
    return {'x': x, 'L0_tok_w_in': _L0_tok_in['w_in'], 'L0_tok_b_in': _L0_tok_in['b_in'], 'L0_tok_wqkv': _L0_tok_in['wqkv'], 'L0_tok_bqkv': _L0_tok_in['bqkv'], 'L0_tok_wo': _L0_tok_in['wo'], 'L0_tok_bo': _L0_tok_in['bo'], 'L0_tok_w1': _L0_tok_in['w1'], 'L0_tok_b1': _L0_tok_in['b1'], 'L0_tok_w2': _L0_tok_in['w2'], 'L0_tok_b2': _L0_tok_in['b2'], 'L0_tok_ln1_g': _L0_tok_in['ln1_g'], 'L0_tok_ln1_b': _L0_tok_in['ln1_b'], 'L0_tok_ln2_g': _L0_tok_in['ln2_g'], 'L0_tok_ln2_b': _L0_tok_in['ln2_b'], 'L0_tok_w_out': _L0_tok_in['w_out'], 'L0_tok_b_out': _L0_tok_in['b_out'], 'L0_attn_qkv_w': _L0_attn_in['qkv_w'], 'L0_attn_qkv_b': _L0_attn_in['qkv_b'], 'L0_attn_proj_w': _L0_attn_in['proj_w'], 'L0_attn_proj_b': _L0_attn_in['proj_b'], 'L0_attn_bias_table': _L0_attn_in['bias_table'], 'L0_ffn_gate_w': _L0_ffn_in['gate_w'], 'L0_ffn_gate_b': _L0_ffn_in['gate_b'], 'L0_ffn_w1': _L0_ffn_in['w1'], 'L0_ffn_b1': _L0_ffn_in['b1'], 'L0_ffn_w2': _L0_ffn_in['w2'], 'L0_ffn_b2': _L0_ffn_in['b2'], 'L0_ffn_gamma': _L0_ffn_in['gamma'], 'L0_ffn_beta': _L0_ffn_in['beta'], 'L1_attn_Wqk': _L1_attn_in['Wqk'], 'L1_attn_Wv': _L1_attn_in['Wv'], 'L1_attn_Wpos': _L1_attn_in['Wpos'], 'L1_attn_bpos': _L1_attn_in['bpos'], 'L1_attn_Wproj': _L1_attn_in['Wproj'], 'L1_attn_bproj': _L1_attn_in['bproj'], 'L1_attn_gating': _L1_attn_in['gating'], 'L1_ffn_Wr': _L1_ffn_in['Wr'], 'L1_ffn_br': _L1_ffn_in['br'], 'L1_ffn_W1': _L1_ffn_in['W1'], 'L1_ffn_b1': _L1_ffn_in['b1'], 'L1_ffn_W2': _L1_ffn_in['W2'], 'L1_ffn_b2': _L1_ffn_in['b2'], 'L2_attn_base_phases': _L2_attn_in['base_phases'], 'L2_attn_Wk1': _L2_attn_in['Wk1'], 'L2_attn_bk1': _L2_attn_in['bk1'], 'L2_attn_Wk2': _L2_attn_in['Wk2'], 'L2_attn_bk2': _L2_attn_in['bk2'], 'L2_attn_Wq1': _L2_attn_in['Wq1'], 'L2_attn_bq1': _L2_attn_in['bq1'], 'L2_attn_Wq2': _L2_attn_in['Wq2'], 'L2_attn_bq2': _L2_attn_in['bq2'], 'L2_attn_Wvc': _L2_attn_in['Wvc'], 'L2_attn_bvc': _L2_attn_in['bvc'], 'L2_attn_Wvp': _L2_attn_in['Wvp'], 'L2_attn_bvp': _L2_attn_in['bvp'], 'L2_attn_Wg1': _L2_attn_in['Wg1'], 'L2_attn_bg1': _L2_attn_in['bg1'], 'L2_attn_Wg2': _L2_attn_in['Wg2'], 'L2_attn_bg2': _L2_attn_in['bg2'], 'L2_attn_ln_g': _L2_attn_in['ln_g'], 'L2_attn_ln_b': _L2_attn_in['ln_b'], 'L2_attn_Wo': _L2_attn_in['Wo'], 'L2_attn_bo': _L2_attn_in['bo'], 'L2_ffn_hl_w': _L2_ffn_in['hl_w'], 'L2_ffn_hl_b': _L2_ffn_in['hl_b'], 'L2_ffn_wq': _L2_ffn_in['wq'], 'L2_ffn_wk': _L2_ffn_in['wk'], 'L2_ffn_wv': _L2_ffn_in['wv'], 'L2_ffn_gate_w': _L2_ffn_in['gate_w'], 'L2_ffn_gate_b': _L2_ffn_in['gate_b'], 'L2_ffn_ln_g': _L2_ffn_in['ln_g'], 'L2_ffn_ln_b': _L2_ffn_in['ln_b'], 'L2_ffn_fc1_w': _L2_ffn_in['fc1_w'], 'L2_ffn_fc1_b': _L2_ffn_in['fc1_b'], 'L2_ffn_fc2_w': _L2_ffn_in['fc2_w'], 'L2_ffn_fc2_b': _L2_ffn_in['fc2_b'], 'L2_ffn_fnorm_g': _L2_ffn_in['fnorm_g'], 'L2_ffn_fnorm_b': _L2_ffn_in['fnorm_b'], 'L2_ffn_fgate_w': _L2_ffn_in['fgate_w'], 'L3_attn_Wq': _L3_attn_in['Wq'], 'L3_attn_bq': _L3_attn_in['bq'], 'L3_attn_Wk': _L3_attn_in['Wk'], 'L3_attn_bk': _L3_attn_in['bk'], 'L3_attn_Wv': _L3_attn_in['Wv'], 'L3_attn_bv': _L3_attn_in['bv'], 'L3_attn_Wo': _L3_attn_in['Wo'], 'L3_attn_bo': _L3_attn_in['bo'], 'L3_ffn_w1s': _L3_ffn_in['w1s'], 'L3_ffn_b1s': _L3_ffn_in['b1s'], 'L3_ffn_w2s': _L3_ffn_in['w2s'], 'L3_ffn_b2s': _L3_ffn_in['b2s']}

def reference(x, L0_tok_w_in, L0_tok_b_in, L0_tok_wqkv, L0_tok_bqkv, L0_tok_wo, L0_tok_bo, L0_tok_w1, L0_tok_b1, L0_tok_w2, L0_tok_b2, L0_tok_ln1_g, L0_tok_ln1_b, L0_tok_ln2_g, L0_tok_ln2_b, L0_tok_w_out, L0_tok_b_out, L0_attn_qkv_w, L0_attn_qkv_b, L0_attn_proj_w, L0_attn_proj_b, L0_attn_bias_table, L0_ffn_gate_w, L0_ffn_gate_b, L0_ffn_w1, L0_ffn_b1, L0_ffn_w2, L0_ffn_b2, L0_ffn_gamma, L0_ffn_beta, L1_attn_Wqk, L1_attn_Wv, L1_attn_Wpos, L1_attn_bpos, L1_attn_Wproj, L1_attn_bproj, L1_attn_gating, L1_ffn_Wr, L1_ffn_br, L1_ffn_W1, L1_ffn_b1, L1_ffn_W2, L1_ffn_b2, L2_attn_base_phases, L2_attn_Wk1, L2_attn_bk1, L2_attn_Wk2, L2_attn_bk2, L2_attn_Wq1, L2_attn_bq1, L2_attn_Wq2, L2_attn_bq2, L2_attn_Wvc, L2_attn_bvc, L2_attn_Wvp, L2_attn_bvp, L2_attn_Wg1, L2_attn_bg1, L2_attn_Wg2, L2_attn_bg2, L2_attn_ln_g, L2_attn_ln_b, L2_attn_Wo, L2_attn_bo, L2_ffn_hl_w, L2_ffn_hl_b, L2_ffn_wq, L2_ffn_wk, L2_ffn_wv, L2_ffn_gate_w, L2_ffn_gate_b, L2_ffn_ln_g, L2_ffn_ln_b, L2_ffn_fc1_w, L2_ffn_fc1_b, L2_ffn_fc2_w, L2_ffn_fc2_b, L2_ffn_fnorm_g, L2_ffn_fnorm_b, L2_ffn_fgate_w, L3_attn_Wq, L3_attn_bq, L3_attn_Wk, L3_attn_bk, L3_attn_Wv, L3_attn_bv, L3_attn_Wo, L3_attn_bo, L3_ffn_w1s, L3_ffn_b1s, L3_ffn_w2s, L3_ffn_b2s):
    import jax
    import jax.numpy as jnp

    def _L0_tok_ref(x_clean, w_in, b_in, wqkv, bqkv, wo, bo, w1, b1, w2, b2, ln1_g, ln1_b, ln2_g, ln2_b, w_out, b_out):
        import jax, jax.numpy as jnp
        import numpy as np
        import math
        D_LAT, D_MODEL, N_LAYERS, N_HEADS, D_FF, K = (32, 64, 2, 4, 256, 10)
        LN_EPS = 1e-05

        def _sinusoidal_pe(length, d):
            pos = jnp.arange(length, dtype=jnp.float32)[:, None]
            div = jnp.exp(jnp.arange(0, d, 2, dtype=jnp.float32) * (-math.log(10000.0) / d))
            ang = pos * div
            return jnp.stack([jnp.sin(ang), jnp.cos(ang)], axis=-1).reshape(length, d)

        def _layernorm(x, g, b):
            mu = jnp.mean(x, axis=-1, keepdims=True)
            var = jnp.mean(jnp.square(x - mu), axis=-1, keepdims=True)
            return (x - mu) * jax.lax.rsqrt(var + LN_EPS) * g + b
        B, S, D = x_clean.shape
        P = S - 1
        positions = jnp.arange(1, S)
        idx = positions[:, None] - K + jnp.arange(K)[None, :]
        valid = (idx >= 0).astype(x_clean.dtype)
        win = x_clean[:, jnp.clip(idx, 0)] * valid[None, :, :, None]
        h = win.reshape(B * P, K, D) @ w_in + b_in
        h = h + _sinusoidal_pe(K, D_MODEL)[None]
        dh = D_MODEL // N_HEADS
        neg_inf = jnp.asarray(-jnp.inf, h.dtype)
        causal = jnp.where(jnp.tril(jnp.ones((K, K), bool)), 0.0, neg_inf)
        N = B * P
        for l in range(N_LAYERS):
            hn = _layernorm(h, ln1_g[l], ln1_b[l])
            qkv = hn @ wqkv[l] + bqkv[l]
            q, k, v = jnp.split(qkv, 3, axis=-1)
            q = q.reshape(N, K, N_HEADS, dh)
            k = k.reshape(N, K, N_HEADS, dh)
            v = v.reshape(N, K, N_HEADS, dh)
            scores = jnp.einsum('nqhd,nkhd->nhqk', q, k) / jnp.sqrt(jnp.asarray(dh, h.dtype))
            attn = jax.nn.softmax(scores + causal, axis=-1)
            o = jnp.einsum('nhqk,nkhd->nqhd', attn, v).reshape(N, K, D_MODEL)
            h = h + o @ wo[l] + bo[l]
            hn = _layernorm(h, ln2_g[l], ln2_b[l])
            h = h + jax.nn.gelu(hn @ w1[l] + b1[l], approximate=False) @ w2[l] + b2[l]
        z = h[:, -1] @ w_out + b_out
        return z.reshape(B, P, D_MODEL)

    def _L0_attn_ref(x, qkv_w, qkv_b, proj_w, proj_b, bias_table):
        import jax, jax.numpy as jnp
        import numpy as np
        DIM = 64
        NUM_HEADS = 8
        WINDOW = 7

        def _rel_bias(bias_table, seq_len):
            w = WINDOW
            coords = jnp.arange(w)
            idx = coords[:, None] - coords[None, :] + (w - 1)
            bias = bias_table[idx]
            if seq_len <= w:
                return bias[:seq_len, :seq_len]
            repeats = (seq_len + w - 1) // w
            bias = jnp.tile(bias, (repeats, repeats))[:seq_len, :seq_len]
            return bias
        B, N, C = x.shape
        H, hd = (NUM_HEADS, C // NUM_HEADS)
        qkv = x @ qkv_w.T + qkv_b
        qkv = qkv.reshape(B, N, 3, H, hd).transpose(2, 0, 3, 1, 4)
        q, k, v = (qkv[0], qkv[1], qkv[2])
        scale = hd ** (-0.5)
        attn = jnp.einsum('bhnd,bhmd->bhnm', q, k) * scale
        bias = _rel_bias(bias_table, N)
        attn = attn + bias[None, None, :, :]
        attn = jax.nn.softmax(attn, axis=-1)
        out = jnp.einsum('bhnm,bhmd->bhnd', attn, v)
        out = out.transpose(0, 2, 1, 3).reshape(B, N, C)
        return out @ proj_w.T + proj_b

    def _L0_ffn_ref(x, gate_w, gate_b, w1, b1, w2, b2, gamma, beta):
        import jax, jax.numpy as jnp
        import numpy as np
        B, S, H, F, E, K = (8, 1024, 64, 128, 16, 2)
        EPS = 1e-05
        gate_logits = x @ gate_w + gate_b
        topk_vals, topk_idx = jax.lax.top_k(gate_logits, K)
        topk_w = jax.nn.softmax(topk_vals, axis=-1)
        h = jax.nn.relu(jnp.einsum('bsh,ehf->bsef', x, w1) + b1)
        expert_out = jnp.einsum('bsef,efh->bseh', h, w2) + b2
        sel = jnp.take_along_axis(expert_out, topk_idx[:, :, :, None], axis=2)
        moe = jnp.sum(topk_w[..., None] * sel, axis=2)
        y = x + moe
        mu = jnp.mean(y, axis=-1, keepdims=True)
        var = jnp.var(y, axis=-1, keepdims=True)
        return (y - mu) / jnp.sqrt(var + EPS) * gamma + beta

    def _L1_attn_ref(x, Wqk, Wv, Wpos, bpos, Wproj, bproj, gating):
        import jax, jax.numpy as jnp
        import numpy as np
        B, N, C, H = (64, 75, 64, 8)
        STD = 0.02

        def _rel_indices(n):
            d = (jnp.arange(n)[None, :] - jnp.arange(n)[:, None]).astype(jnp.float32)
            return jnp.stack([d, jnp.zeros_like(d), d * d], axis=-1)
        Bb, Nn, Cc = x.shape
        Hh = gating.shape[0]
        hd = Cc // Hh
        scale = hd ** (-0.5)
        qk = (x @ Wqk.T).reshape(Bb, Nn, 2, Hh, hd)
        q = qk[:, :, 0].transpose(0, 2, 1, 3)
        k = qk[:, :, 1].transpose(0, 2, 1, 3)
        patch_score = jax.nn.softmax(jnp.einsum('bhnd,bhmd->bhnm', q, k) * scale, axis=-1)
        rel = _rel_indices(Nn)
        pos_score = (rel @ Wpos.T + bpos).transpose(2, 0, 1)
        pos_score = jax.nn.softmax(pos_score, axis=-1)
        g = jax.nn.sigmoid(gating)[None, :, None, None]
        attn = (1.0 - g) * patch_score + g * pos_score[None]
        attn = attn / attn.sum(axis=-1, keepdims=True)
        v = (x @ Wv.T).reshape(Bb, Nn, Hh, hd).transpose(0, 2, 1, 3)
        out = jnp.einsum('bhnm,bhmd->bhnd', attn, v)
        out = out.transpose(0, 2, 1, 3).reshape(Bb, Nn, Cc)
        return out @ Wproj.T + bproj

    def _L1_ffn_ref(x, Wr, br, W1, b1, W2, b2):
        import jax, jax.numpy as jnp
        import numpy as np
        D_IN, D_HID, D_OUT = (64, 128, 64)
        N_EXPERTS, TOP_K = (64, 2)
        B, S = (8, 1024)
        Bx, Sx, D = x.shape
        xf = x.reshape(-1, D)
        T = xf.shape[0]
        E = Wr.shape[1]
        logits = xf @ Wr + br
        topk_logits, topk_idx = jax.lax.top_k(logits, TOP_K)
        gates = jax.nn.softmax(topk_logits, axis=1)
        combine = jnp.zeros((T, E), xf.dtype).at[jnp.arange(T)[:, None], topk_idx].add(gates)
        out = jnp.zeros((T, W2.shape[-1]), xf.dtype)
        for e in range(E):
            h = jax.nn.relu(xf @ W1[e] + b1[e])
            y = h @ W2[e] + b2[e]
            out = out + combine[:, e:e + 1] * y
        return out.reshape(Bx, Sx, -1)

    def _L2_attn_ref(x, base_phases, Wk1, bk1, Wk2, bk2, Wq1, bq1, Wq2, bq2, Wvc, bvc, Wvp, bvp, Wg1, bg1, Wg2, bg2, ln_g, ln_b, Wo, bo):
        import jax, jax.numpy as jnp
        import numpy as np
        import math
        D = 64
        K = 32
        B = 2
        L = 512
        MAX_SEQ = 2048
        PI = math.pi

        def _content_stream(x, Wk1, bk1, Wk2, bk2, Wq1, bq1, Wq2, bq2, Wvc, bvc):
            Bc, Lc, Dc = x.shape
            key_phase = jnp.tanh(jnp.tanh(x @ Wk1 + bk1) @ Wk2 + bk2) * PI
            query_phase = jnp.tanh(jnp.tanh(x @ Wq1 + bq1) @ Wq2 + bq2) * PI
            value = x @ Wvc + bvc
            cos_k = jnp.cos(key_phase)[..., None]
            sin_k = jnp.sin(key_phase)[..., None]
            v_e = value[:, :, None, :]
            mem_real = jnp.cumsum(cos_k * v_e, axis=1)
            mem_imag = jnp.cumsum(sin_k * v_e, axis=1)
            cos_q = jnp.cos(query_phase)[..., None]
            sin_q = jnp.sin(query_phase)[..., None]
            retrieved = (mem_real * cos_q + mem_imag * sin_q).sum(axis=2)
            positions = jnp.arange(1, Lc + 1, dtype=jnp.float32)
            norm = jnp.sqrt(positions * K)[None, :, None]
            return retrieved / norm

        def _pos_stream(x, base_phases, Wvp, bvp):
            Bc, Lc, Dc = x.shape
            phases = base_phases[:Lc][None]
            value = x @ Wvp + bvp
            cos_p = jnp.cos(phases)
            sin_p = jnp.sin(phases)
            mem_real = jnp.cumsum(value * cos_p, axis=1)
            mem_imag = jnp.cumsum(value * sin_p, axis=1)
            retrieved = mem_real * cos_p + mem_imag * sin_p
            positions = jnp.arange(1, Lc + 1, dtype=jnp.float32)
            return retrieved / jnp.sqrt(positions)[None, :, None]
        pos_retrieved = _pos_stream(x, base_phases, Wvp, bvp)
        content_retrieved = _content_stream(x, Wk1, bk1, Wk2, bk2, Wq1, bq1, Wq2, bq2, Wvc, bvc)
        gates = jax.nn.softmax(jax.nn.relu(x @ Wg1 + bg1) @ Wg2 + bg2, axis=-1)
        combined = gates[:, :, 0:1] * pos_retrieved + gates[:, :, 1:2] * content_retrieved
        mu = combined.mean(axis=-1, keepdims=True)
        var = ((combined - mu) ** 2).mean(axis=-1, keepdims=True)
        normed = (combined - mu) / jnp.sqrt(var + 1e-05) * ln_g + ln_b
        return x + normed @ Wo + bo

    def _L2_ffn_ref(x, hl_w, hl_b, wq, wk, wv, gate_w, gate_b, ln_g, ln_b, fc1_w, fc1_b, fc2_w, fc2_b, fnorm_g, fnorm_b, fgate_w):
        import jax, jax.numpy as jnp
        import numpy as np
        B, S, H, NH, NE = (4, 256, 64, 4, 4)
        D = H // NH
        EPS = 1e-08

        def layernorm(x, g, b):
            m = jnp.mean(x, axis=-1, keepdims=True)
            v = jnp.mean((x - m) ** 2, axis=-1, keepdims=True)
            return (x - m) / jnp.sqrt(v + EPS) * g + b
        b, s, h = x.shape
        nh, d, _ = wk.shape
        ne = wq.shape[1]
        sx = jnp.einsum('bsh,ndh->bnsd', x, hl_w) + hl_b[None, :, None, :]
        pad = sx == 0
        q = jnp.einsum('bnsd,neod->bneso', sx, wq)
        k = jnp.einsum('bnsd,nod->bnso', sx, wk)
        v = jnp.einsum('bnsd,nod->bnso', sx, wv)
        causal = jnp.where(jnp.tril(jnp.ones((s, s), bool)), 0.0, -jnp.inf).astype(x.dtype)
        scores = jnp.einsum('bnesd,bntd->bnest', q, k) * d ** 0.5 + causal
        att = jax.nn.softmax(scores, axis=-1)
        qkv = jnp.einsum('bnest,bntd->bnesd', att, v)
        qkv = jnp.where(pad[:, :, None], 0.0, qkv)
        out = jnp.transpose(qkv, (0, 1, 3, 2, 4)).reshape(b, nh, s, ne * d)
        gs = jax.nn.softmax(jnp.einsum('bnsf,nef->bnse', out, gate_w) + gate_b[None, :, None, :], axis=-1)
        mixed = jnp.einsum('bnsed,bnse->bnsd', out.reshape(b, nh, s, ne, d), gs)
        resid = sx[jnp.arange(nh), jnp.arange(nh)]
        hn = layernorm(mixed + resid, ln_g, ln_b)
        f_n = jnp.transpose(hn, (0, 2, 1, 3)).reshape(b, s, h)
        fx = f_n.reshape(b, s, nh, d)
        pm = fx == 0
        hx = jnp.where(pm, 0.0, fx @ fc1_w.T + fc1_b)
        hx = jax.nn.relu(hx)
        hx = jnp.where(pm, 0.0, hx @ fc2_w.T + fc2_b)
        hx = layernorm(hx + fx, fnorm_g, fnorm_b)
        fout = hx.reshape(b, s, h)
        fg = jax.nn.softmax(fout @ fgate_w.T, axis=-1)
        return (fout.reshape(b, s, nh, d) * fg[..., None]).reshape(b, s, h)

    def _L3_attn_ref(x, Wq, bq, Wk, bk, Wv, bv, Wo, bo):
        import jax, jax.numpy as jnp
        import numpy as np
        import math
        D_MODEL = 64
        NHEAD = 8
        D_LATTICE = 512
        D_K = D_LATTICE // NHEAD
        PHI = (1.0 + math.sqrt(5.0)) / 2.0
        PHI_INV = 1.0 / PHI
        PHI_INT = 1618.0
        C1 = PHI * math.sqrt(2.0) * 51.85
        C2 = math.pi / PHI

        def qrt_damping(x):
            return jnp.sin(C1 * x) * jnp.exp(-(x * x) / PHI) + jnp.cos(C2 * x)

        def ttt_filter(scores):
            int_scores = (jnp.abs(scores) * PHI_INT).astype(jnp.int32)
            mod9 = int_scores % 9
            chaos = (mod9 == 0) | (mod9 == 3) | (mod9 == 6)
            penalty = jnp.where(chaos, jnp.float32(PHI_INV), jnp.float32(1.0))
            return scores * penalty
        B, S, _ = x.shape

        def split_heads(t):
            return t.reshape(B, S, NHEAD, D_K).transpose(0, 2, 1, 3)
        q = split_heads(x @ Wq + bq)
        k = split_heads(x @ Wk + bk)
        v = split_heads(x @ Wv + bv)
        scores = jnp.einsum('bhqd,bhkd->bhqk', q, k) / jnp.float32(math.sqrt(D_K))
        scores = ttt_filter(scores)
        attn = jax.nn.softmax(scores, axis=-1)
        attn = attn * qrt_damping(attn)
        ctx = jnp.einsum('bhqk,bhkd->bhqd', attn, v)
        ctx = ctx.transpose(0, 2, 1, 3).reshape(B, S, D_LATTICE)
        return ctx @ Wo + bo

    def _L3_ffn_ref(x, w1s, b1s, w2s, b2s):
        import jax, jax.numpy as jnp
        import numpy as np
        INPUT_WIDTH = 64
        DEPTH = 7
        OUTPUT_WIDTH = 64
        N_NODES = 2 ** (DEPTH + 1) - 1
        B, S, D = x.shape
        flat_x = x.reshape(B * S, D)
        T = flat_x.shape[0]
        current = jnp.zeros((T,), dtype=jnp.int32)
        all_nodes = []
        all_logits = []
        for _ in range(DEPTH + 1):
            all_nodes.append(current)
            score = jnp.einsum('td,td->t', flat_x, w1s[current]) + b1s[current]
            all_logits.append(score)
            choice = ((jnp.sign(score) + 1.0) / 2.0).astype(jnp.int32)
            current = current * 2 + choice + 1
        logits = jnp.stack(all_logits, axis=1)
        path_weights = jax.nn.gelu(jnp.abs(logits), approximate=False)
        out = jnp.zeros((T, OUTPUT_WIDTH), dtype=x.dtype)
        for i in range(DEPTH + 1):
            nodes_i = all_nodes[i]
            t_i = jnp.einsum('td,tdo->to', flat_x, w2s[nodes_i]) + b2s[nodes_i]
            out = out + t_i * path_weights[:, i][:, None]
        return out.reshape(B, S, OUTPUT_WIDTH)
    h = _L0_tok_ref(x, L0_tok_w_in, L0_tok_b_in, L0_tok_wqkv, L0_tok_bqkv, L0_tok_wo, L0_tok_bo, L0_tok_w1, L0_tok_b1, L0_tok_w2, L0_tok_b2, L0_tok_ln1_g, L0_tok_ln1_b, L0_tok_ln2_g, L0_tok_ln2_b, L0_tok_w_out, L0_tok_b_out)
    h = h + _L0_attn_ref(_layernorm(h, axis=-1), L0_attn_qkv_w, L0_attn_qkv_b, L0_attn_proj_w, L0_attn_proj_b, L0_attn_bias_table)
    h = h + _L0_ffn_ref(_layernorm(h, axis=-1), L0_ffn_gate_w, L0_ffn_gate_b, L0_ffn_w1, L0_ffn_b1, L0_ffn_w2, L0_ffn_b2, L0_ffn_gamma, L0_ffn_beta)
    h = h + _L1_attn_ref(_layernorm(h, axis=-1), L1_attn_Wqk, L1_attn_Wv, L1_attn_Wpos, L1_attn_bpos, L1_attn_Wproj, L1_attn_bproj, L1_attn_gating)
    h = h + _L1_ffn_ref(_layernorm(h, axis=-1), L1_ffn_Wr, L1_ffn_br, L1_ffn_W1, L1_ffn_b1, L1_ffn_W2, L1_ffn_b2)
    h = h + _L2_attn_ref(_layernorm(h, axis=-1), L2_attn_base_phases, L2_attn_Wk1, L2_attn_bk1, L2_attn_Wk2, L2_attn_bk2, L2_attn_Wq1, L2_attn_bq1, L2_attn_Wq2, L2_attn_bq2, L2_attn_Wvc, L2_attn_bvc, L2_attn_Wvp, L2_attn_bvp, L2_attn_Wg1, L2_attn_bg1, L2_attn_Wg2, L2_attn_bg2, L2_attn_ln_g, L2_attn_ln_b, L2_attn_Wo, L2_attn_bo)
    h = h + _L2_ffn_ref(_layernorm(h, axis=-1), L2_ffn_hl_w, L2_ffn_hl_b, L2_ffn_wq, L2_ffn_wk, L2_ffn_wv, L2_ffn_gate_w, L2_ffn_gate_b, L2_ffn_ln_g, L2_ffn_ln_b, L2_ffn_fc1_w, L2_ffn_fc1_b, L2_ffn_fc2_w, L2_ffn_fc2_b, L2_ffn_fnorm_g, L2_ffn_fnorm_b, L2_ffn_fgate_w)
    h = h + _L3_attn_ref(_layernorm(h, axis=-1), L3_attn_Wq, L3_attn_bq, L3_attn_Wk, L3_attn_bk, L3_attn_Wv, L3_attn_bv, L3_attn_Wo, L3_attn_bo)
    h = h + _L3_ffn_ref(_layernorm(h, axis=-1), L3_ffn_w1s, L3_ffn_b1s, L3_ffn_w2s, L3_ffn_b2s)
    return h

_drawn_inputs = setup_inputs


def setup_inputs(seed=0):
    import zlib

    import numpy as np

    out = dict(_drawn_inputs(seed))
    spreads = {'L0_tok_b_in': (0.0, 0.1),
     'L0_tok_bqkv': (0.0, 0.1),
     'L0_tok_bo': (0.0, 0.1),
     'L0_tok_b1': (0.0, 0.1),
     'L0_tok_b2': (0.0, 0.1),
     'L0_tok_ln1_g': (1.0, 0.2),
     'L0_tok_ln1_b': (0.0, 0.1),
     'L0_tok_ln2_g': (1.0, 0.2),
     'L0_tok_ln2_b': (0.0, 0.1),
     'L0_tok_b_out': (0.0, 0.1),
     'L0_ffn_gate_b': (0.0, 0.1),
     'L0_ffn_b1': (0.0, 0.1),
     'L0_ffn_b2': (0.0, 0.1),
     'L0_ffn_gamma': (1.0, 0.2),
     'L0_ffn_beta': (0.0, 0.1),
     'L1_attn_bpos': (0.0, 0.8),
     'L1_attn_bproj': (0.0, 0.1),
     'L1_attn_gating': (1.0, 0.6),
     'L2_attn_bk1': (0.0, 0.8),
     'L2_attn_bk2': (0.0, 0.5),
     'L2_attn_bq1': (0.0, 0.641),
     'L2_attn_bq2': (0.0, 0.512),
     'L2_attn_bvc': (0.0, 0.1),
     'L2_attn_bvp': (0.0, 0.406),
     'L2_attn_bg1': (0.0, 0.8),
     'L2_attn_bg2': (0.0, 0.435),
     'L2_attn_ln_g': (1.0, 0.545),
     'L2_attn_ln_b': (0.0, 0.1),
     'L2_attn_bo': (0.0, 0.1),
     'L2_ffn_ln_g': (1.0, 0.2),
     'L2_ffn_ln_b': (0.0, 0.287),
     'L2_ffn_fnorm_g': (1.0, 0.2),
     'L2_ffn_fnorm_b': (0.0, 0.1),
     'L3_ffn_b1s': (0.0, 0.1),
     'L3_ffn_b2s': (0.0, 0.1)}
    factors = {'L0_attn_bias_table': 8.0,
     'L1_attn_Wqk': 8.0,
     'L1_attn_Wpos': 3.088,
     'L2_attn_base_phases': 3.281,
     'L2_attn_Wk1': 8.0,
     'L2_attn_Wk2': 8.0,
     'L2_attn_Wq1': 7.52,
     'L2_attn_Wq2': 8.0,
     'L2_attn_Wvp': 3.408,
     'L2_attn_Wg1': 6.798,
     'L2_attn_Wg2': 6.779,
     'L2_ffn_wq': 8.0,
     'L2_ffn_wk': 8.0,
     'L2_ffn_gate_w': 8.0,
     'L2_ffn_gate_b': 8.0,
     'L2_ffn_fc1_b': 3.262,
     'L2_ffn_fc2_w': 3.375,
     'L3_attn_bq': 3.911,
     'L3_attn_Wk': 2.741,
     'L3_attn_bk': 3.744,
     'L3_attn_bo': 3.393}
    for name, (base, spread) in spreads.items():
        noise = np.random.default_rng([zlib.crc32(name.encode()), seed]).standard_normal(out[name].shape)
        drawn = base * np.exp(spread * noise) if base else spread * noise
        out[name] = jnp.asarray(drawn.astype(out[name].dtype))
    for name, factor in factors.items():
        out[name] = (out[name] * factor).astype(out[name].dtype)
    return out
```

```python
import math
from contextlib import ExitStack

import numpy as np
import concourse.bass as bass
from concourse import mybir

F32 = mybir.dt.float32
U32 = mybir.dt.uint32
ALU = mybir.AluOpType
ACT = mybir.ActivationFunctionType
AX = mybir.AxisListType.X
XY = mybir.AxisListType.XY

NB = 64
NT = 124
D = 64
GS = 4
NG = NB // GS
GT = GS * NT


START = 1
FROM_ZERO = ("loaded", "own", "landed0", "landed1", "stored")


class InOrder:

    def __init__(self, eng, sem, base=0):
        self.eng, self.sem, self.base, self.n = eng, sem, base, 0

    def __call__(self, ins, carrier=None):
        self.n += 1
        ins.then_inc(self.sem, 1)
        self.eng.wait_ge(self.sem, self.base + self.n)
        if carrier is not None:
            carrier()


class Semaphores:

    def __init__(self, nc, ctx, name):
        self.nc, self.ctx, self.name, self.all = nc, ctx, name, []

    def __call__(self, what):
        s = self.ctx.enter_context(self.nc.semaphore(f"{self.name}_{what}"))
        self.all.append((s, 0 if what.endswith(FROM_ZERO) else START))
        return s

    def start(self):
        with self.nc.Block() as block:
            @block.gpsimd
            def _(pool):
                for s, _ in self.all:
                    pool.sem_clear(s)
                for s, first in self.all:
                    if first:
                        pool.sem_inc(s, first)


class Core:

    def __init__(self, nc, ctx, aps):
        self.nc, self.ctx, self.aps = nc, ctx, aps
        self.h = ctx.enter_context(nc.sbuf_tensor("h", [NT, NB, D], F32))
        self.xn = ctx.enter_context(nc.sbuf_tensor("xn", [NT, NB, D], F32))
        self.ident = ctx.enter_context(nc.sbuf_tensor("ident", [128, 128], F32))
        self.eps = ctx.enter_context(nc.sbuf_tensor("eps", [128, 2], F32))


def bc(ap, n, axis):
    ap = ap.unsqueeze(axis)
    shape = list(ap.shape)
    shape[axis] = n
    return ap.broadcast_to(shape)


def transpose_each(core, bank, x, W):
    for s in range(GS):
        wide = x[:, s:s + 2, :].rearrange("p s f -> p (s f)") if s == 0 else x[:, s, :]
        mm = core.nc.tensor.transpose(bank[0:wide.shape[1], s * NT:(s + 1) * NT], wide, core.ident[0:NT, 0:NT])
    return mm


def constants(core):
    nc = core.nc
    with ExitStack() as ctx:
        cleared = ctx.enter_context(nc.semaphore("cleared"))
        block = ctx.enter_context(nc.Block())

        @block.gpsimd
        def _(pool):
            nc.gpsimd.memset(core.eps[:, 0:1], 1e-5)
            nc.gpsimd.memset(core.eps[:, 1:2], 1e-8)
            nc.gpsimd.memset(core.ident[:, :], 0.0).then_inc(cleared, 1)
            pool.wait_ge(cleared, 1)
            nc.gpsimd.affine_select(out=core.ident[:, :], in_=core.ident[:, :], compare_op=ALU.not_equal,
                                    fill=1.0, base=0, pattern=[[-1, 128]], channel_multiplier=1)


def layer_norm(core, name):
    nc = core.nc
    CH = 4
    W = NB // CH
    with ExitStack() as ctx:
        sem = Semaphores(nc, ctx, name)
        sq = ctx.enter_context(nc.sbuf_tensor(f"{name}_sq", [NT, CH, W, D], F32))
        mean = ctx.enter_context(nc.sbuf_tensor(f"{name}_mean", [NT, CH, W], F32))
        var = ctx.enter_context(nc.sbuf_tensor(f"{name}_var", [NT, CH, W], F32))
        root = ctx.enter_context(nc.sbuf_tensor(f"{name}_root", [NT, CH, W], F32))
        centered, squared, summed, rooted, own = (
            sem("centered"), sem("squared"), sem("summed"), sem("rooted"), sem("own"))
        sem.start()
        block = ctx.enter_context(nc.Block())

        @block.vector
        def _(dve):
            own_done = InOrder(dve, own)
            for c in range(CH):
                hc, xc = core.h[:, c * W:(c + 1) * W, :], core.xn[:, c * W:(c + 1) * W, :]
                own_done(nc.vector.tensor_reduce(mean[:, c, :], hc, AX, ALU.add))
                own_done(nc.vector.tensor_scalar(mean[:, c, :], mean[:, c, :], 1.0 / D, None, ALU.mult))
                nc.vector.tensor_tensor(xc, hc, bc(mean[:, c, :], D, 2), ALU.subtract).then_inc(centered, 1)
            for c in range(CH):
                dve.wait_ge(squared, START + c + 1)
                own_done(nc.vector.tensor_reduce(var[:, c, :], sq[:, c], AX, ALU.add))
                nc.vector.tensor_scalar(var[:, c, :], var[:, c, :], 1.0 / D, 1e-5, ALU.mult, ALU.add).then_inc(summed, 1)
            for c in range(CH):
                xc = core.xn[:, c * W:(c + 1) * W, :]
                dve.wait_ge(rooted, START + c + 1)
                own_done(nc.vector.reciprocal(root[:, c, :], root[:, c, :]))
                own_done(nc.vector.tensor_tensor(var[:, c, :], var[:, c, :], root[:, c, :], ALU.mult))
                own_done(nc.vector.tensor_tensor(var[:, c, :], var[:, c, :], root[:, c, :], ALU.mult))
                own_done(nc.vector.tensor_scalar(var[:, c, :], var[:, c, :], -0.5, 1.5, ALU.mult, ALU.add))
                own_done(nc.vector.tensor_tensor(var[:, c, :], var[:, c, :], root[:, c, :], ALU.mult))
                nc.vector.tensor_tensor(xc, xc, bc(var[:, c, :], D, 2), ALU.mult)

        @block.scalar
        def _(act):
            for c in range(CH):
                act.wait_ge(centered, START + c + 1)
                nc.scalar.activation(sq[:, c], core.xn[:, c * W:(c + 1) * W, :], ACT.Square).then_inc(squared, 1)
            for c in range(CH):
                act.wait_ge(summed, START + c + 1)
                nc.scalar.activation(root[:, c, :], var[:, c, :], ACT.Sqrt).then_inc(rooted, 1)


def window_attention(core, name, biased):
    nc, aps = core.nc, core.aps
    NH, HD = 8, 8
    NK = 71 if biased else 64
    with ExitStack() as ctx:
        if not biased:
            posT, gate, antigate, gate_mass = position_scores(core, name, ctx)
        sem = Semaphores(nc, ctx, name)
        sb = lambda n, shape: ctx.enter_context(nc.sbuf_tensor(f"{name}_{n}", shape, F32))
        wqkv = sb("wqkv", [65, 3 * D])
        wproj = sb("wproj", [65, D])
        headmask = sb("headmask", [D, NH])
        xg = sb("xg", [NT, GS, D])
        xT = sb("xT", [65, GT])
        qT = sb("qT", [NK, GT])
        kT = sb("kT", [D, GT])
        kmask = sb("kmask", [NK, 2, NH, NT])
        v = sb("v", [NT, GS, D])
        negmax = sb("negmax", [NT, 2, NH])
        sums = sb("sums", [NT, GS, NH])
        probs = sb("probs", [NT, 2, NH, NT])
        probsT = sb("probsT", [NT, 2, NH, NT])
        on = sb("on", [NT, GS, D])
        oT = sb("oT", [65, GT])
        ps = lambda n, shape: ctx.enter_context(nc.psum_tensor(f"{name}_{n}", shape, F32))
        bT = ps("bT", [128, 512])
        bQ = ps("bQ", [128, 512])
        bS = ps("bS", [128, 2, 2, 512])
        bP = ps("bP", [128, 2, 512])

        loaded, ones = sem("loaded"), sem("ones")
        xg_ready, x_transposed, xT_ready = sem("xg_ready"), sem("x_transposed"), sem("xT_ready")
        q_made, q_taken, k_made, k_taken, v_made, v_taken = (
            sem(n) for n in ("q_made", "q_taken", "k_made", "k_taken", "v_made", "v_taken"))
        kmask_ready, scores_made, max_ready, exp_done = (
            sem(n) for n in ("kmask_ready", "scores_made", "max_ready", "exp_done"))
        pT_made, pT_taken, pv_made, on_ready = (sem(n) for n in ("pT_made", "pT_taken", "pv_made", "on_ready"))
        oT_made, oT_taken, y_made, y_taken = (sem(n) for n in ("oT_made", "oT_taken", "y_made", "y_taken"))
        own = sem("own")
        NLOAD = 6 if biased else 3
        OWN = 1 if biased else 8
        if not biased:
            total = sb("total", [NT, GS, NH])
            posshare = sb("posshare", [NT, GS, NH])
            o2 = sb("o2", [NT, GS, D])
            o2_made = sem("o2_made")
        sem.start()
        block = ctx.enter_context(nc.Block())

        @block.sync
        def _(sp):
            sp.dma_start(wqkv[:, :], aps[f"{name}_wqkv"]).then_inc(loaded, 16)
            sp.dma_start(wproj[:, :], aps[f"{name}_wproj"]).then_inc(loaded, 16)
            sp.dma_start(headmask[:, :], aps["headmask8"]).then_inc(loaded, 16)
            if biased:
                sp.dma_start(qT[D:NK, :], aps["onehot7"]).then_inc(loaded, 16)
                for u in range(2):
                    sp.dma_start(kmask[D:NK, u, :, :], aps[f"{name}_bias7"]).then_inc(loaded, 16)

        @block.gpsimd
        def _(pool):
            nc.gpsimd.memset(xT[D:D + 1, :], 1.0).then_inc(ones, 1)
            nc.gpsimd.memset(oT[D:D + 1, :], 1.0).then_inc(ones, 1)
            pool.wait_ge(ones, START + 2)
            with pool.Fori(0, NG) as g:
                pool.wait_ge(x_transposed, START + g)
                nc.gpsimd.tensor_copy(xg[:, :, :], core.xn[:, bass.ds(g * GS, GS), :]).then_inc(xg_ready, 1)

        @block.tensor
        def _(pe):
            pe.wait_ge(loaded, 16 * NLOAD)
            pe.wait_ge(ones, START + 2)
            with pe.Fori(0, NG) as g:
                pe.wait_ge(y_taken, START + g)
                pe.wait_ge(xg_ready, START + g + 1)
                mm = transpose_each(core, bT, xg, D)
                mm.then_inc(x_transposed, 1)
                pe.wait_ge(xT_ready, START + g + 1)
                pe.wait_ge(oT_taken, START + g)
                nc.tensor.matmul(bQ[0:D, 0:GT], wqkv[:, 0:D], xT[:, :], start=True, stop=True).then_inc(q_made, 1)
                for s in range(GS):
                    mm = nc.tensor.matmul(bT[0:NT, s * D:(s + 1) * D], xT[:, s * NT:(s + 1) * NT],
                                          wqkv[:, 2 * D:3 * D], start=True, stop=True)
                mm.then_inc(v_made, 1)
                pe.wait_ge(q_taken, START + g + 1)
                nc.tensor.matmul(bQ[0:D, 0:GT], wqkv[:, D:2 * D], xT[:, :], start=True, stop=True).then_inc(k_made, 1)

                def scores(s):
                    pe.wait_ge(kmask_ready, START + GS * g + s + 1)
                    pe.wait_ge(exp_done, START + GS * g + max(s - 1, 0))
                    for half in range(2):
                        mm = nc.tensor.matmul(bS[0:NT, s % 2, half, 0:GT], qT[:, s * NT:(s + 1) * NT],
                                              kmask[:, s % 2, half * 4:half * 4 + 4, :].rearrange("p h m -> p (h m)"),
                                              start=True, stop=True)
                    mm.then_inc(scores_made, 1)

                def values(s):
                    pe.wait_ge(exp_done, START + GS * g + s + 1)
                    pe.wait_ge(pT_taken, START + GS * g + s)
                    for h in range(NH):
                        mm = nc.tensor.transpose(bP[0:NT, h // 4, (h % 4) * NT:(h % 4 + 1) * NT],
                                                 probs[:, s % 2, h, :], core.ident[0:NT, 0:NT])
                    mm.then_inc(pT_made, 1)

                def weigh(s):
                    pe.wait_ge(pT_taken, START + GS * g + s + 1)
                    pe.wait_ge(v_taken, START + g + 1)
                    for h in range(NH):
                        mm = nc.tensor.matmul(bT[0:NT, s * D + h * HD:s * D + (h + 1) * HD], probsT[:, s % 2, h, :],
                                              v[:, s, h * HD:(h + 1) * HD], start=True, stop=True)
                    mm.then_inc(pv_made, 1)

                scores(0)
                for s in range(GS):
                    if s + 1 < GS:
                        scores(s + 1)
                    values(s)
                    if s >= 1:
                        weigh(s - 1)
                weigh(GS - 1)
                if not biased:
                    for h in range(NH):
                        mm = nc.tensor.matmul(
                            bQ[0:NT, 0:GS * D].rearrange("p (s f) -> p s f", s=GS)[:, :, h * HD:(h + 1) * HD],
                            posT[:, h, :], v[:, :, h * HD:(h + 1) * HD], start=True, stop=True)
                    mm.then_inc(o2_made, 1)
                pe.wait_ge(on_ready, START + g + 1)
                mm = transpose_each(core, bQ, on, D)
                mm.then_inc(oT_made, 1)
                pe.wait_ge(oT_taken, START + g + 1)
                for s in range(GS):
                    mm = nc.tensor.matmul(bT[0:NT, s * D:(s + 1) * D], oT[:, s * NT:(s + 1) * NT], wproj[:, :],
                                          start=True, stop=True)
                mm.then_inc(y_made, 1)

        @block.scalar
        def _(act):
            with act.Fori(0, NG) as g:
                act.wait_ge(x_transposed, START + g + 1)
                act.wait_ge(k_made, START + g)
                nc.scalar.copy(xT[0:D, :], bT[0:D, 0:GT]).then_inc(xT_ready, 1)
                act.wait_ge(q_made, START + g + 1)
                act.wait_ge(scores_made, START + GS * g)
                nc.scalar.activation(qT[0:D, :], bQ[0:D, 0:GT], ACT.Copy, scale=float(HD) ** -0.5).then_inc(q_taken, 1)
                act.wait_ge(k_made, START + g + 1)
                act.wait_ge(kmask_ready, START + GS * g)
                nc.scalar.copy(kT[:, :], bQ[0:D, 0:GT]).then_inc(k_taken, 1)
                act.wait_ge(v_made, START + g + 1)
                act.wait_ge(pv_made, START + GS * g)
                nc.scalar.copy(v[:, :, :], bT[0:NT, 0:GS * D].rearrange("p (s f) -> p s f", s=GS)).then_inc(v_taken, 1)
                for s in range(GS):
                    act.wait_ge(max_ready, START + GS * g + s + 1)
                    act.wait_ge(pT_made, START + GS * g + max(s - 1, 0))
                    if s == 0:
                        act.wait_ge(on_ready, START + g)
                    for h in range(NH):
                        ins = nc.scalar.activation(probs[:, s % 2, h, :],
                                                   bS[0:NT, s % 2, h // 4, (h % 4) * NT:(h % 4 + 1) * NT],
                                                   ACT.Exp, bias=negmax[:, s % 2, h:h + 1],
                                                   accum_out=sums[:, s, h:h + 1])
                    ins.then_inc(exp_done, 1)
                act.wait_ge(oT_made, START + g + 1)
                nc.scalar.copy(oT[0:D, :], bQ[0:D, 0:GT]).then_inc(oT_taken, 1)

        @block.vector
        def _(dve):
            dve.wait_ge(loaded, 16 * NLOAD)
            with dve.Fori(0, NG) as g:
                own_done = InOrder(dve, own, g * OWN)

                def mask_keys(s):
                    dve.wait_ge(k_taken, START + g + 1)
                    dve.wait_ge(scores_made, START + GS * g + max(s - 1, 0))
                    nc.vector.tensor_tensor(kmask[0:D, s % 2, :, :], bc(kT[:, s * NT:(s + 1) * NT], NH, 1),
                                            bc(headmask[:, :], NT, 2), ALU.mult).then_inc(kmask_ready, 1)

                def maxima(s):
                    dve.wait_ge(scores_made, START + GS * g + s + 1)
                    dve.wait_ge(exp_done, START + GS * g + max(s - 1, 0))
                    for half in range(2):
                        ins = nc.vector.tensor_reduce(negmax[:, s % 2, half * 4:half * 4 + 4],
                                                      bS[0:NT, s % 2, half, 0:GT].rearrange("p (h m) -> p h m", h=4),
                                                      AX, ALU.max, negate=True)
                    ins.then_inc(max_ready, 1)

                def take_probs(s):
                    dve.wait_ge(pT_made, START + GS * g + s + 1)
                    dve.wait_ge(pv_made, START + GS * g + max(s - 1, 0))
                    for half in range(2):
                        ins = nc.vector.tensor_copy(
                            probsT[:, s % 2, half * 4:half * 4 + 4, :].rearrange("p h m -> p (h m)"),
                            bP[0:NT, half, 0:GT])
                    ins.then_inc(pT_taken, 1)

                mask_keys(0)
                mask_keys(1)
                maxima(0)
                for s in range(GS):
                    if s + 2 < GS:
                        mask_keys(s + 2)
                    if s + 1 < GS:
                        maxima(s + 1)
                    take_probs(s)
                if not biased:
                    nc.vector.tensor_copy(total[:, :, :], sums[:, :, :])
                own_done(nc.vector.reciprocal(sums[:, :, :], sums[:, :, :]))
                dve.wait_ge(pv_made, START + GS * (g + 1))
                heads = lambda t: t.rearrange("p s (h e) -> p (s h) e", h=NH)
                pv = bT[0:NT, 0:GS * D].rearrange("p (x e) -> p x e", e=HD)
                each = lambda t: bc(t[:, :, :].rearrange("p s h -> p (s h)"), HD, 2)
                if biased:
                    nc.vector.tensor_tensor(heads(on[:, :, :]), pv, each(sums), ALU.mult).then_inc(on_ready, 1)
                else:
                    own_done(nc.vector.tensor_tensor(sums[:, :, :], sums[:, :, :], bc(antigate[:, :], GS, 1), ALU.mult))
                    own_done(nc.vector.tensor_tensor(total[:, :, :], total[:, :, :], sums[:, :, :], ALU.mult))
                    own_done(nc.vector.tensor_tensor(total[:, :, :], total[:, :, :], bc(gate_mass[:, :], GS, 1), ALU.add))
                    own_done(nc.vector.reciprocal(total[:, :, :], total[:, :, :]))
                    nc.vector.tensor_tensor(posshare[:, :, :], total[:, :, :], bc(gate[:, :], GS, 1), ALU.mult)
                    own_done(nc.vector.tensor_tensor(sums[:, :, :], sums[:, :, :], total[:, :, :], ALU.mult))
                    own_done(nc.vector.tensor_tensor(heads(on[:, :, :]), pv, each(sums), ALU.mult))
                    dve.wait_ge(o2_made, START + g + 1)
                    own_done(nc.vector.tensor_tensor(heads(o2[:, :, :]),
                                                     bQ[0:NT, 0:GS * D].rearrange("p (x e) -> p x e", e=HD),
                                                     each(posshare), ALU.mult))
                    nc.vector.tensor_tensor(on[:, :, :], on[:, :, :], o2[:, :, :], ALU.add).then_inc(on_ready, 1)
                dve.wait_ge(y_made, START + g + 1)
                hg = core.h[:, bass.ds(g * GS, GS), :]
                nc.vector.tensor_tensor(hg, hg, bT[0:NT, 0:GS * D].rearrange("p (s f) -> p s f", s=GS),
                                        ALU.add).then_inc(y_taken, 1)
                assert own_done.n == OWN, own_done.n


def position_scores(core, name, ctx):
    nc, aps = core.nc, core.aps
    NH = 8
    kept = lambda n, shape: ctx.enter_context(nc.sbuf_tensor(f"{name}_{n}", shape, F32))
    posT = kept("posT", [NT, NH, NT])
    gate, antigate, gate_mass = (kept(n, [NT, NH]) for n in ("gate", "antigate", "gate_mass"))
    with ExitStack() as own_ctx:
        sem = Semaphores(nc, own_ctx, name)
        sb = lambda n, shape: own_ctx.enter_context(nc.sbuf_tensor(f"{name}_{n}", shape, F32))
        rel = sb("rel", [NT, 3, NT])
        wpos = sb("wpos", [NT, 3, NH])
        bpos = sb("bpos", [NT, NH])
        score = sb("score", [NT, NH, NT])
        term = sb("term", [NT, NH, NT])
        maxima = sb("posmax", [NT, NH])
        mass = sb("posmass", [NT, NH])
        bP = own_ctx.enter_context(nc.psum_tensor(f"{name}_posP", [128, 2, 512], F32))
        loaded, own, centered, exp_done, softmaxed, transposed, gate_exp = (
            sem(n) for n in ("pos_loaded", "pos_own", "pos_centered", "pos_exp", "pos_softmaxed", "pos_transposed",
                             "gate_exp"))
        sem.start()
        block = own_ctx.enter_context(nc.Block())

        @block.sync
        def _(sp):
            sp.dma_start(rel[:, :, :], aps["posrel"]).then_inc(loaded, 16)
            sp.dma_start(wpos[:, :, :], aps[f"{name}_wpos"].partition_broadcast(NT)).then_inc(loaded, 16)
            sp.dma_start(bpos[:, :], aps[f"{name}_bpos"].partition_broadcast(NT)).then_inc(loaded, 16)
            sp.dma_start(gate[:, :], aps[f"{name}_gating"].partition_broadcast(NT)).then_inc(loaded, 16)

        @block.vector
        def _(dve):
            own_done = InOrder(dve, own)
            dve.wait_ge(loaded, 64)
            for c in range(3):
                to = term if c else score
                own_done(nc.vector.tensor_tensor(to[:, :, :], bc(rel[:, c, :], NH, 1), bc(wpos[:, c, :], NT, 2), ALU.mult))
                if c:
                    own_done(nc.vector.tensor_tensor(score[:, :, :], score[:, :, :], term[:, :, :], ALU.add))
            own_done(nc.vector.tensor_tensor(score[:, :, :], score[:, :, :], bc(bpos[:, :], NT, 2), ALU.add))
            own_done(nc.vector.tensor_reduce(maxima[:, :], score[:, :, :], AX, ALU.max))
            nc.vector.tensor_tensor(score[:, :, :], score[:, :, :], bc(maxima[:, :], NT, 2),
                                    ALU.subtract).then_inc(centered, 1)
            dve.wait_ge(exp_done, START + 1)
            own_done(nc.vector.tensor_reduce(mass[:, :], score[:, :, :], AX, ALU.add))
            own_done(nc.vector.reciprocal(mass[:, :], mass[:, :]))
            own_done(nc.vector.tensor_tensor(score[:, :, :], score[:, :, :], bc(mass[:, :], NT, 2), ALU.mult))
            own_done(nc.vector.tensor_reduce(mass[:, :], score[:, :, :], AX, ALU.add))
            dve.wait_ge(gate_exp, START + 1)
            own_done(nc.vector.tensor_scalar(gate[:, :], gate[:, :], 1.0, None, ALU.add))
            own_done(nc.vector.reciprocal(gate[:, :], gate[:, :]))
            nc.vector.tensor_scalar(antigate[:, :], gate[:, :], -1.0, 1.0, ALU.mult, ALU.add)
            nc.vector.tensor_tensor(gate_mass[:, :], gate[:, :], mass[:, :], ALU.mult).then_inc(softmaxed, 1)
            dve.wait_ge(transposed, START + 1)
            for half in range(2):
                nc.vector.tensor_copy(posT[:, half * 4:half * 4 + 4, :].rearrange("p h m -> p (h m)"),
                                      bP[0:NT, half, 0:4 * NT])

        @block.scalar
        def _(act):
            act.wait_ge(centered, START + 1)
            nc.scalar.activation(score[:, :, :], score[:, :, :], ACT.Exp).then_inc(exp_done, 1)
            act.wait_ge(loaded, 64)
            nc.scalar.activation(gate[:, :], gate[:, :], ACT.Exp, scale=-1.0).then_inc(gate_exp, 1)

        @block.tensor
        def _(pe):
            pe.wait_ge(softmaxed, START + 1)
            for h in range(NH):
                mm = nc.tensor.transpose(bP[0:NT, h // 4, (h % 4) * NT:(h % 4 + 1) * NT], score[:, h, :],
                                         core.ident[0:NT, 0:NT])
            mm.then_inc(transposed, 1)
    return posT, gate, antigate, gate_mass


def experts(core, name, E, F, normed):
    nc, aps = core.nc, core.aps
    with ExitStack() as kept:
        keep = lambda n, shape: kept.enter_context(nc.sbuf_tensor(f"{name}_{n}", shape, F32))
        xT = keep("xT", [2 * D, NB * NT])
        weight = keep("weight", [NT, NB, E])
        acc = core.xn if normed else core.h
        route(core, name, E, xT, weight, acc)

        with ExitStack() as ctx:
            sem = Semaphores(nc, ctx, name)
            sb = lambda n, shape: ctx.enter_context(nc.sbuf_tensor(f"{name}_{n}", shape, F32))
            ps = lambda n, shape: ctx.enter_context(nc.psum_tensor(f"{name}_{n}", shape, F32))
            w1 = sb("w1", [2 * D, 2, F])
            b1 = sb("b1", [F, 2, 2])
            w2 = sb("w2", [F, 2, 2, D])
            xs = sb("xs", [2 * D, 2, GT])
            hid = sb("hid", [F, 2, 2, GT])
            part = sb("part", [NT, 2, 2, GS, D])
            bH = ps("bH", [128, 2, 2, 512])
            bY = ps("bY", [128, 2, 512])
            landed = [sem("landed0"), sem("landed1")]
            xs_ready, h_made, hid_ready, y_made, y_taken, parted = (
                sem(n) for n in ("xs_ready", "h_made", "hid_ready", "y_made", "y_taken", "parted"))
            sem.start()
            block = ctx.enter_context(nc.Block())
            PAIRS = E // 2
            NP = PAIRS // 2
            NL = NG // 2

            @block.sync
            def _(sp):
                def load(slot, p):
                    for to, w in ((w1[:, slot, :], aps[f"{name}_w1"]), (b1[:, slot, :], aps[f"{name}_b1"]),
                                  (w2[:, slot, :, :].rearrange("p e f -> p (e f)"), aps[f"{name}_w2"])):
                        src = w[p, :, :] if isinstance(p, int) else w[bass.ds(p, 1), :, :].squeeze(0)
                        sp.dma_start(to, src).then_inc(landed[slot], 16)

                for slot in range(2):
                    load(slot, slot)
                with sp.Fori(0, NP - 1) as i:
                    for slot in range(2):
                        sp.wait_ge(y_made, START + i * (4 * NL) + 2 * NL * (slot + 1))
                        load(slot, (i + 1) * 2 + slot)

            @block.gpsimd
            def _(pool):
                with pool.Fori(0, NP) as i:
                    for slot in range(2):
                        with pool.Fori(0, NL) as j:
                            t = (i * 2 + slot) * NL + j
                            for u in range(2):
                                pool.wait_ge(h_made, START + t * 4)
                                nc.gpsimd.tensor_copy(xs[:, u, :], xT[:, bass.ds((j * 2 + u) * GT, GT)]).then_inc(xs_ready, 1)

            @block.tensor
            def _(pe):
                with pe.Fori(0, NP) as i:
                    for slot in range(2):
                        with pe.Fori(0, NL) as j:
                            pe.wait_ge(landed[slot], i * 48 + 48)
                            t = (i * 2 + slot) * NL + j
                            for u in range(2):
                                pe.wait_ge(hid_ready, START + t * 4)
                                pe.wait_ge(xs_ready, START + t * 2 + (u + 1))
                                for e in range(2):
                                    nc.tensor.matmul(bH[0:F, u, e, 0:GT], w1[e * D:(e + 1) * D, slot, :],
                                                     xs[e * D:(e + 1) * D, u, :],
                                                     start=True, stop=True).then_inc(h_made, 1)
                            for u in range(2):
                                pe.wait_ge(y_taken, START + t * 2 + u)
                                for e in range(2):
                                    pe.wait_ge(hid_ready, START + t * 4 + (2 * u + e + 1))
                                    for s in range(GS):
                                        c = (e * GS + s) * D
                                        mm = nc.tensor.matmul(bY[0:NT, u, c:c + D], hid[:, u, e, s * NT:(s + 1) * NT],
                                                              w2[:, slot, e, :], start=True, stop=True)
                                mm.then_inc(y_made, 1)

            @block.scalar
            def _(act):
                with act.Fori(0, NP) as i:
                    for slot in range(2):
                        with act.Fori(0, NL) as j:
                            act.wait_ge(landed[slot], i * 48 + 48)
                            t = (i * 2 + slot) * NL + j
                            for u in range(2):
                                act.wait_ge(y_made, START + t * 2 + u)
                                for e in range(2):
                                    act.wait_ge(h_made, START + t * 4 + (2 * u + e + 1))
                                    nc.scalar.activation(hid[:, u, e, :], bH[0:F, u, e, 0:GT], ACT.Relu,
                                                         bias=b1[:, slot, e:e + 1]).then_inc(hid_ready, 1)

            @block.vector
            def _(dve):
                with dve.Fori(0, NP) as i:
                    for slot in range(2):
                        with dve.Fori(0, NL) as j:
                            t = (i * 2 + slot) * NL + j
                            for u in range(2):
                                g = j * 2 + u
                                dve.wait_ge(y_made, START + t * 2 + (u + 1))
                                wg = weight[:, bass.ds(g * GS, GS), bass.ds((i * 2 + slot) * 2, 2)]
                                nc.vector.tensor_tensor(part[:, u], bY[0:NT, u, :].rearrange("p (e s f) -> p e s f", e=2, s=GS),
                                                        bc(wg.rearrange("p s e -> p e s"), D, 3), ALU.mult).then_inc(y_taken, 1)
                                ag = acc[:, bass.ds(g * GS, GS), :]
                                for e in range(2):
                                    dve.wait_ge(y_taken, START + t * 2 + (u + 1))
                                    if e:
                                        dve.wait_ge(parted, START + t * 4 + (2 * u + e))
                                    nc.vector.tensor_tensor(ag, ag, part[:, u, e], ALU.add).then_inc(parted, 1)


def route(core, name, E, xT, weight, acc):
    nc, aps = core.nc, core.aps
    with ExitStack() as ctx:
        sem = Semaphores(nc, ctx, name)
        sb = lambda n, shape, dt=F32: ctx.enter_context(nc.sbuf_tensor(f"{name}_{n}", shape, dt))
        ps = lambda n, shape: ctx.enter_context(nc.psum_tensor(f"{name}_{n}", shape, F32))
        wr = sb("wr", [D, E])
        br = sb("br", [NT, E])
        b2 = sb("b2", [E, D])
        iota = sb("iota", [NT, E])
        xg = sb("xg", [NT, GS, 2, D])
        xgT = sb("xgT", [D, GT])
        logits = sb("logits", [NT, GS, E])
        top = sb("top", [NT, GS, 8])
        topi = sb("topi", [NT, GS, 8], U32)
        topf = sb("topf", [NT, GS, 2])
        idle = sb("idle", [NT, 1])
        carrier = lambda: nc.vector.memset(idle[:, :], 0.0)
        odds = sb("odds", [NT, GS])
        share = sb("share", [NT, 2, GS])
        second = sb("second", [NT, GS, E])
        wg = sb("wg", [NT, GS, E])
        wT = sb("wT", [E, GT])
        bX, bL, bW, bB = (ps(n, [128, 512]) for n in ("bX", "bL", "bW", "bB"))
        loaded, xg_ready, x_transposed, xT_ready, logits_made, gap_ready, odds_ready, wg_ready = (
            sem(n) for n in ("route_loaded", "xg_ready", "x_transposed", "xT_ready", "logits_made", "gap_ready",
                             "odds_ready", "wg_ready"))
        w_transposed, wT_ready, bias_made, bias_taken, own = (
            sem(n) for n in ("w_transposed", "wT_ready", "bias_made", "bias_taken", "own"))
        sem.start()
        block = ctx.enter_context(nc.Block())
        OWN = 10

        @block.sync
        def _(sp):
            sp.dma_start(wr[:, :], aps[f"{name}_wr"]).then_inc(loaded, 16)
            sp.dma_start(br[:, :], aps[f"{name}_br"].partition_broadcast(NT)).then_inc(loaded, 16)
            sp.dma_start(b2[:, :], aps[f"{name}_b2"]).then_inc(loaded, 16)
            sp.dma_start(iota[:, :], aps[f"iota{E}"].partition_broadcast(NT)).then_inc(loaded, 16)

        @block.gpsimd
        def _(pool):
            with pool.Fori(0, NG) as g:
                pool.wait_ge(x_transposed, START + g)
                for c in range(2):
                    ins = nc.gpsimd.tensor_copy(xg[:, :, c, :], core.xn[:, bass.ds(g * GS, GS), :])
                ins.then_inc(xg_ready, 1)

        @block.tensor
        def _(pe):
            pe.wait_ge(loaded, 64)
            with pe.Fori(0, NG) as g:
                pe.wait_ge(xT_ready, START + g)
                pe.wait_ge(xg_ready, START + g + 1)
                for s in range(GS):
                    mm = nc.tensor.transpose(bX[:, s * NT:(s + 1) * NT], xg[:, s, :, :].rearrange("p c f -> p (c f)"),
                                             core.ident[0:NT, 0:NT])
                mm.then_inc(x_transposed, 1)
                pe.wait_ge(xT_ready, START + g + 1)
                pe.wait_ge(gap_ready, START + g)
                for s in range(GS):
                    mm = nc.tensor.matmul(bL[0:NT, s * E:(s + 1) * E], xgT[:, s * NT:(s + 1) * NT], wr[:, :],
                                          start=True, stop=True)
                mm.then_inc(logits_made, 1)
                pe.wait_ge(wT_ready, START + g)
                pe.wait_ge(wg_ready, START + g + 1)
                mm = transpose_each(core, bW, wg, E)
                mm.then_inc(w_transposed, 1)
                pe.wait_ge(wT_ready, START + g + 1)
                pe.wait_ge(bias_taken, START + g)
                for s in range(GS):
                    mm = nc.tensor.matmul(bB[0:NT, s * D:(s + 1) * D], wT[:, s * NT:(s + 1) * NT], b2[:, :],
                                          start=True, stop=True)
                mm.then_inc(bias_made, 1)

        @block.scalar
        def _(act):
            with act.Fori(0, NG) as g:
                act.wait_ge(x_transposed, START + g + 1)
                act.wait_ge(logits_made, START + g)
                nc.scalar.copy(xT[:, bass.ds(g * GT, GT)], bX[:, 0:GT])
                nc.scalar.copy(xgT[:, :], bX[0:D, 0:GT]).then_inc(xT_ready, 1)
                act.wait_ge(gap_ready, START + g + 1)
                nc.scalar.activation(share[:, 1, :], odds[:, :], ACT.Exp).then_inc(odds_ready, 1)
                act.wait_ge(w_transposed, START + g + 1)
                act.wait_ge(bias_made, START + g)
                nc.scalar.copy(wT[:, :], bW[0:E, 0:GT]).then_inc(wT_ready, 1)

        @block.vector
        def _(dve):
            dve.wait_ge(loaded, 64)
            with dve.Fori(0, NG) as g:
                own_done = InOrder(dve, own, g * OWN)
                dve.wait_ge(logits_made, START + g + 1)
                own_done(nc.vector.tensor_tensor(logits[:, :, :], bL[0:NT, 0:GS * E].rearrange("p (s e) -> p s e", s=GS),
                                                 bc(br[:, :], GS, 1), ALU.add), carrier)
                for s in range(GS):
                    ins = nc.vector.max(top[:, s, :], logits[:, s, :])
                own_done(ins, carrier)
                for s in range(GS):
                    ins = nc.vector.max_index(topi[:, s, :], top[:, s, :], logits[:, s, :])
                own_done(ins)
                own_done(nc.vector.tensor_copy(topf[:, :, :], topi[:, :, 0:2]))
                nc.vector.tensor_tensor(odds[:, :], top[:, :, 1], top[:, :, 0], ALU.subtract).then_inc(gap_ready, 1)
                dve.wait_ge(odds_ready, START + g + 1)
                own_done(nc.vector.tensor_scalar(share[:, 0, :], share[:, 1, :], 1.0, None, ALU.add))
                own_done(nc.vector.reciprocal(share[:, 0, :], share[:, 0, :]))
                own_done(nc.vector.tensor_tensor(share[:, 1, :], share[:, 1, :], share[:, 0, :], ALU.mult))
                dve.wait_ge(w_transposed, START + g)
                each = lambda t: bc(t, E, 2)
                at = bc(iota[:, :], GS, 1)
                own_done(nc.vector.tensor_tensor(wg[:, :, :], at, each(topf[:, :, 0]), ALU.is_equal))
                nc.vector.tensor_tensor(second[:, :, :], at, each(topf[:, :, 1]), ALU.is_equal)
                own_done(nc.vector.tensor_tensor(wg[:, :, :], wg[:, :, :], each(share[:, 0, :]), ALU.mult))
                own_done(nc.vector.tensor_tensor(second[:, :, :], second[:, :, :], each(share[:, 1, :]), ALU.mult))
                nc.vector.tensor_tensor(wg[:, :, :], wg[:, :, :], second[:, :, :], ALU.add).then_inc(wg_ready, 1)
                dve.wait_ge(wg_ready, START + g + 1)
                nc.vector.tensor_copy(weight[:, bass.ds(g * GS, GS), :], wg[:, :, :])
                dve.wait_ge(bias_made, START + g + 1)
                dve.wait_ge(x_transposed, START + g + 1)
                ag = acc[:, bass.ds(g * GS, GS), :]
                nc.vector.tensor_tensor(ag, ag, bB[0:NT, 0:GS * D].rearrange("p (s f) -> p s f", s=GS),
                                        ALU.add).then_inc(bias_taken, 1)
                assert own_done.n == OWN, own_done.n


def add_normed(core, name):
    nc, aps = core.nc, core.aps
    CH = 4
    W = NB // CH
    with ExitStack() as ctx:
        sem = Semaphores(nc, ctx, name)
        sb = lambda n, shape: ctx.enter_context(nc.sbuf_tensor(f"{name}_{n}", shape, F32))
        affine = sb("affine", [NT, 2, D])
        sq = sb("sq", [NT, CH, W, D])
        mean = sb("mean", [NT, CH, W])
        var = sb("var", [NT, CH, W])
        loaded, centered, squared, summed, rooted, own = (
            sem(n) for n in ("affine_loaded", "centered", "squared", "summed", "rooted", "own"))
        sem.start()
        block = ctx.enter_context(nc.Block())

        @block.sync
        def _(sp):
            sp.dma_start(affine[:, :, :], aps[f"{name}_affine"].partition_broadcast(NT)).then_inc(loaded, 16)

        @block.vector
        def _(dve):
            own_done = InOrder(dve, own)
            for c in range(CH):
                xc = core.xn[:, c * W:(c + 1) * W, :]
                own_done(nc.vector.tensor_reduce(mean[:, c, :], xc, AX, ALU.add))
                own_done(nc.vector.tensor_scalar(mean[:, c, :], mean[:, c, :], 1.0 / D, None, ALU.mult))
                nc.vector.tensor_tensor(xc, xc, bc(mean[:, c, :], D, 2), ALU.subtract).then_inc(centered, 1)
            for c in range(CH):
                dve.wait_ge(squared, START + c + 1)
                nc.vector.tensor_reduce(var[:, c, :], sq[:, c], AX, ALU.add).then_inc(summed, 1)
            dve.wait_ge(loaded, 16)
            for c in range(CH):
                xc = core.xn[:, c * W:(c + 1) * W, :]
                hc = core.h[:, c * W:(c + 1) * W, :]
                dve.wait_ge(rooted, START + c + 1)
                own_done(nc.vector.reciprocal(var[:, c, :], var[:, c, :]))
                own_done(nc.vector.tensor_tensor(xc, xc, bc(var[:, c, :], D, 2), ALU.mult))
                own_done(nc.vector.tensor_tensor(xc, xc, bc(affine[:, 0, :], W, 1), ALU.mult))
                own_done(nc.vector.tensor_tensor(xc, xc, bc(affine[:, 1, :], W, 1), ALU.add))
                nc.vector.tensor_tensor(hc, hc, xc, ALU.add)

        @block.scalar
        def _(act):
            for c in range(CH):
                act.wait_ge(centered, START + c + 1)
                nc.scalar.activation(sq[:, c], core.xn[:, c * W:(c + 1) * W, :], ACT.Square).then_inc(squared, 1)
            for c in range(CH):
                act.wait_ge(summed, START + c + 1)
                nc.scalar.activation(var[:, c, :], var[:, c, :], ACT.Sqrt, bias=core.eps[0:NT, 0:1],
                                     scale=1.0 / D).then_inc(rooted, 1)


def lattice_attention(core, name):
    nc, aps = core.nc, core.aps
    NH, HD = 8, 64
    NL = NH * HD
    PHI = (1.0 + math.sqrt(5.0)) / 2.0
    C1 = PHI * math.sqrt(2.0) * 51.85
    C2 = math.pi / PHI
    ROUND = 1.5 * 2.0 ** 23
    TURN = 6.283184
    WIDTH = NH * NT
    with ExitStack() as ctx:
        sem = Semaphores(nc, ctx, name)
        sb = lambda n, shape: ctx.enter_context(nc.sbuf_tensor(f"{name}_{n}", shape, F32))
        ps = lambda n, shape: ctx.enter_context(nc.psum_tensor(f"{name}_{n}", shape, F32))
        wqkv = sb("wqkv", [65, 3 * NL])
        wo = sb("wo", [128, 4, D])
        bo = sb("bo", [1, D])
        ones = sb("ones", [1, NT])
        halfpi = sb("halfpi", [NT, 1])
        xg = sb("xg", [NT, GS, D])
        xT = sb("xT", [65, GT])
        qkT = sb("qkT", [128, 8, GT])
        v = sb("v", [NT, GS, NL])
        fold = sb("fold", [NT, GS, WIDTH])
        work = sb("work", [NT, GS, WIDTH])
        low = sb("low", [NT, GS, WIDTH])
        probs = sb("probs", [NT, GS, WIDTH])
        probsT = sb("probsT", [NT, 2, WIDTH])
        negmax = sb("negmax", [NT, GS, NH])
        sums = sb("sums", [NT, GS, NH])
        oT = sb("oT", [128, GS, 4, NT])
        bAB = ps("bAB", [128, 2, 512])
        bS = ps("bS", [128, 2, 2, 512])
        bP = ps("bP", [128, 2, 512])
        loaded, set_up = sem("loaded"), sem("set_up")
        xg_ready, x_transposed, xT_ready, proj_made, proj_taken = (
            sem(n) for n in ("xg_ready", "x_transposed", "xT_ready", "proj_made", "proj_taken"))
        scores_made, folded, filtered, exp_done, normed, falloff_ready, phase_ready, waves_ready, damped = (
            sem(n) for n in ("scores_made", "folded", "filtered", "exp_done", "normed", "falloff_ready",
                             "phase_ready", "waves_ready", "damped"))
        pT_made, pT_taken, o_made, o_taken, y_made, y_taken, own, own_act = (
            sem(n) for n in ("pT_made", "pT_taken", "o_made", "o_taken", "y_made", "y_taken", "own", "act_own"))
        sem.start()
        block = ctx.enter_context(nc.Block())
        NPROJ = 8 + GS
        OWN, OWN_ACT = 10 * GS, GS

        @block.sync
        def _(sp):
            sp.dma_start(wqkv[:, :], aps[f"{name}_wqkv"]).then_inc(loaded, 16)
            sp.dma_start(wo[:, :, :], aps[f"{name}_wo"].rearrange("(j p) n -> p j n", p=128)).then_inc(loaded, 16)
            sp.dma_start(bo[:, :], aps[f"{name}_bo"]).then_inc(loaded, 16)

        @block.gpsimd
        def _(pool):
            nc.gpsimd.memset(xT[D:D + 1, :], 1.0).then_inc(set_up, 1)
            nc.gpsimd.memset(ones[:, :], 1.0).then_inc(set_up, 1)
            pool.wait_ge(set_up, START + 2)
            nc.gpsimd.memset(halfpi[:, :], math.pi / 2).then_inc(set_up, 1)
            pool.wait_ge(set_up, START + 3)
            with pool.Fori(0, NG) as g:
                pool.wait_ge(x_transposed, START + g)
                nc.gpsimd.tensor_copy(xg[:, :, :], core.xn[:, bass.ds(g * GS, GS), :]).then_inc(xg_ready, 1)

        @block.tensor
        def _(pe):
            pe.wait_ge(loaded, 48)
            pe.wait_ge(set_up, START + 3)
            with pe.Fori(0, NG) as g:
                pe.wait_ge(y_taken, START + g)
                pe.wait_ge(xg_ready, START + g + 1)
                transpose_each(core, bAB[:, 0, :], xg, D).then_inc(x_transposed, 1)
                pe.wait_ge(xT_ready, START + g + 1)
                for n in range(NPROJ):
                    pe.wait_ge(proj_taken, START + NPROJ * g + max(n - 1, 0))
                    if n < 8:
                        mm = nc.tensor.matmul(bAB[:, n % 2, 0:GT], wqkv[:, n * 128:(n + 1) * 128], xT[:, :],
                                              start=True, stop=True)
                    else:
                        s = n - 8
                        mm = nc.tensor.matmul(bAB[0:NT, n % 2, :], xT[:, s * NT:(s + 1) * NT], wqkv[:, 2 * NL:3 * NL],
                                              start=True, stop=True)
                    mm.then_inc(proj_made, 1)

                def scores(s):
                    pe.wait_ge(proj_taken, START + NPROJ * g + 8)
                    pe.wait_ge(filtered, START + GS * g + max(s - 1, 0))
                    for j in range(4):
                        for half in range(2):
                            rows = slice(half * HD, (half + 1) * HD)
                            mm = nc.tensor.matmul(bS[0:NT, s % 2, half, j * NT:(j + 1) * NT],
                                                  qkT[rows, j, s * NT:(s + 1) * NT],
                                                  qkT[rows, 4 + j, s * NT:(s + 1) * NT], start=True, stop=True)
                    mm.then_inc(scores_made, 1)

                for s in range(GS):
                    scores(s)

                def turn(s):
                    pe.wait_ge(damped, START + GS * g + s + 1)
                    pe.wait_ge(pT_taken, START + GS * g + s)
                    for n in range(NH):
                        mm = nc.tensor.transpose(bP[0:NT, n // 4, (n % 4) * NT:(n % 4 + 1) * NT],
                                                 probs[:, s, n * NT:(n + 1) * NT], core.ident[0:NT, 0:NT])
                    mm.then_inc(pT_made, 1)

                def weigh(s):
                    pe.wait_ge(pT_taken, START + GS * g + s + 1)
                    pe.wait_ge(proj_taken, START + NPROJ * (g + 1))
                    pe.wait_ge(o_taken, START + GS * g + s)
                    for j in range(4):
                        for half in range(2):
                            h = 2 * j + half
                            mm = nc.tensor.matmul(bAB[half * HD:(half + 1) * HD, 1, j * NT:(j + 1) * NT],
                                                  v[:, s, h * HD:(h + 1) * HD],
                                                  probsT[:, s % 2, (half * 4 + j) * NT:(half * 4 + j + 1) * NT],
                                                  start=True, stop=True)
                    mm.then_inc(o_made, 1)

                turn(0)
                for s in range(GS):
                    if s + 1 < GS:
                        turn(s + 1)
                    weigh(s)
                pe.wait_ge(o_taken, START + GS * (g + 1))
                for s in range(GS):
                    to = bAB[0:NT, 0, s * D:(s + 1) * D]
                    nc.tensor.matmul(to, ones[:, :], bo[:, :], start=True, stop=False)
                    for j in range(4):
                        mm = nc.tensor.matmul(to, oT[:, s, j, :], wo[:, j, :], start=False, stop=(j == 3))
                mm.then_inc(y_made, 1)

        @block.scalar
        def _(act):
            act.wait_ge(set_up, START + 3)
            with act.Fori(0, NG) as g:
                own_done = InOrder(act, own_act, g * OWN_ACT)
                act.wait_ge(x_transposed, START + g + 1)
                nc.scalar.copy(xT[0:D, :], bAB[0:D, 0, 0:GT]).then_inc(xT_ready, 1)
                for n in range(NPROJ):
                    act.wait_ge(proj_made, START + NPROJ * g + n + 1)
                    if n < 8:
                        ins = nc.scalar.copy(qkT[:, n, :], bAB[:, n % 2, 0:GT])
                    else:
                        ins = nc.scalar.copy(v[:, n - 8, :], bAB[0:NT, n % 2, :])
                    ins.then_inc(proj_taken, 1)

                def magnitude(s):
                    act.wait_ge(scores_made, START + GS * g + s + 1)
                    for half in range(2):
                        ins = nc.scalar.activation(fold[:, s, half * GT:(half + 1) * GT], bS[0:NT, s % 2, half, 0:GT],
                                                   ACT.Abs, scale=1618.0 / 8 / 3)
                    ins.then_inc(folded, 1)

                def exponentials(s):
                    act.wait_ge(filtered, START + GS * g + s + 1)
                    for n in range(NH):
                        p = probs[:, s, n * NT:(n + 1) * NT]
                        ins = nc.scalar.activation(p, p, ACT.Exp, bias=negmax[:, s, n:n + 1],
                                                   accum_out=sums[:, s, n:n + 1])
                    ins.then_inc(exp_done, 1)

                magnitude(0)
                magnitude(1)
                for s in range(GS):
                    exponentials(s)
                    if s + 2 < GS:
                        magnitude(s + 2)
                for s in range(GS):
                    act.wait_ge(normed, START + GS * g + s + 1)
                    nc.scalar.activation(fold[:, s, :], probs[:, s, :], ACT.Copy, scale=C1 / (2 * math.pi))
                    own_done(nc.scalar.activation(low[:, s, :], probs[:, s, :], ACT.Square))
                    nc.scalar.activation(low[:, s, :], low[:, s, :], ACT.Exp, scale=-1.0 / PHI).then_inc(falloff_ready, 1)
                for s in range(GS):
                    act.wait_ge(phase_ready, START + GS * g + s + 1)
                    nc.scalar.activation(fold[:, s, :], fold[:, s, :], ACT.Sin, scale=TURN)
                    nc.scalar.activation(work[:, s, :], probs[:, s, :], ACT.Sin, bias=halfpi[:, :],
                                         scale=-C2).then_inc(waves_ready, 1)
                for s in range(GS):
                    act.wait_ge(pT_made, START + GS * g + s + 1)
                    for half in range(2):
                        ins = nc.scalar.copy(probsT[:, s % 2, half * GT:(half + 1) * GT], bP[0:NT, half, 0:GT])
                    ins.then_inc(pT_taken, 1)
                    act.wait_ge(o_made, START + GS * g + s + 1)
                    nc.scalar.copy(oT[:, s, :, :].rearrange("p j t -> p (j t)"), bAB[:, 1, 0:GT]).then_inc(o_taken, 1)

        @block.vector
        def _(dve):
            with dve.Fori(0, NG) as g:
                own_done = InOrder(dve, own, g * OWN)
                for s in range(GS):
                    f, w, l, p = fold[:, s, :], work[:, s, :], low[:, s, :], probs[:, s, :]
                    dve.wait_ge(folded, START + GS * g + s + 1)
                    own_done(nc.vector.tensor_scalar(w, f, ROUND, ROUND, ALU.add, ALU.subtract))
                    own_done(nc.vector.tensor_tensor(f, f, w, ALU.subtract))
                    own_done(nc.vector.tensor_scalar(w, f, 0.0, None, ALU.is_ge))
                    own_done(nc.vector.scalar_tensor_tensor(out=w, in0=f, scalar=1.0 / 3, in1=w, op0=ALU.is_lt, op1=ALU.mult))
                    own_done(nc.vector.tensor_scalar(w, w, (1.0 / PHI - 1.0) / 8, 1.0 / 8, ALU.mult, ALU.add))
                    for half in range(2):
                        ins = nc.vector.tensor_tensor(probs[:, s, half * GT:(half + 1) * GT],
                                                      bS[0:NT, s % 2, half, 0:GT], work[:, s, half * GT:(half + 1) * GT],
                                                      ALU.mult)
                    own_done(ins)
                    nc.vector.tensor_reduce(negmax[:, s, :], p.rearrange("p (n m) -> p n m", n=NH), AX, ALU.max,
                                            negate=True).then_inc(filtered, 1)
                for s in range(GS):
                    dve.wait_ge(exp_done, START + GS * g + s + 1)
                    p3 = probs[:, s, :].rearrange("p (n m) -> p n m", n=NH)
                    own_done(nc.vector.reciprocal(sums[:, s, :], sums[:, s, :]))
                    nc.vector.tensor_tensor(p3, p3, bc(sums[:, s, :], NT, 2), ALU.mult).then_inc(normed, 1)
                for s in range(GS):
                    f, w = fold[:, s, :], work[:, s, :]
                    dve.wait_ge(falloff_ready, START + GS * g + s + 1)
                    own_done(nc.vector.tensor_scalar(w, f, ROUND, ROUND, ALU.add, ALU.subtract))
                    nc.vector.tensor_tensor(f, f, w, ALU.subtract).then_inc(phase_ready, 1)
                for s in range(GS):
                    f, w, l, p = fold[:, s, :], work[:, s, :], low[:, s, :], probs[:, s, :]
                    dve.wait_ge(waves_ready, START + GS * g + s + 1)
                    own_done(nc.vector.tensor_tensor(f, f, l, ALU.mult))
                    own_done(nc.vector.tensor_tensor(f, f, w, ALU.add))
                    nc.vector.tensor_tensor(p, p, f, ALU.mult).then_inc(damped, 1)
                dve.wait_ge(y_made, START + g + 1)
                hg = core.h[:, bass.ds(g * GS, GS), :]
                nc.vector.tensor_tensor(hg, hg, bAB[0:NT, 0, 0:GS * D].rearrange("p (s f) -> p s f", s=GS),
                                        ALU.add).then_inc(y_taken, 1)
                assert own_done.n == OWN, own_done.n


def tree_experts(core, name):
    nc, aps = core.nc, core.aps
    LEVELS = 8
    SLOTS = 2 ** LEVELS
    WIDE = 8
    PAIRS = SLOTS // (2 * WIDE)
    RW = 2 * WIDE
    ROWS = LEVELS - 3
    with ExitStack() as ctx:
        sem = Semaphores(nc, ctx, name)
        sb = lambda n, shape: ctx.enter_context(nc.sbuf_tensor(f"{name}_{n}", shape, F32))
        ps = lambda n, shape: ctx.enter_context(nc.psum_tensor(f"{name}_{n}", shape, F32))
        w1 = sb("w1", [65, SLOTS])
        w2 = sb("w2", [2 * D, PAIRS, WIDE * D])
        b2 = sb("b2", [128, 2, D])
        xg = sb("xg", [NT, GS, 2, D])
        xT = sb("xT", [2 * D, GT])
        x1T = sb("x1T", [65, GT])
        score = sb("score", [NT, GS, SLOTS])
        size = sb("size", [NT, GS, SLOTS])
        right = sb("right", [NT, GS, SLOTS])
        here = sb("here", [NT, GS, SLOTS])
        share = sb("share", [NT, GS, SLOTS])
        row_share = sb("row_share", [NT, GS, ROWS, RW])
        shareT = sb("shareT", [128, GS, 2, NT])
        chosen = sb("chosen", [NT, 2, ROWS * RW, D])
        shared = sb("shared", [NT, 2, ROWS * RW, D])
        idle = sb("idle", [NT, 2, PAIRS])
        total = sb("total", [NT, GS, D])
        bX = ps("bX", [128, 512])
        bL = ps("bL", [128, 2, 512])
        bY = ps("bY", [128, 2, 2, 512])
        loaded, set_up = sem("loaded"), sem("set_up")
        xg_ready, x_transposed, xT_ready, scores_made, scores_taken, size_ready = (
            sem(n) for n in ("xg_ready", "x_transposed", "xT_ready", "scores_made", "scores_taken", "size_ready"))
        share_ready, share_transposed, shareT_ready, bias_made, bias_taken, y_made, y_taken, own = (
            sem(n) for n in ("share_ready", "share_transposed", "shareT_ready", "bias_made", "bias_taken",
                             "y_made", "y_taken", "own"))
        weighed, path_shared, path_summed = (sem(n) for n in ("weighed", "path_shared", "path_summed"))
        sem.start()
        block = ctx.enter_context(nc.Block())
        OWN = 1 + 2 * (LEVELS - 1) + 1 + 1

        @block.sync
        def _(sp):
            sp.dma_start(w1[:, :], aps[f"{name}_w1"]).then_inc(loaded, 16)
            sp.dma_start(b2[:, :, :], aps[f"{name}_b2"].rearrange("(c p) n -> p c n", p=128)).then_inc(loaded, 16)
            sp.dma_start(w2[:, :, :], aps[f"{name}_w2"]).then_inc(loaded, 16)

        @block.gpsimd
        def _(pool):
            nc.gpsimd.memset(x1T[D:D + 1, :], 1.0).then_inc(set_up, 1)
            pool.wait_ge(set_up, START + 1)
            nc.gpsimd.memset(chosen[:, :, :, :], 0.0).then_inc(set_up, 1)
            pool.wait_ge(set_up, START + 2)
            nc.gpsimd.memset(here[:, :, 0:1], 0.0).then_inc(set_up, 1)
            nc.gpsimd.memset(here[:, :, 1:2], 1.0).then_inc(set_up, 1)
            pool.wait_ge(set_up, START + 4)
            with pool.Fori(0, NG) as g:
                pool.wait_ge(x_transposed, START + g)
                for c in range(2):
                    ins = nc.gpsimd.tensor_copy(xg[:, :, c, :], core.xn[:, bass.ds(g * GS, GS), :])
                ins.then_inc(xg_ready, 1)
                for s in range(GS):
                    pool.wait_ge(y_taken, START + GS * PAIRS * g + 2 * PAIRS * (s // 2) + 2 * PAIRS + s % 2 - 1)
                    pool.wait_ge(path_summed, START + GS * g + max(s - 1, 0))
                    nc.gpsimd.tensor_tensor(shared[:, s % 2, :, :], chosen[:, s % 2, :, :],
                                            bc(row_share[:, s, :, :].rearrange("p r k -> p (r k)"), D, 2),
                                            ALU.mult).then_inc(weighed, 1)
                    pool.wait_ge(weighed, START + GS * g + s + 1)
                    rows = shared[:, s % 2, :, :].rearrange("p (r k) f -> p r (k f)", r=ROWS)
                    nc.gpsimd.tensor_tensor(rows[:, :, 0:WIDE * D], rows[:, :, 0:WIDE * D],
                                            rows[:, :, WIDE * D:RW * D], ALU.add).then_inc(path_shared, 1)

        @block.tensor
        def _(pe):
            pe.wait_ge(loaded, 48)
            pe.wait_ge(set_up, START + 4)
            with pe.Fori(0, NG) as g:
                pe.wait_ge(bias_taken, START + g)
                pe.wait_ge(xg_ready, START + g + 1)
                for s in range(GS):
                    mm = nc.tensor.transpose(bX[:, s * NT:(s + 1) * NT], xg[:, s, :, :].rearrange("p c f -> p (c f)"),
                                             core.ident[0:NT, 0:NT])
                mm.then_inc(x_transposed, 1)
                pe.wait_ge(xT_ready, START + g + 1)
                pe.wait_ge(shareT_ready, START + g)
                for s in range(GS):
                    mm = nc.tensor.matmul(bL[0:NT, s // 2, (s % 2) * SLOTS:(s % 2 + 1) * SLOTS],
                                          x1T[:, s * NT:(s + 1) * NT], w1[:, :], start=True, stop=True)
                mm.then_inc(scores_made, 1)
                for n in range(GS * PAIRS):
                        s = n // (2 * PAIRS) * 2 + n % 2
                        p = n // 2 % PAIRS
                        pe.wait_ge(y_taken, START + GS * PAIRS * g + max(n - 1, 0))
                        for half in range(2):
                            rows = slice(half * D, (half + 1) * D)
                            mm = nc.tensor.matmul(bY[0:NT, s % 2, half, :], xT[rows, s * NT:(s + 1) * NT],
                                                  w2[rows, p, :], start=True, stop=True)
                        mm.then_inc(y_made, 1)
                pe.wait_ge(share_ready, START + g + 1)
                for s in range(GS):
                    for c in range(2):
                        mm = nc.tensor.transpose(bL[:, s // 2, ((s % 2) * 2 + c) * NT:((s % 2) * 2 + c + 1) * NT],
                                                 share[:, s, c * 128:(c + 1) * 128], core.ident[0:NT, 0:NT])
                mm.then_inc(share_transposed, 1)
                pe.wait_ge(shareT_ready, START + g + 1)
                for s in range(GS):
                    for c in range(2):
                        mm = nc.tensor.matmul(bX[0:NT, s * D:(s + 1) * D], shareT[:, s, c, :], b2[:, c, :],
                                              start=(c == 0), stop=(c == 1))
                mm.then_inc(bias_made, 1)

        @block.scalar
        def _(act):
            with act.Fori(0, NG) as g:
                act.wait_ge(x_transposed, START + g + 1)
                act.wait_ge(bias_made, START + g)
                nc.scalar.copy(xT[:, :], bX[:, 0:GT])
                nc.scalar.copy(x1T[0:D, :], bX[0:D, 0:GT]).then_inc(xT_ready, 1)
                act.wait_ge(scores_made, START + g + 1)
                act.wait_ge(share_ready, START + g)
                nc.scalar.copy(score[:, :, :].rearrange("p (b s) k -> p b (s k)", b=2), bL[0:NT, :, :]).then_inc(scores_taken, 1)
                act.wait_ge(scores_taken, START + g + 1)
                nc.scalar.activation(size[:, :, :], score[:, :, :], ACT.Abs).then_inc(size_ready, 1)
                act.wait_ge(size_ready, START + 2 * g + 1)
                nc.scalar.activation(size[:, :, :], size[:, :, :], ACT.Gelu).then_inc(size_ready, 1)
                act.wait_ge(share_transposed, START + g + 1)
                act.wait_ge(bias_made, START + g)
                for b in range(2):
                    ins = nc.scalar.copy(shareT[:, 2 * b:2 * b + 2, :, :].rearrange("p s c t -> p (s c t)"),
                                         bL[:, b, 0:4 * NT])
                ins.then_inc(shareT_ready, 1)

        @block.vector
        def _(dve):
            dve.wait_ge(set_up, START + 4)
            with dve.Fori(0, NG) as g:
                own_done = InOrder(dve, own, g * OWN)
                dve.wait_ge(scores_taken, START + g + 1)
                own_done(nc.vector.tensor_scalar(right[:, :, :], score[:, :, :], 0.0, None, ALU.is_gt))
                for l in range(LEVELS - 1):
                    a, b = 2 ** l, 2 ** (l + 1)
                    children = here[:, :, 2 * a:2 * b].rearrange("p s (k c) -> p s k c", c=2)
                    own_done(nc.vector.tensor_tensor(children[:, :, :, 1], here[:, :, a:b], right[:, :, a:b], ALU.mult))
                    own_done(nc.vector.tensor_tensor(children[:, :, :, 0], here[:, :, a:b], children[:, :, :, 1],
                                                     ALU.subtract))
                dve.wait_ge(size_ready, START + 2 * g + 2)
                dve.wait_ge(share_transposed, START + g)
                own_done(nc.vector.tensor_tensor(share[:, :, :], size[:, :, :], here[:, :, :], ALU.mult))
                ins = nc.vector.tensor_copy(row_share[:, :, 0, :], share[:, :, 0:RW])
                for r in range(1, ROWS):
                    a = 2 ** (r + 3)
                    for s in range(GS):
                        ins = nc.vector.tensor_reduce(row_share[:, s, r, :],
                                                      share[:, s, a:2 * a].rearrange("p (c k) -> p k c", k=RW),
                                                      AX, ALU.add)
                ins.then_inc(share_ready, 1)

                def sum_path(s):
                    dve.wait_ge(path_shared, START + GS * g + s + 1)
                    rows = shared[:, s % 2, :, :].rearrange("p (r k) f -> p f r k", r=ROWS)
                    nc.vector.tensor_reduce(total[:, s, :], rows[:, :, :, 0:WIDE], XY, ALU.add).then_inc(path_summed, 1)

                for s0 in range(0, GS, 2):
                    for p in range(PAIRS):
                        for s in (s0, s0 + 1):
                            n = (s0 * PAIRS) + 2 * p + s - s0
                            dve.wait_ge(y_made, START + GS * PAIRS * g + n + 1)
                            dve.wait_ge(y_taken, START + GS * PAIRS * g + max(n - 1, 0))
                            if p == 0 and s0:
                                dve.wait_ge(path_shared, START + GS * g + s - 1)
                            nc.vector.memset(idle[:, s % 2, p:p + 1], 0.0)
                            row = p.bit_length()
                            nc.vector.copy_predicated(
                                chosen[:, s % 2, row * RW:(row + 1) * RW, :],
                                bc(here[:, s, p * RW:(p + 1) * RW].bitcast(U32), D, 2),
                                bY[0:NT, s % 2, :, :].rearrange("p b (k f) -> p (b k) f", k=WIDE)).then_inc(y_taken, 1)
                        if p == PAIRS // 2 and s0:
                            sum_path(s0 - 2)
                            sum_path(s0 - 1)
                sum_path(GS - 2)
                sum_path(GS - 1)
                dve.wait_ge(path_summed, START + GS * (g + 1))
                hg = core.h[:, bass.ds(g * GS, GS), :]
                nc.vector.tensor_tensor(total[:, :, :], total[:, :, :], hg, ALU.add).then_inc(own, 1)
                dve.wait_ge(own, g * OWN + OWN)
                dve.wait_ge(bias_made, START + g + 1)
                nc.vector.tensor_tensor(hg, total[:, :, :], bX[0:NT, 0:GS * D].rearrange("p (s f) -> p s f", s=GS),
                                        ALU.add).then_inc(bias_taken, 1)
                assert own_done.n == OWN - 1, own_done.n


def phase_attention(core, name):
    nc, aps = core.nc, core.aps
    K = 32
    ROUND = 1.5 * 2.0 ** 23
    TURN = 6.283184
    HALF = TURN / 2
    with ExitStack() as ctx:
        sem = Semaphores(nc, ctx, name)
        sb = lambda n, shape: ctx.enter_context(nc.sbuf_tensor(f"{name}_{n}", shape, F32))
        ps = lambda n: ctx.enter_context(nc.psum_tensor(f"{name}_{n}", [128, 512], F32))
        wkq1 = sb("wkq1", [65, 2 * D])
        wv = sb("wv", [65, 2 * D])
        wg1 = sb("wg1", [65, 16])
        w2 = sb("w2", [2 * D, 2, 2 * K])
        b2 = sb("b2", [2 * K, 2])
        wg2 = sb("wg2", [17, 2])
        wo = sb("wo", [65, D])
        affine = sb("affine", [NT, 2, D])
        upto = sb("upto", [NT, NT])
        scale = sb("scale", [NT, 2])
        wave = sb("wave", [NT, 2, D])
        turns = sb("turns", [NT, 2, D])
        halfpi = sb("halfpi", [128, 1])
        xg = sb("xg", [NT, GS, D])
        xT = sb("xT", [65, GT])
        hid = sb("hid", [2 * D, GT])
        ph = sb("ph", [2 * K, 2, GT])
        feat = sb("feat", [2 * K, 2, GT])
        vv = sb("vv", [NT, GS, 2, D])
        gT = sb("gT", [17, GT])
        gate = sb("gate", [NT, GS, 2])
        gsum = sb("gsum", [NT, GS])
        turned = sb("turned", [NT, GS, 2, D])
        mix = sb("mix", [NT, GS, 2, D])
        causal = sb("causal", [NT, GS, NT])
        both = sb("both", [NT, GS, D])
        sq = sb("sq", [NT, GS, D])
        mean = sb("mean", [NT, GS])
        var = sb("var", [NT, GS])
        nT = sb("nT", [65, GT])
        bX, bH, bV, bG, bK, bQ, bC, bR = (ps(n) for n in ("bX", "bH", "bV", "bG", "bK", "bQ", "bC", "bR"))
        loaded, set_up, phase_turned, wave_ready = (sem(n) for n in ("loaded", "set_up", "phase_turned", "wave_ready"))
        xg_ready, x_transposed, xT_ready, hid_made, hid_ready, v_made, v_taken, g1_made, g1_taken = (
            sem(n) for n in ("xg_ready", "x_transposed", "xT_ready", "hid_made", "hid_ready", "v_made", "v_taken",
                             "g1_made", "g1_taken"))
        g2_made, gate_centered, gate_exp, phases_made, feat_ready, a_made, a_taken, content_made = (
            sem(n) for n in ("g2_made", "gate_centered", "gate_exp", "phases_made", "feat_ready", "a_made", "a_taken",
                             "content_made"))
        turned_ready, run_made, centered, squared, summed, rooted, normed, n_transposed, nT_ready, y_made, y_taken = (
            sem(n) for n in ("turned_ready", "run_made", "centered", "squared", "summed", "rooted", "normed",
                             "n_transposed", "nT_ready", "y_made", "y_taken"))
        own, own_act = sem("own"), sem("act_own")
        sem.start()
        block = ctx.enter_context(nc.Block())
        OWN, OWN_ACT = 17, 2
        NLOAD = 11

        @block.sync
        def _(sp):
            for to, what in ((wkq1, "wkq1"), (wv, "wv"), (wg1, "wg1"), (w2, "w2"), (b2, "b2"), (wg2, "wg2"), (wo, "wo")):
                sp.dma_start(to[:], aps[f"{name}_{what}"]).then_inc(loaded, 16)
            sp.dma_start(affine[:, :, :], aps[f"{name}_affine"].partition_broadcast(NT)).then_inc(loaded, 16)
            sp.dma_start(upto[:, :], aps["upto"]).then_inc(loaded, 16)
            sp.dma_start(scale[:, :], aps["position_scale"]).then_inc(loaded, 16)
            sp.dma_start(turns[:, 1, :], aps[f"{name}_base_phases"]).then_inc(loaded, 16)

        @block.gpsimd
        def _(pool):
            for n, to in enumerate((xT[D:D + 1, :], nT[D:D + 1, :], gT[:, :])):
                nc.gpsimd.memset(to, 1.0).then_inc(set_up, 1)
                pool.wait_ge(set_up, START + n + 1)
            nc.gpsimd.memset(halfpi[:, :], math.pi / 2).then_inc(set_up, 1)
            pool.wait_ge(set_up, START + 4)
            with pool.Fori(0, NG) as g:
                pool.wait_ge(x_transposed, START + g)
                nc.gpsimd.tensor_copy(xg[:, :, :], core.xn[:, bass.ds(g * GS, GS), :]).then_inc(xg_ready, 1)

        @block.tensor
        def _(pe):
            pe.wait_ge(loaded, 16 * NLOAD)
            pe.wait_ge(set_up, START + 4)
            of = lambda s: slice(s * NT, (s + 1) * NT)
            with pe.Fori(0, NG) as g:
                pe.wait_ge(xg_ready, START + g + 1)
                transpose_each(core, bX, xg, D).then_inc(x_transposed, 1)
                pe.wait_ge(xT_ready, START + g + 1)
                nc.tensor.matmul(bH[:, 0:GT], wkq1[:, :], xT[:, :], start=True, stop=True).then_inc(hid_made, 1)
                for s in range(GS):
                    mm = nc.tensor.matmul(bV[0:NT, s * 2 * D:(s + 1) * 2 * D], xT[:, of(s)], wv[:, :], start=True, stop=True)
                mm.then_inc(v_made, 1)
                pe.wait_ge(gate_centered, START + g)
                nc.tensor.matmul(bG[0:16, 0:GT], wg1[:, :], xT[:, :], start=True, stop=True).then_inc(g1_made, 1)
                pe.wait_ge(hid_ready, START + g + 1)
                pe.wait_ge(a_taken, START + g)
                pe.wait_ge(nT_ready, START + g)
                nc.tensor.matmul(bK[0:2 * K, 0:GT], w2[:, 0, :], hid[:, :], start=True, stop=True)
                nc.tensor.matmul(bQ[0:2 * K, 0:GT], w2[:, 1, :], hid[:, :], start=True, stop=True).then_inc(phases_made, 1)
                pe.wait_ge(g1_taken, START + g + 1)
                for s in range(GS):
                    mm = nc.tensor.matmul(bG[0:NT, 2 * s:2 * s + 2], gT[:, of(s)], wg2[:, :], start=True, stop=True)
                mm.then_inc(g2_made, 1)
                pe.wait_ge(feat_ready, START + g + 1)
                for s in range(GS):
                    mm = nc.tensor.matmul(bK[0:NT, of(s)], feat[:, 0, of(s)], feat[:, 1, of(s)], start=True, stop=True)
                mm.then_inc(a_made, 1)
                pe.wait_ge(turned_ready, START + g + 1)
                nc.tensor.matmul(bR[0:NT, :], upto[:, :], turned[:, :, :, :].rearrange("p s c f -> p (s c f)"),
                                 start=True, stop=True).then_inc(run_made, 1)
                pe.wait_ge(a_taken, START + g + 1)
                pe.wait_ge(y_taken, START + g)
                for s in range(GS):
                    mm = nc.tensor.matmul(bC[0:NT, s * D:(s + 1) * D], causal[:, s, :], vv[:, s, 0, :], start=True, stop=True)
                mm.then_inc(content_made, 1)
                pe.wait_ge(normed, START + g + 1)
                transpose_each(core, bQ, both, D).then_inc(n_transposed, 1)
                pe.wait_ge(nT_ready, START + g + 1)
                for s in range(GS):
                    mm = nc.tensor.matmul(bC[0:NT, s * D:(s + 1) * D], nT[:, of(s)], wo[:, :], start=True, stop=True)
                mm.then_inc(y_made, 1)

        @block.scalar
        def _(act):
            act.wait_ge(loaded, 16 * NLOAD)
            act.wait_ge(set_up, START + 4)
            act.wait_ge(phase_turned, START + 1)
            nc.scalar.activation(wave[:, 0, :], turns[:, 0, :], ACT.Sin, bias=halfpi[0:NT, :], scale=-TURN)
            nc.scalar.activation(wave[:, 1, :], turns[:, 1, :], ACT.Sin, scale=TURN).then_inc(wave_ready, 1)
            with act.Fori(0, NG) as g:
                own_done = InOrder(act, own_act, g * OWN_ACT)
                act.wait_ge(x_transposed, START + g + 1)
                nc.scalar.copy(xT[0:D, :], bX[0:D, 0:GT]).then_inc(xT_ready, 1)
                act.wait_ge(hid_made, START + g + 1)
                nc.scalar.activation(hid[:, :], bH[:, 0:GT], ACT.Tanh).then_inc(hid_ready, 1)
                act.wait_ge(v_made, START + g + 1)
                act.wait_ge(content_made, START + g)
                act.wait_ge(turned_ready, START + g)
                nc.scalar.copy(vv[:, :, :, :].rearrange("p s c f -> p (s c f)"), bV[0:NT, :]).then_inc(v_taken, 1)
                act.wait_ge(g1_made, START + g + 1)
                nc.scalar.activation(gT[0:16, :], bG[0:16, 0:GT], ACT.Relu).then_inc(g1_taken, 1)
                act.wait_ge(phases_made, START + g + 1)
                nc.scalar.activation(ph[:, 0, :], bK[0:2 * K, 0:GT], ACT.Tanh, bias=b2[:, 0:1])
                own_done(nc.scalar.activation(ph[:, 1, :], bQ[0:2 * K, 0:GT], ACT.Tanh, bias=b2[:, 1:2]))
                own_done(nc.scalar.activation(ph[0:K, :, :], ph[0:K, :, :], ACT.Abs))
                nc.scalar.activation(feat[0:K, :, :], ph[0:K, :, :], ACT.Sin, bias=halfpi[0:K, :], scale=-HALF)
                nc.scalar.activation(feat[K:2 * K, :, :], ph[K:2 * K, :, :], ACT.Sin, scale=HALF).then_inc(feat_ready, 1)
                act.wait_ge(gate_centered, START + g + 1)
                nc.scalar.activation(gate[:, :, :], gate[:, :, :], ACT.Exp).then_inc(gate_exp, 1)
                act.wait_ge(centered, START + g + 1)
                nc.scalar.activation(sq[:, :, :], both[:, :, :], ACT.Square).then_inc(squared, 1)
                act.wait_ge(summed, START + g + 1)
                nc.scalar.activation(var[:, :], var[:, :], ACT.Sqrt, bias=core.eps[0:NT, 0:1], scale=1.0 / D).then_inc(rooted, 1)
                act.wait_ge(n_transposed, START + g + 1)
                nc.scalar.copy(nT[0:D, :], bQ[0:D, 0:GT]).then_inc(nT_ready, 1)

        @block.vector
        def _(dve):
            dve.wait_ge(loaded, 16 * NLOAD)
            first = InOrder(dve, own)
            first(nc.vector.tensor_scalar(turns[:, 1, :], turns[:, 1, :], 1 / (2 * math.pi), None, ALU.mult))
            first(nc.vector.tensor_scalar(turns[:, 0, :], turns[:, 1, :], ROUND, ROUND, ALU.add, ALU.subtract))
            first(nc.vector.tensor_tensor(turns[:, 1, :], turns[:, 1, :], turns[:, 0, :], ALU.subtract))
            first(nc.vector.tensor_scalar(turns[:, 0, :], turns[:, 1, :], -1.0, None, ALU.mult))
            nc.vector.tensor_tensor(turns[:, 0, :], turns[:, 0, :], turns[:, 1, :], ALU.max).then_inc(phase_turned, 1)
            dve.wait_ge(wave_ready, START + 1)
            with dve.Fori(0, NG) as g:
                own_done = InOrder(dve, own, g * OWN + 4)
                dve.wait_ge(v_taken, START + g + 1)
                dve.wait_ge(run_made, START + g)
                for c in range(2):
                    ins = nc.vector.tensor_tensor(turned[:, :, c, :], vv[:, :, 1, :], bc(wave[:, c, :], GS, 1), ALU.mult)
                ins.then_inc(turned_ready, 1)
                dve.wait_ge(g2_made, START + g + 1)
                own_done(nc.vector.tensor_copy(gate[:, :, :], bG[0:NT, 0:2 * GS].rearrange("p (s c) -> p s c", c=2)))
                own_done(nc.vector.tensor_tensor(gsum[:, :], gate[:, :, 0], gate[:, :, 1], ALU.max))
                nc.vector.tensor_tensor(gate[:, :, :], gate[:, :, :], bc(gsum[:, :], 2, 2), ALU.subtract).then_inc(gate_centered, 1)
                dve.wait_ge(a_made, START + g + 1)
                dve.wait_ge(content_made, START + g)
                nc.vector.tensor_tensor(causal[:, :, :], bK[0:NT, 0:GT].rearrange("p (s t) -> p s t", s=GS),
                                        bc(upto[:, :], GS, 1), ALU.mult).then_inc(a_taken, 1)
                dve.wait_ge(gate_exp, START + g + 1)
                own_done(nc.vector.tensor_tensor(gsum[:, :], gate[:, :, 0], gate[:, :, 1], ALU.add))
                own_done(nc.vector.reciprocal(gsum[:, :], gsum[:, :]))
                own_done(nc.vector.tensor_tensor(gate[:, :, :], gate[:, :, :], bc(gsum[:, :], 2, 2), ALU.mult))
                own_done(nc.vector.tensor_tensor(gate[:, :, :], gate[:, :, :], bc(scale[:, :], GS, 1), ALU.mult))
                dve.wait_ge(run_made, START + g + 1)
                own_done(nc.vector.tensor_tensor(mix[:, :, :, :].rearrange("p s c f -> p s (c f)"),
                                                 bR[0:NT, :].rearrange("p (s x) -> p s x", s=GS),
                                                 bc(wave[:, :, :].rearrange("p c f -> p (c f)"), GS, 1), ALU.mult))
                own_done(nc.vector.tensor_tensor(both[:, :, :], mix[:, :, 0, :], mix[:, :, 1, :], ALU.add))
                own_done(nc.vector.tensor_tensor(both[:, :, :], both[:, :, :], bc(gate[:, :, 0], D, 2), ALU.mult))
                dve.wait_ge(content_made, START + g + 1)
                own_done(nc.vector.tensor_tensor(mix[:, :, 0, :], bC[0:NT, 0:GS * D].rearrange("p (s f) -> p s f", s=GS),
                                                 bc(gate[:, :, 1], D, 2), ALU.mult))
                own_done(nc.vector.tensor_tensor(both[:, :, :], both[:, :, :], mix[:, :, 0, :], ALU.add))
                own_done(nc.vector.tensor_reduce(mean[:, :], both[:, :, :], AX, ALU.add))
                own_done(nc.vector.tensor_scalar(mean[:, :], mean[:, :], 1.0 / D, None, ALU.mult))
                nc.vector.tensor_tensor(both[:, :, :], both[:, :, :], bc(mean[:, :], D, 2), ALU.subtract).then_inc(centered, 1)
                dve.wait_ge(squared, START + g + 1)
                nc.vector.tensor_reduce(var[:, :], sq[:, :, :], AX, ALU.add).then_inc(summed, 1)
                dve.wait_ge(rooted, START + g + 1)
                own_done(nc.vector.reciprocal(var[:, :], var[:, :]))
                own_done(nc.vector.tensor_tensor(both[:, :, :], both[:, :, :], bc(var[:, :], D, 2), ALU.mult))
                own_done(nc.vector.tensor_tensor(both[:, :, :], both[:, :, :], bc(affine[:, 0, :], GS, 1), ALU.mult))
                nc.vector.tensor_tensor(both[:, :, :], both[:, :, :], bc(affine[:, 1, :], GS, 1), ALU.add).then_inc(normed, 1)
                hg = core.h[:, bass.ds(g * GS, GS), :]
                own_done(nc.vector.tensor_tensor(hg, hg, core.xn[:, bass.ds(g * GS, GS), :], ALU.add))
                dve.wait_ge(y_made, START + g + 1)
                nc.vector.tensor_tensor(hg, hg, bC[0:NT, 0:GS * D].rearrange("p (s f) -> p s f", s=GS),
                                        ALU.add).then_inc(y_taken, 1)
                assert own_done.n == OWN, own_done.n


def expert_heads(core, name):
    nc, aps = core.nc, core.aps
    NH, NE, HD = 4, 4, 16
    NEG = -3.0e38
    with ExitStack() as ctx:
        sem = Semaphores(nc, ctx, name)
        sb = lambda n, shape: ctx.enter_context(nc.sbuf_tensor(f"{name}_{n}", shape, F32))
        ps = lambda n, shape: ctx.enter_context(nc.psum_tensor(f"{name}_{n}", shape, F32))
        whl = sb("whl", [65, D])
        wqk = sb("wqk", [D, NE + 1, D])
        wv = sb("wv", [D, D])
        wgate = sb("wgate", [128, 2, NH * NE])
        bgate = sb("bgate", [NT, NH * NE])
        wfc1 = sb("wfc1", [65, D])
        wfc2 = sb("wfc2", [65, D])
        wfg = sb("wfg", [D, NH])
        affine = sb("affine", [NT, 4, HD])
        headmask = sb("headmask", [D, NH])
        future = sb("future", [NT, NT])
        resid = sb("resid", [NT, NH, HD])
        xg = sb("xg", [NT, GS, D])
        xT = sb("xT", [65, GT])
        sT = sb("sT", [D, GT])
        qkT = sb("qkT", [D, NE + 1, GT])
        kmask = sb("kmask", [D, GS, NH, NT])
        v = sb("v", [NT, GS, NH, 32])
        present = sb("present", [NT, GS, D])
        probs = sb("probs", [NT, 2, 2, NH, NT])
        probsT = sb("probsT", [NT, 2, NH, NE, NT])
        negmax = sb("negmax", [NT, 2, 2 * NH])
        sums = sb("sums", [NT, GS, NE, NH])
        oT = sb("oT", [128, NE, NT])
        outs = sb("outs", [NT, GS, NH, NE, HD])
        outsT = sb("outsT", [128, GS, 2, NT])
        gate = sb("gate", [NT, GS * NH, NE])
        fold = sb("fold", [NT, GS * NH])
        mixed = sb("mixed", [NT, GS, NH * HD])
        fx = sb("fx", [NT, GS, D])
        kept = sb("kept", [NT, GS, D])
        fT = sb("fT", [65, GT])
        keptT = sb("keptT", [D, GT])
        hT = sb("hT", [65, GT])
        sq = sb("sq", [NT, GS, D])
        var = sb("var", [NT, GS * NH])
        headgate = sb("headgate", [NT, GS, NH])
        headsum = sb("headsum", [NT, GS])
        bAB = ps("bAB", [128, 2, 512])
        bS = ps("bS", [128, 2, 2, 512])
        bP = ps("bP", [128, 2, 512])
        bA, bB = bAB[:, 0, :], bAB[:, 1, :]

        loaded, set_up, own, own_act = sem("loaded"), sem("set_up"), sem("own"), sem("act_own")
        pre_x, pre_xT, pre_s, pre_taken = (sem(n) for n in ("pre_x", "pre_xT", "pre_s", "pre_taken"))
        xg_ready, x_transposed, xT_ready, proj_made, proj_taken, sx_made, sx_taken, kmask_ready = (
            sem(n) for n in ("xg_ready", "x_transposed", "xT_ready", "proj_made", "proj_taken", "sx_made",
                             "sx_taken", "kmask_ready"))
        scores_made, masked, exp_done, pT_made, pT_taken, o_made, o_taken, o_turned, outs_ready = (
            sem(n) for n in ("scores_made", "masked", "exp_done", "pT_made", "pT_taken", "o_made", "o_taken",
                             "o_turned", "outs_ready"))
        outs_turned, outsT_ready, gate_made, gate_centered, gate_exp, f_ready, f_turned, fT_ready = (
            sem(n) for n in ("outs_turned", "outsT_ready", "gate_made", "gate_centered", "gate_exp", "f_ready",
                             "f_turned", "fT_ready"))
        fc1_made, h_ready, fc2_made, fout_ready, fout_turned, foutT_ready, hg_made, hg_centered, hg_exp = (
            sem(n) for n in ("fc1_made", "h_ready", "fc2_made", "fout_ready", "fout_turned", "foutT_ready",
                             "hg_made", "hg_centered", "hg_exp"))
        norm_sems = [[sem(f"{w}{n}") for w in ("centered", "squared", "summed", "rooted")] for n in range(2)]
        done = sem("done")
        sem.start()
        block = ctx.enter_context(nc.Block())
        NLOAD = 11
        PAIRS = (0, 2, 3)
        NPROJ = len(PAIRS) + 2
        NU = 2 * GS
        OWN, OWN_ACT = 43, 2
        of = lambda s: slice(s * NT, (s + 1) * NT)

        @block.sync
        def _(sp):
            for to, what in ((whl, "whl"), (wqk, "wqk"), (wv, "wv"), (wgate, "wgate"), (wfc1, "wfc1"), (wfc2, "wfc2"),
                             (wfg, "wfg")):
                sp.dma_start(to[:], aps[f"{name}_{what}"]).then_inc(loaded, 16)
            sp.dma_start(bgate[:, :], aps[f"{name}_bgate"].partition_broadcast(NT)).then_inc(loaded, 16)
            sp.dma_start(affine[:, :, :], aps[f"{name}_affine"].partition_broadcast(NT)).then_inc(loaded, 16)
            sp.dma_start(headmask[:, :], aps["headmask4"]).then_inc(loaded, 16)
            sp.dma_start(future[:, :], aps["future"]).then_inc(loaded, 16)

        @block.gpsimd
        def _(pool):
            for n, (to, value) in enumerate(((xT[D:D + 1, :], 1.0), (fT[D:D + 1, :], 1.0), (hT[D:D + 1, :], 1.0),
                                             (v[:, :, :, :], 0.0))):
                nc.gpsimd.memset(to, value).then_inc(set_up, 1)
                pool.wait_ge(set_up, START + n + 1)
            with pool.Fori(0, NG) as g:
                pool.wait_ge(x_transposed, START + g)
                nc.gpsimd.tensor_copy(xg[:, :, :], core.xn[:, bass.ds(g * GS, GS), :]).then_inc(xg_ready, 1)

        @block.tensor
        def _(pe):
            pe.wait_ge(loaded, 16 * NLOAD)
            pe.wait_ge(set_up, START + 4)
            for s in range(GS):
                mm = nc.tensor.transpose(bA[0:D, of(s)], core.xn[:, s, :], core.ident[0:NT, 0:NT])
            mm.then_inc(pre_x, 1)
            pe.wait_ge(pre_xT, START + 1)
            for s in range(GS):
                mm = nc.tensor.matmul(bB[0:NT, s * D:(s + 1) * D], xT[:, of(s)], whl[:, :], start=True, stop=True)
            mm.then_inc(pre_s, 1)
            pe.wait_ge(pre_taken, START + 1)
            with pe.Fori(0, NG) as g:
                pe.wait_ge(done, START + g)
                pe.wait_ge(xg_ready, START + g + 1)
                transpose_each(core, bA, xg, D).then_inc(x_transposed, 1)
                pe.wait_ge(xT_ready, START + g + 1)
                for n in range(NPROJ):
                    bank = bAB[:, n % 2, :]
                    if n == 1:
                        pe.wait_ge(proj_taken, START + NPROJ * g + 1)
                    elif n > 1:
                        pe.wait_ge(proj_taken, START + NPROJ * g + n - 1)
                    if n == 0:
                        mm = nc.tensor.matmul(bank[0:D, 0:GT], whl[:, :], xT[:, :], start=True, stop=True)
                    elif n <= len(PAIRS):
                        first = PAIRS[n - 1]
                        mm = nc.tensor.matmul(bank[:, 0:GT], wqk[:, first:first + 2, :].rearrange("p e f -> p (e f)"),
                                              sT[:, :], start=True, stop=True)
                    else:
                        for s in range(GS):
                            mm = nc.tensor.matmul(bank[0:NT, s * D:(s + 1) * D], sT[:, of(s)], wv[:, :], start=True, stop=True)
                    mm.then_inc(proj_made, 1)
                pe.wait_ge(proj_taken, START + NPROJ * g + NPROJ - 1)
                for s in range(GS):
                    mm = nc.tensor.matmul(bB[0:NT, s * D:(s + 1) * D], xT[:, of(s)], whl[:, :], start=True, stop=True)
                mm.then_inc(sx_made, 1)

                def scores(u):
                    s, pair = u // 2, u % 2
                    pe.wait_ge(kmask_ready, START + GS * g + s + 1)
                    pe.wait_ge(masked, START + NU * g + max(u - 1, 0))
                    for e in range(2):
                        mm = nc.tensor.matmul(bS[0:NT, u % 2, e, 0:GT], qkT[:, 2 * pair + e, of(s)],
                                              kmask[:, s, :, :].rearrange("p n t -> p (n t)"), start=True, stop=True)
                    mm.then_inc(scores_made, 1)

                def turn(u):
                    pe.wait_ge(exp_done, START + NU * g + u + 1)
                    pe.wait_ge(pT_taken, START + NU * g + u)
                    for n in range(NH):
                        for e in range(2):
                            mm = nc.tensor.transpose(bP[0:NT, n // 2, of(n % 2 * 2 + e)], probs[:, u % 2, e, n, :],
                                                     core.ident[0:NT, 0:NT])
                    mm.then_inc(pT_made, 1)

                def weigh(s):
                    pe.wait_ge(pT_taken, START + NU * g + 2 * s + 2)
                    pe.wait_ge(proj_taken, START + NPROJ * (g + 1))
                    for n in range(NH):
                        mm = nc.tensor.matmul(bA[32 * n:32 * n + 32, 0:GT], v[:, s, n, :],
                                              probsT[:, s % 2, n, :, :].rearrange("p e t -> p (e t)"),
                                              start=True, stop=True, tile_position=(0, 32 * n))
                    mm.then_inc(o_made, 1)
                    pe.wait_ge(o_taken, START + GS * g + s + 1)
                    pe.wait_ge(sx_taken, START + g + 1)
                    pe.wait_ge(outs_ready, START + GS * g + s)
                    for e in range(NE):
                        mm = nc.tensor.transpose(bB[0:NT, e * 128:(e + 1) * 128], oT[:, e, :], core.ident[:, :])
                    mm.then_inc(o_turned, 1)

                scores(0)
                for u in range(NU):
                    if u + 1 < NU:
                        scores(u + 1)
                    turn(u)
                    if u % 2 == 0 and u:
                        weigh(u // 2 - 1)
                weigh(GS - 1)
                pe.wait_ge(outs_ready, START + GS * (g + 1))
                for s in range(GS):
                    for c in range(2):
                        mm = nc.tensor.transpose(bAB[:, s // 2, of(s % 2 * 2 + c)],
                                                 outs[:, s, 2 * c:2 * c + 2, :, :].rearrange("p n e f -> p (n e f)"),
                                                 core.ident[0:NT, 0:NT])
                mm.then_inc(outs_turned, 1)
                pe.wait_ge(outsT_ready, START + g + 1)
                for s in range(GS):
                    for c in range(2):
                        mm = nc.tensor.matmul(bA[0:NT, s * 16:(s + 1) * 16], outsT[:, s, c, :], wgate[:, c, :],
                                              start=(c == 0), stop=(c == 1))
                mm.then_inc(gate_made, 1)
                pe.wait_ge(f_ready, START + g + 1)
                transpose_each(core, bB, fx, D).then_inc(f_turned, 1)
                pe.wait_ge(fT_ready, START + g + 1)
                nc.tensor.matmul(bA[0:D, 0:GT], wfc1[:, :], fT[:, :], start=True, stop=True).then_inc(fc1_made, 1)
                pe.wait_ge(h_ready, START + g + 1)
                for s in range(GS):
                    mm = nc.tensor.matmul(bB[0:NT, s * D:(s + 1) * D], hT[:, of(s)], wfc2[:, :], start=True, stop=True)
                mm.then_inc(fc2_made, 1)
                pe.wait_ge(fout_ready, START + g + 1)
                transpose_each(core, bA, fx, D).then_inc(fout_turned, 1)
                pe.wait_ge(foutT_ready, START + g + 1)
                for s in range(GS):
                    mm = nc.tensor.matmul(bB[0:NT, s * NH:(s + 1) * NH], fT[0:D, of(s)], wfg[:, :], start=True, stop=True)
                mm.then_inc(hg_made, 1)

        @block.scalar
        def _(act):
            act.wait_ge(loaded, 16 * NLOAD)
            act.wait_ge(set_up, START + 4)
            act.wait_ge(pre_x, START + 1)
            nc.scalar.copy(xT[0:D, :], bA[0:D, 0:GT]).then_inc(pre_xT, 1)
            with act.Fori(0, NG) as g:
                act.wait_ge(x_transposed, START + g + 1)
                nc.scalar.copy(xT[0:D, :], bA[0:D, 0:GT]).then_inc(xT_ready, 1)
                for n in range(NPROJ):
                    act.wait_ge(proj_made, START + NPROJ * g + n + 1)
                    bank = bAB[:, n % 2, :]
                    if n == 0:
                        ins = nc.scalar.copy(sT[:, :], bank[0:D, 0:GT])
                    elif n <= len(PAIRS):
                        for m in range(2):
                            e = PAIRS[n - 1] + m
                            if (e, n) != (3, 3):
                                ins = nc.scalar.activation(qkT[:, e, :], bank[m * D:(m + 1) * D, 0:GT], ACT.Copy,
                                                           scale=float(HD) ** 0.5 if e < NE else 1.0)
                    else:
                        ins = nc.scalar.copy(v[:, :, :, 0:HD].rearrange("p s n f -> p (s n) f"),
                                             bank[0:NT, 0:GS * D].rearrange("p (x f) -> p x f", f=HD))
                    ins.then_inc(proj_taken, 1)

                def exponentials(u):
                    s, pair = u // 2, u % 2
                    act.wait_ge(masked, START + NU * g + u + 1)
                    for e in range(2):
                        for n in range(NH):
                            p = probs[:, u % 2, e, n, :]
                            ins = nc.scalar.activation(p, p, ACT.Exp, bias=negmax[:, u % 2, e * NH + n:e * NH + n + 1],
                                                       accum_out=sums[:, s, 2 * pair + e, n:n + 1])
                    ins.then_inc(exp_done, 1)

                def take_context(s):
                    act.wait_ge(o_made, START + GS * g + s + 1)
                    act.wait_ge(o_turned, START + GS * g + s)
                    nc.scalar.copy(oT[:, :, :].rearrange("p e t -> p (e t)"), bA[:, 0:GT]).then_inc(o_taken, 1)

                for u in range(NU):
                    exponentials(u)
                    act.wait_ge(pT_made, START + NU * g + u + 1)
                    act.wait_ge(o_made, START + GS * g + max(u // 2 - 1, 0))
                    pair = u % 2
                    for b in range(2):
                        ins = nc.scalar.copy(probsT[:, u // 2 % 2, 2 * b:2 * b + 2, 2 * pair:2 * pair + 2, :]
                                             .rearrange("p n e t -> p n (e t)"),
                                             bP[0:NT, b, 0:GT].rearrange("p (n x) -> p n x", n=2))
                    ins.then_inc(pT_taken, 1)
                    if u % 2 == 0 and u:
                        take_context(u // 2 - 1)
                take_context(GS - 1)
                act.wait_ge(outs_turned, START + g + 1)
                for b in range(2):
                    ins = nc.scalar.copy(outsT[:, 2 * b:2 * b + 2, :, :].rearrange("p s c t -> p (s c t)"),
                                         bAB[:, b, 0:4 * NT])
                ins.then_inc(outsT_ready, 1)
                act.wait_ge(gate_centered, START + g + 1)
                nc.scalar.activation(gate[:, :, :], gate[:, :, :], ACT.Exp).then_inc(gate_exp, 1)

                def norm(n):
                    centered, squared, summed, rooted = norm_sems[n]
                    act.wait_ge(centered, START + g + 1)
                    nc.scalar.activation(sq[:, :, :], mixed[:, :, :], ACT.Square).then_inc(squared, 1)
                    act.wait_ge(summed, START + g + 1)
                    nc.scalar.activation(var[:, :], var[:, :], ACT.Sqrt, bias=core.eps[0:NT, 1:2],
                                         scale=1.0 / HD).then_inc(rooted, 1)

                norm(0)
                act.wait_ge(f_turned, START + g + 1)
                nc.scalar.copy(fT[0:D, :], bB[0:D, 0:GT]).then_inc(fT_ready, 1)
                norm(1)
                act.wait_ge(fout_turned, START + g + 1)
                nc.scalar.copy(fT[0:D, :], bA[0:D, 0:GT]).then_inc(foutT_ready, 1)
                act.wait_ge(hg_centered, START + g + 1)
                nc.scalar.activation(headgate[:, :, :], headgate[:, :, :], ACT.Exp).then_inc(hg_exp, 1)

        @block.vector
        def _(dve):
            dve.wait_ge(loaded, 16 * NLOAD)
            dve.wait_ge(pre_s, START + 1)
            for n in range(NH):
                ins = nc.vector.tensor_copy(resid[:, n, :], bB[0:NT, n * D + n * HD:n * D + (n + 1) * HD])
            ins.then_inc(pre_taken, 1)
            dve.wait_ge(pre_taken, START + 1)
            heads = lambda t: t.rearrange("p s (n f) -> p (s n) f", n=NH)
            with dve.Fori(0, NG) as g:
                own_done = InOrder(dve, own, g * OWN)
                dve.wait_ge(proj_taken, START + NPROJ * g + NPROJ - 1)
                for s in range(GS):
                    ins = nc.vector.tensor_tensor(kmask[:, s, :, :], bc(qkT[:, NE, of(s)], NH, 1),
                                                  bc(headmask[:, :], NT, 2), ALU.mult).then_inc(kmask_ready, 1)
                dve.wait_ge(sx_made, START + g + 1)
                nc.vector.tensor_scalar(present[:, :, :].rearrange("p s f -> p (s f)"), bB[0:NT, 0:GS * D], 0.0, None,
                                        ALU.not_equal).then_inc(sx_taken, 1)

                def mask(u):
                    dve.wait_ge(scores_made, START + NU * g + u + 1)
                    dve.wait_ge(pT_made, START + NU * g + max(u - 1, 0))
                    for e in range(2):
                        ins = nc.vector.tensor_tensor(probs[:, u % 2, e, :, :],
                                                      bS[0:NT, u % 2, e, 0:GT].rearrange("p (n t) -> p n t", n=NH),
                                                      bc(future[:, :], NH, 1), ALU.add)
                    own_done(ins)
                    nc.vector.tensor_reduce(negmax[:, u % 2, :], probs[:, u % 2, :, :, :].rearrange("p e n t -> p (e n) t"),
                                            AX, ALU.max, negate=True).then_inc(masked, 1)

                def contexts(s):
                    dve.wait_ge(o_turned, START + GS * g + s + 1)
                    own_done(nc.vector.reciprocal(sums[:, s, :, :], sums[:, s, :, :]))
                    for n in range(NH):
                        ins = nc.vector.tensor_tensor(
                            outs[:, s, n, :, :],
                            bB[0:NT, :].rearrange("p (e n f) -> p n e f", e=NE, n=NH)[:, n, :, 0:HD],
                            bc(sums[:, s, :, n], HD, 2), ALU.mult)
                    own_done(ins)
                    nc.vector.tensor_tensor(outs[:, s, :, :, :], outs[:, s, :, :, :],
                                            bc(present[:, s, :].rearrange("p (n f) -> p n f", n=NH), NE, 2),
                                            ALU.mult).then_inc(outs_ready, 1)

                mask(0)
                for u in range(NU):
                    if u + 1 < NU:
                        mask(u + 1)
                    if u % 2 == 0 and u:
                        contexts(u // 2 - 1)
                contexts(GS - 1)
                dve.wait_ge(gate_made, START + g + 1)
                own_done(nc.vector.tensor_tensor(gate[:, :, :].rearrange("p (s n) e -> p s (n e)", s=GS),
                                                 bA[0:NT, 0:GS * 16].rearrange("p (s x) -> p s x", s=GS),
                                                 bc(bgate[:, :], GS, 1), ALU.add))
                own_done(nc.vector.tensor_reduce(fold[:, :], gate[:, :, :], AX, ALU.max))
                nc.vector.tensor_tensor(gate[:, :, :], gate[:, :, :], bc(fold[:, :], NE, 2), ALU.subtract).then_inc(gate_centered, 1)
                dve.wait_ge(gate_exp, START + g + 1)
                own_done(nc.vector.tensor_reduce(fold[:, :], gate[:, :, :], AX, ALU.add))
                own_done(nc.vector.reciprocal(fold[:, :], fold[:, :]))
                own_done(nc.vector.tensor_tensor(gate[:, :, :], gate[:, :, :], bc(fold[:, :], NE, 2), ALU.mult))
                flat = outs[:, :, :, :, :].rearrange("p s n e f -> p (s n e) f")
                own_done(nc.vector.tensor_tensor(flat, flat, bc(gate[:, :, :].rearrange("p x e -> p (x e)"), HD, 2), ALU.mult))
                own_done(nc.vector.tensor_reduce(heads(mixed[:, :, :]), outs[:, :, :, :, :].rearrange("p s n e f -> p (s n) f e"),
                                                 AX, ALU.add))
                own_done(nc.vector.tensor_tensor(mixed[:, :, :], mixed[:, :, :],
                                                 bc(resid[:, :, :].rearrange("p n f -> p (n f)"), GS, 1), ALU.add))

                def norm(n, to, ready):
                    centered, squared, summed, rooted = norm_sems[n]
                    own_done(nc.vector.tensor_reduce(fold[:, :], heads(mixed[:, :, :]), AX, ALU.add))
                    own_done(nc.vector.tensor_scalar(fold[:, :], fold[:, :], 1.0 / HD, None, ALU.mult))
                    nc.vector.tensor_tensor(heads(mixed[:, :, :]), heads(mixed[:, :, :]), bc(fold[:, :], HD, 2),
                                            ALU.subtract).then_inc(centered, 1)
                    dve.wait_ge(squared, START + g + 1)
                    nc.vector.tensor_reduce(var[:, :], heads(sq[:, :, :]), AX, ALU.add).then_inc(summed, 1)
                    dve.wait_ge(rooted, START + g + 1)
                    own_done(nc.vector.reciprocal(var[:, :], var[:, :]))
                    own_done(nc.vector.tensor_tensor(heads(mixed[:, :, :]), heads(mixed[:, :, :]), bc(var[:, :], HD, 2), ALU.mult))
                    own_done(nc.vector.tensor_tensor(heads(mixed[:, :, :]), heads(mixed[:, :, :]),
                                                     bc(affine[:, 2 * n, :], GS * NH, 1), ALU.mult))
                    nc.vector.tensor_tensor(heads(to), heads(mixed[:, :, :]), bc(affine[:, 2 * n + 1, :], GS * NH, 1),
                                            ALU.add).then_inc(ready, 1)

                norm(0, fx[:, :, :], f_ready)
                dve.wait_ge(fT_ready, START + g + 1)
                nc.vector.tensor_scalar(kept[:, :, :], fx[:, :, :], 0.0, None, ALU.not_equal)
                own_done(nc.vector.tensor_scalar(keptT[:, :], fT[0:D, :], 0.0, None, ALU.not_equal))
                dve.wait_ge(fc1_made, START + g + 1)
                nc.vector.scalar_tensor_tensor(out=hT[0:D, :], in0=bA[0:D, 0:GT], scalar=0.0, in1=keptT[:, :],
                                               op0=ALU.max, op1=ALU.mult).then_inc(h_ready, 1)
                dve.wait_ge(fc2_made, START + g + 1)
                own_done(nc.vector.tensor_tensor(mixed[:, :, :], bB[0:NT, 0:GS * D].rearrange("p (s f) -> p s f", s=GS),
                                                 kept[:, :, :], ALU.mult))
                own_done(nc.vector.tensor_tensor(mixed[:, :, :], mixed[:, :, :], fx[:, :, :], ALU.add))
                norm(1, fx[:, :, :], fout_ready)
                dve.wait_ge(hg_made, START + g + 1)
                own_done(nc.vector.tensor_copy(headgate[:, :, :], bB[0:NT, 0:GS * NH].rearrange("p (s n) -> p s n", s=GS)))
                own_done(nc.vector.tensor_reduce(headsum[:, :], headgate[:, :, :], AX, ALU.max))
                nc.vector.tensor_tensor(headgate[:, :, :], headgate[:, :, :], bc(headsum[:, :], NH, 2),
                                        ALU.subtract).then_inc(hg_centered, 1)
                dve.wait_ge(hg_exp, START + g + 1)
                own_done(nc.vector.tensor_reduce(headsum[:, :], headgate[:, :, :], AX, ALU.add))
                own_done(nc.vector.reciprocal(headsum[:, :], headsum[:, :]))
                own_done(nc.vector.tensor_tensor(headgate[:, :, :], headgate[:, :, :], bc(headsum[:, :], NH, 2), ALU.mult))
                own_done(nc.vector.tensor_tensor(heads(fx[:, :, :]), heads(fx[:, :, :]),
                                                 bc(headgate[:, :, :].rearrange("p s n -> p (s n)"), HD, 2), ALU.mult))
                hg = core.h[:, bass.ds(g * GS, GS), :]
                nc.vector.tensor_tensor(hg, hg, fx[:, :, :], ALU.add).then_inc(done, 1)
                assert own_done.n == OWN, own_done.n


def window_encoder(core, name):
    nc, aps = core.nc, core.aps
    K, NH, HD, NI = 10, 4, 16, 34
    NF = NT + K - 1
    ON_POOL = (8, 9)
    CHUNKS = ((0, 4), (4, 8), (8, 10))
    NC = len(CHUNKS)
    BANK = 512 // D
    first_pair = lambda q: q * (q + 1) // 2
    PAIRS = first_pair(K)
    with ExitStack() as ctx:
        sem = Semaphores(nc, ctx, name)
        sb = lambda n, shape: ctx.enter_context(nc.sbuf_tensor(f"{name}_{n}", shape, F32))
        frames = sb("frames", [NI, NB, NF])
        xw = sb("xw", [NI, NF])
        win = sb("win", [NI, K, D])
        wqkv, wqkv2 = sb("wqkv", [65, 3 * D]), sb("wqkv2", [65, 3 * D])
        wo, w1, w2 = sb("wo", [65, D]), sb("w1", [D, 2, 128]), sb("w2", [128, 2, D])
        b1, b2 = sb("b1", [128, 2]), sb("b2", [NT, D])
        affine = sb("affine", [D, 3, 2])
        h0, hb = sb("h0", [NT, K, D]), sb("hb", [NT, K, D])
        x1, x3, sq = sb("x1", [NT, K, D]), sb("x3", [NT, K, D]), sb("sq", [NT, K, D])
        mean, var = sb("mean", [NT, 3, K]), sb("var", [NT, 3, K])
        xT, oT, x2T, x3T = (sb(n, [65, K * NT]) for n in ("xT", "oT", "x2T", "x3T"))
        qkv = sb("qkv", [NT, K, 3 * D])
        kv2, q2 = sb("kv2", [NT, K, 2 * D]), sb("q2", [NT, D])
        prod = sb("prod", [NT, PAIRS * D])
        score, e = sb("score", [NT, K, NH, K]), sb("e", [NT, K, NH, K])
        maxima, sums = sb("maxima", [NT, K, NH]), sb("sums", [NT, K, NH])
        o = sb("o", [NT, K, D])
        prod2 = sb("prod2", [NT, K * D])
        score2, maxima2, sums2, o2 = sb("score2", [NT, NH, K]), sb("maxima2", [NT, NH]), sb("sums2", [NT, NH]), sb("o2", [NT, D])
        hidden = sb("hidden", [128, 2, 2, GT])
        ps = lambda n, shape: ctx.enter_context(nc.psum_tensor(f"{name}_{n}", shape, F32))
        bT, bQ, bH, bO = ps("bT", [128, 2, 512]), ps("bQ", [128, 2, 512]), ps("bH", [128, 2, 512]), ps("bO", [128, 2, 512])

        loaded, set_up = sem("loaded"), sem("set_up")
        xw_ready, h0_made, h0_ready, x1_ready, x1_turned, x1_taken, qkv_made, qkv_taken = (
            sem(n) for n in ("xw_ready", "h0_made", "h0_ready", "x1_ready", "x1_turned", "x1_taken", "qkv_made",
                             "qkv_taken"))
        pool_scores, centered, exp_done, pool_values, o_ready, o_turned, o_taken, wo_made, wo_taken = (
            sem(n) for n in ("pool_scores", "centered", "exp_done", "pool_values", "o_ready", "o_turned", "o_taken",
                             "wo_made", "wo_taken"))
        x2_ready, x2_turned, x2_taken, b2_added = (
            sem(n) for n in ("x2_ready", "x2_turned", "x2_taken", "b2_added"))
        hidden_made, hidden_ready, w2_made, w2_taken, x3_ready, x3_turned, x3_taken = (
            sem(n) for n in ("hidden_made", "hidden_ready", "w2_made", "w2_taken", "x3_ready", "x3_turned", "x3_taken"))
        kv_made, kv_taken, centered2, exp2_done = (
            sem(n) for n in ("kv_made", "kv_taken", "centered2", "exp2_done"))
        front_own, back_own = sem("front_own"), sem("back_own")
        norm_sems = [[sem(f"{w}{n}") for w in ("norm_centered", "norm_squared", "norm_summed", "norm_rooted")]
                     for n in range(3)]
        x2_centered = norm_sems[1][0]
        sem.start()
        block = ctx.enter_context(nc.Block())
        NLOAD = 10
        OWN_FRONT, OWN_BACK = 12, 10
        units = lambda c: range(*CHUNKS[c])
        cols = lambda c: slice(CHUNKS[c][0] * NT, CHUNKS[c][1] * NT)
        of = lambda k: slice(k * NT, (k + 1) * NT)
        wide_of = lambda c: (CHUNKS[c][1] - CHUNKS[c][0]) * NT
        at = lambda k: bO[0:NT, k // BANK, k % BANK * D:(k % BANK + 1) * D]

        def query_products(eng, q):
            to = prod[:, first_pair(q) * D:first_pair(q + 1) * D].rearrange("p (k f) -> p k f", f=D)
            return eng.tensor_tensor(to, qkv[:, 0:q + 1, D:2 * D], bc(qkv[:, q, 0:D], q + 1, 1), ALU.mult)

        def value_products(eng, q):
            to = prod[:, first_pair(q) * D:first_pair(q + 1) * D].rearrange("p (h f k) -> p h f k", h=NH, f=HD)
            return eng.tensor_tensor(to, qkv[:, 0:q + 1, 2 * D:3 * D].rearrange("p k (h f) -> p h f k", h=NH),
                                     bc(e[:, q, :, 0:q + 1], HD, 2), ALU.mult)

        def sequence(t, b):
            return t[:, b, :] if isinstance(b, int) else t[:, bass.ds(b, 1), :].rearrange("p o f -> p (o f)")

        @block.sync
        def _(sp):
            for to, what in ((frames, "frames"), (win, "win"), (wqkv, "wqkv"), (wqkv2, "wqkv2"), (wo, "wo"), (w1, "w1"),
                             (w2, "w2"), (b1, "b1"), (affine, "affine")):
                sp.dma_start(to[:], aps[f"{name}_{what}"]).then_inc(loaded, 16)
            sp.dma_start(b2[:, :], aps[f"{name}_b2"].partition_broadcast(NT)).then_inc(loaded, 16)

        @block.gpsimd
        def _(pool):
            for n, (to, value) in enumerate(((xT[D:D + 1, :], 1.0), (oT[D:D + 1, :], 1.0), (x3T[D:D + 1, :], 1.0),
                                             (score[:, :, :, :], -3.0e38))):
                nc.gpsimd.memset(to, value).then_inc(set_up, 1)
                pool.wait_ge(set_up, START + n + 1)
            pool.wait_ge(loaded, 16 * NLOAD)
            with pool.Fori(0, NB) as f:
                pool.wait_ge(h0_made, START + f)
                nc.gpsimd.tensor_copy(xw[:, :], frames[:, bass.ds(f, 1), :].rearrange("p o t -> p (o t)")).then_inc(xw_ready, 1)
                pool.wait_ge(qkv_taken, START + 5 * f + 5)
                for q in ON_POOL:
                    ins = query_products(nc.gpsimd, q)
                ins.then_inc(pool_scores, 1)
                pool.wait_ge(exp_done, START + f + 1)
                for q in ON_POOL:
                    ins = value_products(nc.gpsimd, q)
                ins.then_inc(pool_values, 1)
                pool.wait_ge(x2_centered, START + f + 1)
                nc.gpsimd.tensor_tensor(hb[:, :, :], hb[:, :, :], bc(b2[:, :], K, 1), ALU.add).then_inc(b2_added, 1)

        @block.tensor
        def _(pe):
            pe.wait_ge(loaded, 16 * NLOAD)
            pe.wait_ge(set_up, START + 4)

            def turn(src, c, signal):
                for k in units(c):
                    wide = src[:, k:k + 2, :].rearrange("p s f -> p (s f)") if k == CHUNKS[c][0] else src[:, k, :]
                    j = k - CHUNKS[c][0]
                    mm = nc.tensor.transpose(bT[0:wide.shape[1], c % 2, of(j)], wide, core.ident[0:NT, 0:NT])
                mm.then_inc(signal, 1)

            def embed_and_project(f):
                pe.wait_ge(xw_ready, START + f + 1)
                pe.wait_ge(wo_taken, START + f)
                for k in range(K):
                    mm = nc.tensor.matmul(at(k), xw[:, k:k + NT], win[:, k, :], start=True, stop=True)
                mm.then_inc(h0_made, 1)
                pe.wait_ge(x1_ready, START + f + 1)
                pe.wait_ge(x2_taken, START + NC * f)
                for c in range(NC):
                    if c == 2:
                        pe.wait_ge(x1_taken, START + NC * f + 1)
                    turn(x1, c, x1_turned)
                for j in range(K // 2):
                    pe.wait_ge(x1_taken, START + NC * f + 2 * j // 4 + 1)
                    if j >= 2:
                        pe.wait_ge(qkv_taken, START + 5 * f + j - 1)
                    for u in range(2):
                        mm = nc.tensor.matmul(bQ[0:NT, j % 2, u * 3 * D:(u + 1) * 3 * D], xT[:, of(2 * j + u)], wqkv[:, :],
                                              start=True, stop=True)
                    mm.then_inc(qkv_made, 1)

            def context_out(f):
                pe.wait_ge(o_ready, START + f + 1)
                for c in range(NC):
                    if c == 2:
                        pe.wait_ge(o_taken, START + NC * f + 1)
                    turn(o, c, o_turned)
                pe.wait_ge(w2_taken, START + f)
                for c in range(NC):
                    pe.wait_ge(o_taken, START + NC * f + c + 1)
                    for k in units(c):
                        mm = nc.tensor.matmul(at(k), oT[:, of(k)], wo[:, :], start=True, stop=True)
                mm.then_inc(wo_made, 1)

            def turn_x2(f):
                pe.wait_ge(x2_ready, START + f + 1)
                for c in range(NC):
                    if c == 2:
                        pe.wait_ge(x2_taken, START + NC * f + 1)
                    turn(x1, c, x2_turned)

            def mlp(b):
                def first(c):
                    pe.wait_ge(x2_taken, START + NC * b + c + 1)
                    for m in range(2):
                        if c:
                            pe.wait_ge(hidden_ready, START + 2 * NC * b + 2 * (c - 1) + m + 1)
                        nc.tensor.matmul(bH[:, m, 0:wide_of(c)], w1[:, m, :], x2T[0:D, cols(c)],
                                         start=True, stop=True).then_inc(hidden_made, 1)

                def second(c):
                    pe.wait_ge(hidden_ready, START + 2 * NC * b + 2 * c + 2)
                    for j, k in enumerate(units(c)):
                        for m in range(2):
                            mm = nc.tensor.matmul(at(k), hidden[:, c % 2, m, of(j)], w2[:, m, :],
                                                  start=(m == 0), stop=(m == 1))
                    mm.then_inc(w2_made, 1)

                first(0)
                for c in range(NC):
                    if c + 1 < NC:
                        first(c + 1)
                    second(c)

            def project_again(b):
                pe.wait_ge(x3_ready, START + b + 1)
                for c in range(NC):
                    if c == 2:
                        pe.wait_ge(x3_taken, START + NC * b + 1)
                    turn(x3, c, x3_turned)
                for c in range(NC):
                    pe.wait_ge(x3_taken, START + NC * b + c + 1)
                    if c == 2:
                        pe.wait_ge(kv_taken, START + NC * b + 1)
                    for j, k in enumerate(units(c)):
                        mm = nc.tensor.matmul(bQ[0:NT, c % 2, j * 2 * D:(j + 1) * 2 * D], x3T[:, of(k)], wqkv2[:, D:3 * D],
                                              start=True, stop=True)
                    if c == 2:
                        mm = nc.tensor.matmul(bQ[0:NT, 0, 4 * D:5 * D], x3T[:, of(K - 1)], wqkv2[:, 0:D],
                                              start=True, stop=True)
                    mm.then_inc(kv_made, 1)

            embed_and_project(0)
            context_out(0)
            turn_x2(0)
            with pe.Fori(1, NB) as f:
                embed_and_project(f)
                mlp(f - 1)
                context_out(f)
                project_again(f - 1)
                turn_x2(f)
            mlp(NB - 1)
            project_again(NB - 1)

        @block.scalar
        def _(act):
            act.wait_ge(loaded, 16 * NLOAD)
            act.wait_ge(set_up, START + 4)

            def squares(n, x, i):
                was_centered, was_squared, _, _ = norm_sems[n]
                act.wait_ge(was_centered, START + i + 1)
                nc.scalar.activation(sq[:, :, :], x[:, :, :], ACT.Square).then_inc(was_squared, 1)

            def roots(n, i):
                _, _, was_summed, was_rooted = norm_sems[n]
                act.wait_ge(was_summed, START + i + 1)
                nc.scalar.activation(var[:, n, :], var[:, n, :], ACT.Sqrt, bias=core.eps[0:NT, 0:1],
                                     scale=1.0 / D).then_inc(was_rooted, 1)

            def take_turned(to, turned, taken, i, norm=None):
                for c in range(NC):
                    act.wait_ge(turned, START + NC * i + c + 1)
                    src = bT[0:D, c % 2, 0:wide_of(c)]
                    if norm is None:
                        ins = nc.scalar.copy(to[0:D, cols(c)], src)
                    else:
                        ins = nc.scalar.activation(to[0:D, cols(c)], src, ACT.Identity, bias=affine[:, norm, 1:2],
                                                   scale=affine[:, norm, 0:1])
                    ins.then_inc(taken, 1)

            def embedded(f):
                act.wait_ge(h0_made, START + f + 1)
                for b, (n0, n1) in enumerate(((0, BANK), (BANK, K))):
                    ins = nc.scalar.copy(h0[:, n0:n1, :].rearrange("p k f -> p (k f)"), bO[0:NT, b, 0:(n1 - n0) * D])
                ins.then_inc(h0_ready, 1)
                squares(0, x1, f)
                roots(0, f)
                take_turned(xT, x1_turned, x1_taken, f, 0)
                for j in range(K // 2):
                    act.wait_ge(qkv_made, START + 5 * f + j + 1)
                    nc.scalar.copy(qkv[:, 2 * j:2 * j + 2, :].rearrange("p k f -> p (k f)"),
                                   bQ[0:NT, j % 2, 0:6 * D]).then_inc(qkv_taken, 1)

            def exponentials(f):
                act.wait_ge(centered, START + f + 1)
                nc.scalar.activation(e[:, :, :, :], e[:, :, :, :], ACT.Exp, scale=float(HD) ** -0.5).then_inc(exp_done, 1)

            def gelu(b, c):
                for m in range(2):
                    act.wait_ge(hidden_made, START + 2 * NC * b + 2 * c + m + 1)
                    if m == 0 and c == 0:
                        act.wait_ge(w2_made, START + NC * b)
                    if m == 0 and c == 2:
                        act.wait_ge(w2_made, START + NC * b + 1)
                    nc.scalar.activation(hidden[:, c % 2, m, 0:wide_of(c)], bH[:, m, 0:wide_of(c)], ACT.Gelu,
                                         bias=b1[:, m:m + 1]).then_inc(hidden_ready, 1)

            def keys_again(b):
                for c in range(NC):
                    act.wait_ge(kv_made, START + NC * b + c + 1)
                    n = len(units(c))
                    if c == 2:
                        nc.scalar.copy(q2[:, :], bQ[0:NT, 0, 4 * D:5 * D])
                    nc.scalar.copy(kv2[:, CHUNKS[c][0]:CHUNKS[c][1], :].rearrange("p k f -> p (k f)"),
                                   bQ[0:NT, c % 2, 0:n * 2 * D]).then_inc(kv_taken, 1)

            def exponentials_again(b):
                act.wait_ge(centered2, START + b + 1)
                nc.scalar.activation(score2[:, :, :], score2[:, :, :], ACT.Exp, scale=float(HD) ** -0.5).then_inc(exp2_done, 1)

            embedded(0)
            exponentials(0)
            take_turned(oT, o_turned, o_taken, 0)
            squares(1, x1, 0)
            roots(1, 0)
            take_turned(x2T, x2_turned, x2_taken, 0, 1)
            with act.Fori(1, NB) as f:
                embedded(f)
                gelu(f - 1, 0)
                exponentials(f)
                gelu(f - 1, 1)
                gelu(f - 1, 2)
                take_turned(oT, o_turned, o_taken, f)
                squares(2, x3, f - 1)
                roots(2, f - 1)
                take_turned(x3T, x3_turned, x3_taken, f - 1, 2)
                squares(1, x1, f)
                roots(1, f)
                keys_again(f - 1)
                take_turned(x2T, x2_turned, x2_taken, f, 1)
                exponentials_again(f - 1)
            for c in range(NC):
                gelu(NB - 1, c)
            squares(2, x3, NB - 1)
            roots(2, NB - 1)
            take_turned(x3T, x3_turned, x3_taken, NB - 1, 2)
            keys_again(NB - 1)
            exponentials_again(NB - 1)

        @block.vector
        def _(dve):
            def norm(n, own_done, src, to, i, ready):
                was_centered, was_squared, was_summed, was_rooted = norm_sems[n]
                own_done(nc.vector.tensor_reduce(mean[:, n, :], src[:, :, :], AX, ALU.add))
                own_done(nc.vector.tensor_scalar(mean[:, n, :], mean[:, n, :], 1.0 / D, None, ALU.mult))
                nc.vector.tensor_tensor(to[:, :, :], src[:, :, :], bc(mean[:, n, :], D, 2), ALU.subtract).then_inc(
                    was_centered, 1)
                dve.wait_ge(was_squared, START + i + 1)
                nc.vector.tensor_reduce(var[:, n, :], sq[:, :, :], AX, ALU.add).then_inc(was_summed, 1)
                dve.wait_ge(was_rooted, START + i + 1)
                own_done(nc.vector.reciprocal(var[:, n, :], var[:, n, :]))
                nc.vector.tensor_tensor(to[:, :, :], to[:, :, :], bc(var[:, n, :], D, 2), ALU.mult).then_inc(ready, 1)

            def add_banks(own_done, to, src, taken):
                for b, (n0, n1) in enumerate(((0, BANK), (BANK, K))):
                    flat = lambda t: t[:, n0:n1, :].rearrange("p k f -> p (k f)")
                    ins = nc.vector.tensor_tensor(flat(to), flat(src), bO[0:NT, b, 0:(n1 - n0) * D], ALU.add)
                ins.then_inc(taken, 1)

            def attention(f, own_done):
                dve.wait_ge(h0_ready, START + f + 1)
                dve.wait_ge(x2_turned, START + NC * f)
                norm(0, own_done, h0, x1, f, x1_ready)
                dve.wait_ge(qkv_taken, START + 5 * f + 5)
                for q in range(K):
                    if q not in ON_POOL:
                        ins = query_products(nc.vector, q)
                own_done(ins)
                dve.wait_ge(pool_scores, START + f + 1)
                for q in range(K):
                    ins = nc.vector.tensor_reduce(
                        score[:, q, :, 0:q + 1].rearrange("p h k -> p k h"),
                        prod[:, first_pair(q) * D:first_pair(q + 1) * D].rearrange("p (k h f) -> p k h f", h=NH, f=HD),
                        AX, ALU.add)
                own_done(ins)
                own_done(nc.vector.tensor_reduce(maxima[:, :, :], score[:, :, :, :], AX, ALU.max))
                nc.vector.tensor_tensor(e[:, :, :, :], score[:, :, :, :], bc(maxima[:, :, :], K, 3), ALU.subtract).then_inc(
                    centered, 1)
                dve.wait_ge(exp_done, START + f + 1)
                for q in range(K):
                    if q not in ON_POOL:
                        value_products(nc.vector, q)
                own_done(nc.vector.tensor_reduce(sums[:, :, :], e[:, :, :, :], AX, ALU.add))
                own_done(nc.vector.reciprocal(sums[:, :, :], sums[:, :, :]))
                dve.wait_ge(pool_values, START + f + 1)
                dve.wait_ge(o_turned, START + NC * f)
                for q in range(K):
                    ins = nc.vector.tensor_reduce(
                        o[:, q, :],
                        prod[:, first_pair(q) * D:first_pair(q + 1) * D].rearrange("p (f k) -> p f k", f=D),
                        AX, ALU.add)
                own_done(ins)
                heads = o[:, :, :].rearrange("p k (h f) -> p (k h) f", h=NH)
                nc.vector.tensor_tensor(heads, heads, bc(sums[:, :, :].rearrange("p k h -> p (k h)"), HD, 2),
                                        ALU.mult).then_inc(o_ready, 1)

            def residual_and_norm(f, own_done):
                dve.wait_ge(wo_made, START + f + 1)
                add_banks(own_done, hb, h0, wo_taken)
                dve.wait_ge(wo_taken, START + f + 1)
                norm(1, own_done, hb, x1, f, x2_ready)

            def mlp_residual(b, own_done):
                dve.wait_ge(w2_made, START + NC * b + NC)
                dve.wait_ge(b2_added, START + b + 1)
                own_done(nc.vector.tensor_tensor(sequence(core.h, b), hb[:, K - 1, :], at(K - 1), ALU.add))
                add_banks(own_done, hb, hb, w2_taken)
                dve.wait_ge(w2_taken, START + b + 1)
                norm(2, own_done, hb, x3, b, x3_ready)

            def last_attention(b, own_done):
                dve.wait_ge(kv_taken, START + NC * b + NC)
                keyed = prod2[:, :].rearrange("p (k f) -> p k f", f=D)
                own_done(nc.vector.tensor_tensor(keyed, kv2[:, :, 0:D], bc(q2[:, :], K, 1), ALU.mult))
                own_done(nc.vector.tensor_reduce(score2[:, :, :].rearrange("p h k -> p k h"),
                                                 prod2[:, :].rearrange("p (k h f) -> p k h f", h=NH, f=HD), AX, ALU.add))
                own_done(nc.vector.tensor_reduce(maxima2[:, :], score2[:, :, :], AX, ALU.max))
                nc.vector.tensor_tensor(score2[:, :, :], score2[:, :, :], bc(maxima2[:, :], K, 2),
                                        ALU.subtract).then_inc(centered2, 1)
                dve.wait_ge(exp2_done, START + b + 1)
                nc.vector.tensor_tensor(prod2[:, :].rearrange("p (h f k) -> p h f k", h=NH, f=HD),
                                        kv2[:, :, D:2 * D].rearrange("p k (h f) -> p h f k", h=NH),
                                        bc(score2[:, :, :], HD, 2), ALU.mult)
                own_done(nc.vector.tensor_reduce(sums2[:, :], score2[:, :, :], AX, ALU.add))
                own_done(nc.vector.reciprocal(sums2[:, :], sums2[:, :]))
                own_done(nc.vector.tensor_reduce(o2[:, :], prod2[:, :].rearrange("p (f k) -> p f k", f=D), AX, ALU.add))
                nc.vector.tensor_tensor(sequence(core.xn, b).rearrange("p (h f) -> p h f", h=NH),
                                        o2[:, :].rearrange("p (h f) -> p h f", h=NH), bc(sums2[:, :], HD, 2), ALU.mult)

            dve.wait_ge(loaded, 16 * NLOAD)
            dve.wait_ge(set_up, START + 4)
            own_front = InOrder(dve, front_own)
            attention(0, own_front)
            residual_and_norm(0, own_front)
            assert own_front.n == OWN_FRONT, own_front.n
            with dve.Fori(1, NB) as f:
                own_front = InOrder(dve, front_own, f * OWN_FRONT)
                own_back = InOrder(dve, back_own, (f - 1) * OWN_BACK)
                attention(f, own_front)
                mlp_residual(f - 1, own_back)
                residual_and_norm(f, own_front)
                last_attention(f - 1, own_back)
                assert (own_front.n, own_back.n) == (OWN_FRONT, OWN_BACK), (own_front.n, own_back.n)
            own_back = InOrder(dve, back_own, (NB - 1) * OWN_BACK)
            mlp_residual(NB - 1, own_back)
            last_attention(NB - 1, own_back)


def last_slot(core, name):
    nc, aps = core.nc, core.aps
    with ExitStack() as ctx:
        sem = Semaphores(nc, ctx, name)
        sb = lambda n, shape: ctx.enter_context(nc.sbuf_tensor(f"{name}_{n}", shape, F32))
        wo, w1, w2, wout = sb("wo", [65, D]), sb("w1", [D, 2, 128]), sb("w2", [128, 2, D]), sb("wout", [65, D])
        b1, b2, affine = sb("b1", [128, 2]), sb("b2", [NT, D]), sb("affine", [D, 2])
        xg, hs, x, sq = (sb(n, [NT, GS, D]) for n in ("xg", "hs", "x", "sq"))
        mean, var, carrier = sb("mean", [NT, GS]), sb("var", [NT, GS]), sb("carrier", [1, 1])
        xT, x2T = sb("xT", [65, GT]), sb("x2T", [D, GT])
        hidden = sb("hidden", [128, 2, GT])
        ps = lambda n, shape: ctx.enter_context(nc.psum_tensor(f"{name}_{n}", shape, F32))
        bA, bB, bH = ps("bA", [128, 512]), ps("bB", [128, 512]), ps("bH", [128, 2, 512])
        loaded, set_up, own = sem("loaded"), sem("set_up"), sem("own")
        (xg_ready, o_turned, o_taken, wo_made, centered, squared, summed, rooted, x_ready, x_turned, x_taken) = (
            sem(n) for n in ("xg_ready", "o_turned", "o_taken", "wo_made", "centered", "squared", "summed", "rooted",
                             "x_ready", "x_turned", "x_taken"))
        hidden_made, hidden_ready, w2_made, h_ready, h_turned, h_taken, z_made, z_taken = (
            sem(n) for n in ("hidden_made", "hidden_ready", "w2_made", "h_ready", "h_turned", "h_taken", "z_made",
                             "z_taken"))
        sem.start()
        block = ctx.enter_context(nc.Block())
        NLOAD = 7
        OWN = 5
        of = lambda s: slice(s * NT, (s + 1) * NT)

        @block.sync
        def _(sp):
            for to, what in ((wo, "wo"), (w1, "w1"), (w2, "w2"), (wout, "wout"), (b1, "b1"), (affine, "affine")):
                sp.dma_start(to[:], aps[f"{name}_{what}"]).then_inc(loaded, 16)
            sp.dma_start(b2[:, :], aps[f"{name}_b2"].partition_broadcast(NT)).then_inc(loaded, 16)

        @block.gpsimd
        def _(pool):
            nc.gpsimd.memset(xT[D:D + 1, :], 1.0).then_inc(set_up, 1)
            pool.wait_ge(set_up, START + 1)
            with pool.Fori(0, NG) as g:
                pool.wait_ge(o_turned, START + g)
                nc.gpsimd.tensor_copy(xg[:, :, :], core.xn[:, bass.ds(g * GS, GS), :]).then_inc(xg_ready, 1)

        @block.tensor
        def _(pe):
            pe.wait_ge(loaded, 16 * NLOAD)
            pe.wait_ge(set_up, START + 1)
            with pe.Fori(0, NG) as g:
                pe.wait_ge(xg_ready, START + g + 1)
                transpose_each(core, bA, xg, D).then_inc(o_turned, 1)
                pe.wait_ge(o_taken, START + g + 1)
                pe.wait_ge(z_taken, START + g)
                for s in range(GS):
                    mm = nc.tensor.matmul(bB[0:NT, s * D:(s + 1) * D], xT[:, of(s)], wo[:, :], start=True, stop=True)
                mm.then_inc(wo_made, 1)
                pe.wait_ge(x_ready, START + g + 1)
                transpose_each(core, bA, x, D).then_inc(x_turned, 1)
                pe.wait_ge(x_taken, START + g + 1)
                for m in range(2):
                    nc.tensor.matmul(bH[:, m, 0:GT], w1[:, m, :], x2T[:, :], start=True, stop=True).then_inc(hidden_made, 1)
                pe.wait_ge(hidden_ready, START + 2 * g + 2)
                for s in range(GS):
                    for m in range(2):
                        mm = nc.tensor.matmul(bB[0:NT, s * D:(s + 1) * D], hidden[:, m, of(s)], w2[:, m, :],
                                              start=(m == 0), stop=(m == 1))
                mm.then_inc(w2_made, 1)
                pe.wait_ge(h_ready, START + g + 1)
                transpose_each(core, bA, x, D).then_inc(h_turned, 1)
                pe.wait_ge(h_taken, START + g + 1)
                for s in range(GS):
                    mm = nc.tensor.matmul(bB[0:NT, s * D:(s + 1) * D], xT[:, of(s)], wout[:, :], start=True, stop=True)
                mm.then_inc(z_made, 1)

        @block.scalar
        def _(act):
            act.wait_ge(loaded, 16 * NLOAD)
            act.wait_ge(set_up, START + 1)
            with act.Fori(0, NG) as g:
                act.wait_ge(o_turned, START + g + 1)
                nc.scalar.copy(xT[0:D, :], bA[0:D, 0:GT]).then_inc(o_taken, 1)
                act.wait_ge(centered, START + g + 1)
                nc.scalar.activation(sq[:, :, :], x[:, :, :], ACT.Square).then_inc(squared, 1)
                act.wait_ge(summed, START + g + 1)
                nc.scalar.activation(var[:, :], var[:, :], ACT.Sqrt, bias=core.eps[0:NT, 0:1], scale=1.0 / D).then_inc(rooted, 1)
                act.wait_ge(x_turned, START + g + 1)
                nc.scalar.activation(x2T[:, :], bA[0:D, 0:GT], ACT.Identity, bias=affine[:, 1:2],
                                     scale=affine[:, 0:1]).then_inc(x_taken, 1)
                for m in range(2):
                    act.wait_ge(hidden_made, START + 2 * g + m + 1)
                    nc.scalar.activation(hidden[:, m, :], bH[:, m, 0:GT], ACT.Gelu, bias=b1[:, m:m + 1]).then_inc(hidden_ready, 1)
                act.wait_ge(h_turned, START + g + 1)
                nc.scalar.copy(xT[0:D, :], bA[0:D, 0:GT]).then_inc(h_taken, 1)

        @block.vector
        def _(dve):
            dve.wait_ge(loaded, 16 * NLOAD)
            with dve.Fori(0, NG) as g:
                own_done = InOrder(dve, own, g * OWN)
                hg = core.h[:, bass.ds(g * GS, GS), :]
                made = bB[0:NT, 0:GS * D].rearrange("p (s f) -> p s f", s=GS)
                dve.wait_ge(wo_made, START + g + 1)
                own_done(nc.vector.tensor_tensor(hs[:, :, :], hg, made, ALU.add))
                own_done(nc.vector.tensor_reduce(mean[:, :], hs[:, :, :], AX, ALU.add))
                own_done(nc.vector.tensor_scalar(mean[:, :], mean[:, :], 1.0 / D, None, ALU.mult))
                nc.vector.tensor_tensor(x[:, :, :], hs[:, :, :], bc(mean[:, :], D, 2), ALU.subtract).then_inc(centered, 1)
                own_done(nc.vector.tensor_tensor(hs[:, :, :], hs[:, :, :], bc(b2[:, :], GS, 1), ALU.add))
                dve.wait_ge(squared, START + g + 1)
                nc.vector.tensor_reduce(var[:, :], sq[:, :, :], AX, ALU.add).then_inc(summed, 1)
                dve.wait_ge(rooted, START + g + 1)
                own_done(nc.vector.reciprocal(var[:, :], var[:, :]))
                nc.vector.tensor_tensor(x[:, :, :], x[:, :, :], bc(var[:, :], D, 2), ALU.mult).then_inc(x_ready, 1)
                dve.wait_ge(w2_made, START + g + 1)
                nc.vector.tensor_tensor(x[:, :, :], hs[:, :, :], made, ALU.add).then_inc(h_ready, 1)
                dve.wait_ge(z_made, START + g + 1)
                nc.vector.memset(carrier[:, :], 0.0)
                nc.vector.tensor_copy(hg, made).then_inc(z_taken, 1)
                assert own_done.n == OWN, own_done.n


def program(nc, aps, out):
    with ExitStack() as ctx:
        core = Core(nc, ctx, aps)
        constants(core)
        window_encoder(core, "L0t")
        last_slot(core, "L0z")
        layer_norm(core, "L0a_ln")
        window_attention(core, "L0a", True)
        layer_norm(core, "L0f_ln")
        experts(core, "L0f", 16, 128, True)
        add_normed(core, "L0f")
        layer_norm(core, "L1a_ln")
        window_attention(core, "L1a", False)
        layer_norm(core, "L1f_ln")
        experts(core, "L1f", 64, 128, False)
        layer_norm(core, "L2a_ln")
        phase_attention(core, "L2a")
        layer_norm(core, "L2f_ln")
        expert_heads(core, "L2f")
        layer_norm(core, "L3a_ln")
        lattice_attention(core, "L3a")
        layer_norm(core, "L3f_ln")
        tree_experts(core, "L3f")
        sem = Semaphores(nc, ctx, "out")
        stored = sem("stored")
        sem.start()
        block = ctx.enter_context(nc.Block())

        @block.sync
        def _(sp):
            sp.dma_start(out.rearrange("b t d -> t b d"), core.h[:, :, :]).then_inc(stored, 16)
            sp.wait_ge(stored, 16)


def laid_out(inputs):
    a = {k: np.asarray(v) for k, v in inputs.items()}
    out = {}
    f = np.float32
    tok = np.arange(NT)
    out["headmask8"] = (np.arange(D)[:, None] // 8 == np.arange(8)[None, :]).astype(f)
    out["onehot7"] = np.tile((tok[None, :] % 7 == np.arange(7)[:, None]).astype(f), (1, GS))
    rel = (tok[None, :] - tok[:, None]).astype(f)
    out["posrel"] = np.stack([rel, np.zeros_like(rel), rel * rel], axis=1)

    def under(w, b):
        return np.concatenate([w, b[None, :]], axis=0)

    t = {k: a[f"L0_tok_{k}"] for k in ("w_in", "b_in", "wqkv", "bqkv", "wo", "bo", "w1", "b1", "w2", "b2", "ln1_g",
                                       "ln1_b", "ln2_g", "ln2_b", "w_out", "b_out")}
    K = 10
    frames = np.ones((34, NB, NT + K - 1), f)
    frames[:32, :, :K - 1] = 0
    frames[:32, :, K - 1:] = a["x"][:, :NT].transpose(2, 0, 1)
    out["L0t_frames"] = frames
    angle = np.arange(K)[:, None] * np.exp(np.arange(0, D, 2) * (-math.log(10000.0) / D))
    slots_pe = np.stack([np.sin(angle), np.cos(angle)], axis=-1).reshape(K, D).astype(f)
    out["L0t_win"] = np.concatenate([np.broadcast_to(under(t["w_in"], t["b_in"])[:, None, :], (33, K, D)), slots_pe[None]])
    affine = lambda *names: np.stack([np.stack([t[f"{n}_g"][l], t[f"{n}_b"][l]], axis=-1) for n, l in names], axis=1)
    out["L0t_wqkv"], out["L0t_wqkv2"] = (under(t["wqkv"][l], t["bqkv"][l]) for l in range(2))
    out["L0t_affine"] = affine(("ln1", 0), ("ln2", 0), ("ln1", 1))
    out["L0z_affine"] = affine(("ln2", 1))[:, 0]
    out["L0z_wout"] = under(t["w_out"], t["b_out"])
    for l, name in enumerate(("L0t", "L0z")):
        out[f"{name}_wo"] = under(t["wo"][l], t["bo"][l])
        out[f"{name}_w1"] = t["w1"][l].reshape(D, 2, 128)
        out[f"{name}_b1"] = t["b1"][l].reshape(2, 128).T
        out[f"{name}_w2"] = t["w2"][l].reshape(2, 128, D).transpose(1, 0, 2)
        out[f"{name}_b2"] = t["b2"][l]
    out["L0a_wqkv"] = under(a["L0_attn_qkv_w"].T, a["L0_attn_qkv_b"])
    out["L0a_wproj"] = under(a["L0_attn_proj_w"].T, a["L0_attn_proj_b"])
    bias = a["L0_attn_bias_table"][np.arange(7)[:, None] - (tok % 7)[None, :] + 6]
    out["L0a_bias7"] = np.repeat(bias[:, None, :], 8, axis=1)
    out["L1a_wqkv"] = under(np.concatenate([a["L1_attn_Wqk"], a["L1_attn_Wv"]], axis=0).T, np.zeros(3 * D, f))
    out["L1a_wproj"] = under(a["L1_attn_Wproj"].T, a["L1_attn_bproj"])
    out["L1a_wpos"] = a["L1_attn_Wpos"].T
    out["L1a_bpos"] = a["L1_attn_bpos"]
    out["L1a_gating"] = a["L1_attn_gating"]

    def mixture(name, wr, br, w1, b1, w2, b2):
        E, _, F = w1.shape
        out[f"{name}_wr"], out[f"{name}_br"], out[f"{name}_b2"] = wr, br, b2
        out[f"{name}_w1"] = w1.reshape(E // 2, 2 * D, F)
        out[f"{name}_b1"] = b1.reshape(E // 2, 2, F).transpose(0, 2, 1)
        out[f"{name}_w2"] = w2.reshape(E // 2, 2, F, D).transpose(0, 2, 1, 3).reshape(E // 2, F, 2 * D)
        out[f"iota{E}"] = np.arange(E, dtype=f)

    mixture("L0f", *(a[f"L0_ffn_{k}"] for k in ("gate_w", "gate_b", "w1", "b1", "w2", "b2")))
    mixture("L1f", *(a[f"L1_ffn_{k}"] for k in ("Wr", "br", "W1", "b1", "W2", "b2")))
    out["L0f_affine"] = np.stack([a["L0_ffn_gamma"], a["L0_ffn_beta"]])
    out["L3a_wqkv"] = under(np.concatenate([a[f"L3_attn_W{k}"] for k in "qkv"], axis=1),
                            np.concatenate([a[f"L3_attn_b{k}"] for k in "qkv"]))
    out["L3a_wo"], out["L3a_bo"] = a["L3_attn_Wo"], a["L3_attn_bo"][None, :]
    def slots(w):
        return np.concatenate([np.zeros_like(w[:1]), w], axis=0)

    out["L3f_w1"] = under(slots(a["L3_ffn_w1s"]).T, slots(a["L3_ffn_b1s"]))
    out["L3f_w2"] = slots(a["L3_ffn_w2s"]).reshape(16, 2, 8, D, D).transpose(1, 3, 0, 2, 4).reshape(2 * D, 16, 8 * D)
    out["L3f_b2"] = slots(a["L3_ffn_b2s"])
    p = {k: a[f"L2_attn_{k}"] for k in ("Wk1", "bk1", "Wk2", "bk2", "Wq1", "bq1", "Wq2", "bq2", "Wvc", "bvc", "Wvp",
                                        "bvp", "Wg1", "bg1", "Wg2", "bg2", "ln_g", "ln_b", "Wo", "bo")}
    side = lambda *w: np.concatenate(w, axis=-1)
    out["L2a_wkq1"] = under(side(p["Wk1"], p["Wq1"]), side(p["bk1"], p["bq1"]))
    out["L2a_wv"] = under(side(p["Wvc"], p["Wvp"]), side(p["bvc"], p["bvp"]))
    out["L2a_wg1"], out["L2a_wg2"] = under(p["Wg1"], p["bg1"]), under(p["Wg2"], p["bg2"])
    out["L2a_wo"] = under(p["Wo"], p["bo"])
    k2, q2 = side(p["Wk2"], p["Wk2"]), side(p["Wq2"], p["Wq2"])
    out["L2a_w2"] = np.stack([np.concatenate([k2, np.zeros_like(k2)]), np.concatenate([np.zeros_like(q2), q2])], axis=1)
    out["L2a_b2"] = np.stack([side(p["bk2"], p["bk2"]), side(p["bq2"], p["bq2"])], axis=1)
    out["L2a_affine"] = np.stack([p["ln_g"], p["ln_b"]])
    out["L2a_base_phases"] = a["L2_attn_base_phases"][:NT]
    out["upto"] = np.triu(np.ones((NT, NT), f))
    out["position_scale"] = np.stack([1 / np.sqrt(tok + 1.0), 1 / np.sqrt((tok + 1.0) * 32)], axis=1).astype(f)
    p = {k: a[f"L2_ffn_{k}"] for k in ("hl_w", "hl_b", "wq", "wk", "wv", "gate_w", "gate_b", "ln_g", "ln_b", "fc1_w",
                                       "fc1_b", "fc2_w", "fc2_b", "fnorm_g", "fnorm_b", "fgate_w")}

    def diagonal(blocks):
        n, r, c = blocks.shape
        m = np.zeros((n, r, n, c), blocks.dtype)
        for k in range(n):
            m[k, :, k, :] = blocks[k]
        return m.reshape(n * r, n * c)

    out["L2f_whl"] = under(p["hl_w"].reshape(D, D).T, p["hl_b"].reshape(D))
    out["L2f_wqk"] = np.stack([diagonal(p["wq"][:, e].transpose(0, 2, 1)) for e in range(4)]
                              + [diagonal(p["wk"].transpose(0, 2, 1))], axis=1)
    out["L2f_wv"] = diagonal(p["wv"].transpose(0, 2, 1))
    out["L2f_wgate"] = diagonal(p["gate_w"].transpose(0, 2, 1)).reshape(2, 128, 16).transpose(1, 0, 2)
    out["L2f_bgate"] = p["gate_b"].reshape(16)
    out["L2f_wfc1"] = under(diagonal(np.stack([p["fc1_w"].T] * 4)), np.tile(p["fc1_b"], 4))
    out["L2f_wfc2"] = under(diagonal(np.stack([p["fc2_w"].T] * 4)), np.tile(p["fc2_b"], 4))
    out["L2f_wfg"] = p["fgate_w"].T
    out["L2f_affine"] = np.stack([p["ln_g"], p["ln_b"], p["fnorm_g"], p["fnorm_b"]])
    out["headmask4"] = (np.arange(D)[:, None] // 16 == np.arange(4)[None, :]).astype(f)
    out["future"] = np.where(tok[None, :] > tok[:, None], f(-3.0e38), f(0))
    return {k: np.ascontiguousarray(v) for k, v in out.items()}


def kernel(**inputs):
    import concourse.bacc as _bacc
    from concourse.bass_utils import run_bass_kernel_spmd as _run

    nc = _bacc.Bacc("TRN2", target_bir_lowering=False, num_devices=1)
    arrays = laid_out(inputs)
    aps = {n: nc.dram_tensor(f"in_{n}", v.shape, mybir.dt.from_np(v.dtype), kind="ExternalInput").ap()
           for n, v in arrays.items()}
    out = nc.dram_tensor("out_0", (NB, NT, D), F32, kind="ExternalOutput").ap()
    program(nc, aps, out)
    r = _run(nc, [{f"in_{n}": v for n, v in arrays.items()}], core_ids=[0])
    return r.results[0]["out_0"]
```

```python
import math
from contextlib import ExitStack

import numpy as np
import concourse.bass as bass
from concourse import mybir

F32 = mybir.dt.float32
U32 = mybir.dt.uint32
BF16 = mybir.dt.bfloat16
ALU = mybir.AluOpType
ACT = mybir.ActivationFunctionType
AX = mybir.AxisListType.X
XY = mybir.AxisListType.XY

NB = 64
NT = 124
D = 64
GS = 4
NG = NB // GS
GT = GS * NT


START = 1
FROM_ZERO = ("loaded", "own", "landed0", "landed1", "stored")


class InOrder:

    def __init__(self, eng, sem, base=0):
        self.eng, self.sem, self.base, self.n = eng, sem, base, 0

    def __call__(self, ins, carrier=None):
        self.n += 1
        ins.then_inc(self.sem, 1)
        self.eng.wait_ge(self.sem, self.base + self.n)
        if carrier is not None:
            carrier()


class Semaphores:

    def __init__(self, nc, ctx, name):
        self.nc, self.ctx, self.name, self.all = nc, ctx, name, []

    def __call__(self, what):
        s = self.ctx.enter_context(self.nc.semaphore(f"{self.name}_{what}"))
        self.all.append((s, 0 if what.endswith(FROM_ZERO) else START))
        return s

    def start(self):
        with self.nc.Block() as block:
            @block.gpsimd
            def _(pool):
                for s, _ in self.all:
                    pool.sem_clear(s)
                for s, first in self.all:
                    if first:
                        pool.sem_inc(s, first)


class Core:

    def __init__(self, nc, ctx, aps):
        self.nc, self.ctx, self.aps = nc, ctx, aps
        self.h = ctx.enter_context(nc.sbuf_tensor("h", [NT, NB, D], F32))
        self.xn = ctx.enter_context(nc.sbuf_tensor("xn", [NT, NB, D], F32))
        self.ident = ctx.enter_context(nc.sbuf_tensor("ident", [128, 128], F32))
        self.eps = ctx.enter_context(nc.sbuf_tensor("eps", [128, 2], F32))


def bc(ap, n, axis):
    ap = ap.unsqueeze(axis)
    shape = list(ap.shape)
    shape[axis] = n
    return ap.broadcast_to(shape)


def transpose_each(core, bank, x, W):
    for s in range(GS):
        wide = x[:, s:s + 2, :].rearrange("p s f -> p (s f)") if s == 0 else x[:, s, :]
        mm = core.nc.tensor.transpose(bank[0:wide.shape[1], s * NT:(s + 1) * NT], wide, core.ident[0:NT, 0:NT])
    return mm


def constants(core):
    nc = core.nc
    with ExitStack() as ctx:
        cleared = ctx.enter_context(nc.semaphore("cleared"))
        block = ctx.enter_context(nc.Block())

        @block.gpsimd
        def _(pool):
            nc.gpsimd.memset(core.eps[:, 0:1], 1e-5)
            nc.gpsimd.memset(core.eps[:, 1:2], 1e-8)
            nc.gpsimd.memset(core.ident[:, :], 0.0).then_inc(cleared, 1)
            pool.wait_ge(cleared, 1)
            nc.gpsimd.affine_select(out=core.ident[:, :], in_=core.ident[:, :], compare_op=ALU.not_equal,
                                    fill=1.0, base=0, pattern=[[-1, 128]], channel_multiplier=1)


def inverse_root(nc, own_done, v, root):
    own_done(nc.vector.reciprocal(root, root))
    own_done(nc.vector.tensor_tensor(v, v, root, ALU.mult))
    own_done(nc.vector.tensor_tensor(v, v, root, ALU.mult))
    own_done(nc.vector.tensor_scalar(v, v, -0.5, 1.5, ALU.mult, ALU.add))
    own_done(nc.vector.tensor_tensor(root, root, v, ALU.mult))


def layer_norm(core, name):
    nc = core.nc
    CH = 4
    W = NB // CH
    with ExitStack() as ctx:
        sem = Semaphores(nc, ctx, name)
        sq = ctx.enter_context(nc.sbuf_tensor(f"{name}_sq", [NT, CH, W, D], F32))
        mean = ctx.enter_context(nc.sbuf_tensor(f"{name}_mean", [NT, CH, W], F32))
        var = ctx.enter_context(nc.sbuf_tensor(f"{name}_var", [NT, CH, W], F32))
        root = ctx.enter_context(nc.sbuf_tensor(f"{name}_root", [NT, CH, W], F32))
        centered, squared, summed, rooted, own = (
            sem("centered"), sem("squared"), sem("summed"), sem("rooted"), sem("own"))
        sem.start()
        block = ctx.enter_context(nc.Block())

        @block.vector
        def _(dve):
            own_done = InOrder(dve, own)
            for c in range(CH):
                hc, xc = core.h[:, c * W:(c + 1) * W, :], core.xn[:, c * W:(c + 1) * W, :]
                own_done(nc.vector.tensor_reduce(mean[:, c, :], hc, AX, ALU.add))
                own_done(nc.vector.tensor_scalar(mean[:, c, :], mean[:, c, :], 1.0 / D, None, ALU.mult))
                nc.vector.tensor_tensor(xc, hc, bc(mean[:, c, :], D, 2), ALU.subtract).then_inc(centered, 1)
            for c in range(CH):
                dve.wait_ge(squared, START + c + 1)
                own_done(nc.vector.tensor_reduce(var[:, c, :], sq[:, c], AX, ALU.add))
                nc.vector.tensor_scalar(var[:, c, :], var[:, c, :], 1.0 / D, 1e-5, ALU.mult, ALU.add).then_inc(summed, 1)
            for c in range(CH):
                xc = core.xn[:, c * W:(c + 1) * W, :]
                dve.wait_ge(rooted, START + c + 1)
                inverse_root(nc, own_done, var[:, c, :], root[:, c, :])
                nc.vector.tensor_tensor(xc, xc, bc(root[:, c, :], D, 2), ALU.mult)

        @block.scalar
        def _(act):
            for c in range(CH):
                act.wait_ge(centered, START + c + 1)
                nc.scalar.activation(sq[:, c], core.xn[:, c * W:(c + 1) * W, :], ACT.Square).then_inc(squared, 1)
            for c in range(CH):
                act.wait_ge(summed, START + c + 1)
                nc.scalar.activation(root[:, c, :], var[:, c, :], ACT.Sqrt).then_inc(rooted, 1)


def window_attention(core, name, biased):
    nc, aps = core.nc, core.aps
    NH, HD = 8, 8
    NK = 71 if biased else 64
    with ExitStack() as ctx:
        if not biased:
            posT, gate, antigate, gate_mass = position_scores(core, name, ctx)
        sem = Semaphores(nc, ctx, name)
        sb = lambda n, shape: ctx.enter_context(nc.sbuf_tensor(f"{name}_{n}", shape, F32))
        wqkv = sb("wqkv", [65, 3 * D])
        wproj = sb("wproj", [65, D])
        headmask = sb("headmask", [D, NH])
        xg = sb("xg", [NT, GS, D])
        xT = sb("xT", [65, GT])
        qT = sb("qT", [NK, GT])
        kT = sb("kT", [D, GT])
        kmask = sb("kmask", [NK, 2, NH, NT])
        v = sb("v", [NT, GS, D])
        negmax = sb("negmax", [NT, 2, NH])
        sums = sb("sums", [NT, GS, NH])
        probs = sb("probs", [NT, 2, NH, NT])
        probsT = sb("probsT", [NT, 2, NH, NT])
        on = sb("on", [NT, GS, D])
        oT = sb("oT", [65, GT])
        ps = lambda n, shape: ctx.enter_context(nc.psum_tensor(f"{name}_{n}", shape, F32))
        bT = ps("bT", [128, 512])
        bQ = ps("bQ", [128, 512])
        bS = ps("bS", [128, 2, 2, 512])
        bP = ps("bP", [128, 2, 512])

        loaded, ones = sem("loaded"), sem("ones")
        xg_ready, x_transposed, xT_ready = sem("xg_ready"), sem("x_transposed"), sem("xT_ready")
        q_made, q_taken, k_made, k_taken, v_made, v_taken = (
            sem(n) for n in ("q_made", "q_taken", "k_made", "k_taken", "v_made", "v_taken"))
        kmask_ready, scores_made, max_ready, exp_done = (
            sem(n) for n in ("kmask_ready", "scores_made", "max_ready", "exp_done"))
        pT_made, pT_taken, pv_made, on_ready = (sem(n) for n in ("pT_made", "pT_taken", "pv_made", "on_ready"))
        oT_made, oT_taken, y_made, y_taken = (sem(n) for n in ("oT_made", "oT_taken", "y_made", "y_taken"))
        own = sem("own")
        NLOAD = 6 if biased else 3
        OWN = 1 if biased else 8
        if not biased:
            total = sb("total", [NT, GS, NH])
            posshare = sb("posshare", [NT, GS, NH])
            o2 = sb("o2", [NT, GS, D])
            o2_made = sem("o2_made")
        sem.start()
        block = ctx.enter_context(nc.Block())

        @block.sync
        def _(sp):
            sp.dma_start(wqkv[:, :], aps[f"{name}_wqkv"]).then_inc(loaded, 16)
            sp.dma_start(wproj[:, :], aps[f"{name}_wproj"]).then_inc(loaded, 16)
            sp.dma_start(headmask[:, :], aps["headmask8"]).then_inc(loaded, 16)
            if biased:
                sp.dma_start(qT[D:NK, :], aps["onehot7"]).then_inc(loaded, 16)
                for u in range(2):
                    sp.dma_start(kmask[D:NK, u, :, :], aps[f"{name}_bias7"]).then_inc(loaded, 16)

        @block.gpsimd
        def _(pool):
            nc.gpsimd.memset(xT[D:D + 1, :], 1.0).then_inc(ones, 1)
            nc.gpsimd.memset(oT[D:D + 1, :], 1.0).then_inc(ones, 1)
            pool.wait_ge(ones, START + 2)
            with pool.Fori(0, NG) as g:
                pool.wait_ge(x_transposed, START + g)
                nc.gpsimd.tensor_copy(xg[:, :, :], core.xn[:, bass.ds(g * GS, GS), :]).then_inc(xg_ready, 1)

        @block.tensor
        def _(pe):
            pe.wait_ge(loaded, 16 * NLOAD)
            pe.wait_ge(ones, START + 2)

            def queries(g):
                pe.wait_ge(pT_taken, START + GS * g)
                pe.wait_ge(xg_ready, START + g + 1)
                transpose_each(core, bP[:, 0, :], xg, D).then_inc(x_transposed, 1)
                pe.wait_ge(xT_ready, START + g + 1)
                nc.tensor.matmul(bP[0:D, 1, 0:GT], wqkv[:, 0:D], xT[:, :], start=True, stop=True).then_inc(q_made, 1)
                for s in range(GS):
                    mm = nc.tensor.matmul(bP[0:NT, 0, s * D:(s + 1) * D], xT[:, s * NT:(s + 1) * NT],
                                          wqkv[:, 2 * D:3 * D], start=True, stop=True)
                mm.then_inc(v_made, 1)

            def keys(g):
                pe.wait_ge(q_taken, START + g + 1)
                nc.tensor.matmul(bP[0:D, 1, 0:GT], wqkv[:, D:2 * D], xT[:, :], start=True, stop=True).then_inc(k_made, 1)

            def turn(g, more):
                def scores(s):
                    pe.wait_ge(kmask_ready, START + GS * g + s + 1)
                    pe.wait_ge(exp_done, START + GS * g + max(s - 1, 0))
                    for half in range(2):
                        mm = nc.tensor.matmul(bS[0:NT, s % 2, half, 0:GT], qT[:, s * NT:(s + 1) * NT],
                                              kmask[:, s % 2, half * 4:half * 4 + 4, :].rearrange("p h m -> p (h m)"),
                                              start=True, stop=True)
                    mm.then_inc(scores_made, 1)

                def values(s):
                    pe.wait_ge(v_taken, START + g + 1)
                    pe.wait_ge(exp_done, START + GS * g + s + 1)
                    pe.wait_ge(pT_taken, START + GS * g + s)
                    for h in range(NH):
                        mm = nc.tensor.transpose(bP[0:NT, h // 4, (h % 4) * NT:(h % 4 + 1) * NT],
                                                 probs[:, s % 2, h, :], core.ident[0:NT, 0:NT])
                    mm.then_inc(pT_made, 1)

                def weigh(s):
                    pe.wait_ge(pT_taken, START + GS * g + s + 1)
                    pe.wait_ge(y_taken, START + g)
                    for h in range(NH):
                        mm = nc.tensor.matmul(bT[0:NT, s * D + h * HD:s * D + (h + 1) * HD], probsT[:, s % 2, h, :],
                                              v[:, s, h * HD:(h + 1) * HD], start=True, stop=True)
                    mm.then_inc(pv_made, 1)

                scores(0)
                for s in range(GS):
                    if s + 1 < GS:
                        scores(s + 1)
                    values(s)
                    if s >= 1:
                        weigh(s - 1)
                weigh(GS - 1)
                if not biased:
                    for h in range(NH):
                        mm = nc.tensor.matmul(
                            bQ[0:NT, 0:GS * D].rearrange("p (s f) -> p s f", s=GS)[:, :, h * HD:(h + 1) * HD],
                            posT[:, h, :], v[:, :, h * HD:(h + 1) * HD], start=True, stop=True)
                    mm.then_inc(o2_made, 1)
                if more:
                    queries(g + 1)
                pe.wait_ge(on_ready, START + g + 1)
                mm = transpose_each(core, bQ, on, D)
                mm.then_inc(oT_made, 1)
                if more:
                    keys(g + 1)
                pe.wait_ge(oT_taken, START + g + 1)
                for s in range(GS):
                    mm = nc.tensor.matmul(bT[0:NT, s * D:(s + 1) * D], oT[:, s * NT:(s + 1) * NT], wproj[:, :],
                                          start=True, stop=True)
                mm.then_inc(y_made, 1)

            queries(0)
            keys(0)
            with pe.Fori(0, NG - 1) as g:
                turn(g, True)
            turn(NG - 1, False)

        @block.scalar
        def _(act):
            def take_queries(g):
                act.wait_ge(x_transposed, START + g + 1)
                act.wait_ge(k_made, START + g)
                nc.scalar.copy(xT[0:D, :], bP[0:D, 0, 0:GT]).then_inc(xT_ready, 1)
                act.wait_ge(q_made, START + g + 1)
                act.wait_ge(scores_made, START + GS * g)
                nc.scalar.activation(qT[0:D, :], bP[0:D, 1, 0:GT], ACT.Copy, scale=float(HD) ** -0.5).then_inc(q_taken, 1)
                act.wait_ge(v_made, START + g + 1)
                act.wait_ge(pv_made, START + GS * g)
                if not biased:
                    act.wait_ge(o2_made, START + g)
                nc.scalar.copy(v[:, :, :], bP[0:NT, 0, 0:GS * D].rearrange("p (s f) -> p s f", s=GS)).then_inc(v_taken, 1)

            def take_keys(g):
                act.wait_ge(k_made, START + g + 1)
                act.wait_ge(kmask_ready, START + GS * g)
                nc.scalar.copy(kT[:, :], bP[0:D, 1, 0:GT]).then_inc(k_taken, 1)

            def turn(g, more):
                for s in range(GS):
                    act.wait_ge(max_ready, START + GS * g + s + 1)
                    act.wait_ge(pT_made, START + GS * g + max(s - 1, 0))
                    if s == 0:
                        act.wait_ge(on_ready, START + g)
                    for h in range(NH):
                        ins = nc.scalar.activation(probs[:, s % 2, h, :],
                                                   bS[0:NT, s % 2, h // 4, (h % 4) * NT:(h % 4 + 1) * NT],
                                                   ACT.Exp, bias=negmax[:, s % 2, h:h + 1],
                                                   accum_out=sums[:, s, h:h + 1])
                    ins.then_inc(exp_done, 1)
                if more:
                    take_queries(g + 1)
                act.wait_ge(oT_made, START + g + 1)
                nc.scalar.copy(oT[0:D, :], bQ[0:D, 0:GT]).then_inc(oT_taken, 1)
                if more:
                    take_keys(g + 1)

            take_queries(0)
            take_keys(0)
            with act.Fori(0, NG - 1) as g:
                turn(g, True)
            turn(NG - 1, False)

        @block.vector
        def _(dve):
            dve.wait_ge(loaded, 16 * NLOAD)
            with dve.Fori(0, NG) as g:
                own_done = InOrder(dve, own, g * OWN)

                def mask_keys(s):
                    dve.wait_ge(k_taken, START + g + 1)
                    dve.wait_ge(scores_made, START + GS * g + max(s - 1, 0))
                    nc.vector.tensor_tensor(kmask[0:D, s % 2, :, :], bc(kT[:, s * NT:(s + 1) * NT], NH, 1),
                                            bc(headmask[:, :], NT, 2), ALU.mult).then_inc(kmask_ready, 1)

                def maxima(s):
                    dve.wait_ge(scores_made, START + GS * g + s + 1)
                    dve.wait_ge(exp_done, START + GS * g + max(s - 1, 0))
                    for half in range(2):
                        ins = nc.vector.tensor_reduce(negmax[:, s % 2, half * 4:half * 4 + 4],
                                                      bS[0:NT, s % 2, half, 0:GT].rearrange("p (h m) -> p h m", h=4),
                                                      AX, ALU.max, negate=True)
                    ins.then_inc(max_ready, 1)

                def take_probs(s):
                    dve.wait_ge(pT_made, START + GS * g + s + 1)
                    dve.wait_ge(pv_made, START + GS * g + max(s - 1, 0))
                    for half in range(2):
                        ins = nc.vector.tensor_copy(
                            probsT[:, s % 2, half * 4:half * 4 + 4, :].rearrange("p h m -> p (h m)"),
                            bP[0:NT, half, 0:GT])
                    ins.then_inc(pT_taken, 1)

                mask_keys(0)
                mask_keys(1)
                maxima(0)
                for s in range(GS):
                    if s + 2 < GS:
                        mask_keys(s + 2)
                    if s + 1 < GS:
                        maxima(s + 1)
                    take_probs(s)
                if not biased:
                    nc.vector.tensor_copy(total[:, :, :], sums[:, :, :])
                own_done(nc.vector.reciprocal(sums[:, :, :], sums[:, :, :]))
                dve.wait_ge(pv_made, START + GS * (g + 1))
                heads = lambda t: t.rearrange("p s (h e) -> p (s h) e", h=NH)
                pv = bT[0:NT, 0:GS * D].rearrange("p (x e) -> p x e", e=HD)
                each = lambda t: bc(t[:, :, :].rearrange("p s h -> p (s h)"), HD, 2)
                if biased:
                    nc.vector.tensor_tensor(heads(on[:, :, :]), pv, each(sums), ALU.mult).then_inc(on_ready, 1)
                else:
                    own_done(nc.vector.tensor_tensor(sums[:, :, :], sums[:, :, :], bc(antigate[:, :], GS, 1), ALU.mult))
                    own_done(nc.vector.tensor_tensor(total[:, :, :], total[:, :, :], sums[:, :, :], ALU.mult))
                    own_done(nc.vector.tensor_tensor(total[:, :, :], total[:, :, :], bc(gate_mass[:, :], GS, 1), ALU.add))
                    own_done(nc.vector.reciprocal(total[:, :, :], total[:, :, :]))
                    nc.vector.tensor_tensor(posshare[:, :, :], total[:, :, :], bc(gate[:, :], GS, 1), ALU.mult)
                    own_done(nc.vector.tensor_tensor(sums[:, :, :], sums[:, :, :], total[:, :, :], ALU.mult))
                    own_done(nc.vector.tensor_tensor(heads(on[:, :, :]), pv, each(sums), ALU.mult))
                    dve.wait_ge(o2_made, START + g + 1)
                    own_done(nc.vector.tensor_tensor(heads(o2[:, :, :]),
                                                     bQ[0:NT, 0:GS * D].rearrange("p (x e) -> p x e", e=HD),
                                                     each(posshare), ALU.mult))
                    nc.vector.tensor_tensor(on[:, :, :], on[:, :, :], o2[:, :, :], ALU.add).then_inc(on_ready, 1)
                dve.wait_ge(y_made, START + g + 1)
                hg = core.h[:, bass.ds(g * GS, GS), :]
                nc.vector.tensor_tensor(hg, hg, bT[0:NT, 0:GS * D].rearrange("p (s f) -> p s f", s=GS),
                                        ALU.add).then_inc(y_taken, 1)
                assert own_done.n == OWN, own_done.n


def position_scores(core, name, ctx):
    nc, aps = core.nc, core.aps
    NH = 8
    kept = lambda n, shape: ctx.enter_context(nc.sbuf_tensor(f"{name}_{n}", shape, F32))
    posT = kept("posT", [NT, NH, NT])
    gate, antigate, gate_mass = (kept(n, [NT, NH]) for n in ("gate", "antigate", "gate_mass"))
    with ExitStack() as own_ctx:
        sem = Semaphores(nc, own_ctx, name)
        sb = lambda n, shape: own_ctx.enter_context(nc.sbuf_tensor(f"{name}_{n}", shape, F32))
        rel = sb("rel", [NT, 3, NT])
        wpos = sb("wpos", [NT, 3, NH])
        bpos = sb("bpos", [NT, NH])
        score = sb("score", [NT, NH, NT])
        term = sb("term", [NT, NH, NT])
        maxima = sb("posmax", [NT, NH])
        mass = sb("posmass", [NT, NH])
        bP = own_ctx.enter_context(nc.psum_tensor(f"{name}_posP", [128, 2, 512], F32))
        loaded, own, centered, exp_done, softmaxed, transposed, gate_exp = (
            sem(n) for n in ("pos_loaded", "pos_own", "pos_centered", "pos_exp", "pos_softmaxed", "pos_transposed",
                             "gate_exp"))
        sem.start()
        block = own_ctx.enter_context(nc.Block())

        @block.sync
        def _(sp):
            sp.dma_start(rel[:, :, :], aps["posrel"]).then_inc(loaded, 16)
            sp.dma_start(wpos[:, :, :], aps[f"{name}_wpos"].partition_broadcast(NT)).then_inc(loaded, 16)
            sp.dma_start(bpos[:, :], aps[f"{name}_bpos"].partition_broadcast(NT)).then_inc(loaded, 16)
            sp.dma_start(gate[:, :], aps[f"{name}_gating"].partition_broadcast(NT)).then_inc(loaded, 16)

        @block.vector
        def _(dve):
            own_done = InOrder(dve, own)
            dve.wait_ge(loaded, 64)
            for c in range(3):
                to = term if c else score
                own_done(nc.vector.tensor_tensor(to[:, :, :], bc(rel[:, c, :], NH, 1), bc(wpos[:, c, :], NT, 2), ALU.mult))
                if c:
                    own_done(nc.vector.tensor_tensor(score[:, :, :], score[:, :, :], term[:, :, :], ALU.add))
            own_done(nc.vector.tensor_tensor(score[:, :, :], score[:, :, :], bc(bpos[:, :], NT, 2), ALU.add))
            own_done(nc.vector.tensor_reduce(maxima[:, :], score[:, :, :], AX, ALU.max))
            nc.vector.tensor_tensor(score[:, :, :], score[:, :, :], bc(maxima[:, :], NT, 2),
                                    ALU.subtract).then_inc(centered, 1)
            dve.wait_ge(exp_done, START + 1)
            own_done(nc.vector.tensor_reduce(mass[:, :], score[:, :, :], AX, ALU.add))
            own_done(nc.vector.reciprocal(mass[:, :], mass[:, :]))
            own_done(nc.vector.tensor_tensor(score[:, :, :], score[:, :, :], bc(mass[:, :], NT, 2), ALU.mult))
            own_done(nc.vector.tensor_reduce(mass[:, :], score[:, :, :], AX, ALU.add))
            dve.wait_ge(gate_exp, START + 1)
            own_done(nc.vector.tensor_scalar(gate[:, :], gate[:, :], 1.0, None, ALU.add))
            own_done(nc.vector.reciprocal(gate[:, :], gate[:, :]))
            nc.vector.tensor_scalar(antigate[:, :], gate[:, :], -1.0, 1.0, ALU.mult, ALU.add)
            nc.vector.tensor_tensor(gate_mass[:, :], gate[:, :], mass[:, :], ALU.mult).then_inc(softmaxed, 1)
            dve.wait_ge(transposed, START + 1)
            for half in range(2):
                nc.vector.tensor_copy(posT[:, half * 4:half * 4 + 4, :].rearrange("p h m -> p (h m)"),
                                      bP[0:NT, half, 0:4 * NT])

        @block.scalar
        def _(act):
            act.wait_ge(centered, START + 1)
            nc.scalar.activation(score[:, :, :], score[:, :, :], ACT.Exp).then_inc(exp_done, 1)
            act.wait_ge(loaded, 64)
            nc.scalar.activation(gate[:, :], gate[:, :], ACT.Exp, scale=-1.0).then_inc(gate_exp, 1)

        @block.tensor
        def _(pe):
            pe.wait_ge(softmaxed, START + 1)
            for h in range(NH):
                mm = nc.tensor.transpose(bP[0:NT, h // 4, (h % 4) * NT:(h % 4 + 1) * NT], score[:, h, :],
                                         core.ident[0:NT, 0:NT])
            mm.then_inc(transposed, 1)
    return posT, gate, antigate, gate_mass


def experts(core, name, E, F, normed):
    nc, aps = core.nc, core.aps
    with ExitStack() as kept:
        keep = lambda n, shape: kept.enter_context(nc.sbuf_tensor(f"{name}_{n}", shape, F32))
        parts = [kept.enter_context(nc.sbuf_tensor(f"{name}_parts{n}", [2 * D, NB * NT], BF16)) for n in ("11", "22", "31")]
        weight = keep("weight", [NT, NB, E])
        acc = core.xn if normed else core.h
        route(core, name, E, parts, weight, acc)

        with ExitStack() as ctx:
            sem = Semaphores(nc, ctx, name)
            sb = lambda n, shape: ctx.enter_context(nc.sbuf_tensor(f"{name}_{n}", shape, F32))
            ps = lambda n, shape: ctx.enter_context(nc.psum_tensor(f"{name}_{n}", shape, F32))
            w1 = sb("w1", [2 * D, 2, 2, F])
            w12 = ctx.enter_context(nc.sbuf_tensor(f"{name}_w12", [2 * D, 2, 2, F], BF16))
            w13 = ctx.enter_context(nc.sbuf_tensor(f"{name}_w13", [2 * D, 2, 2, F], BF16))
            b1 = sb("b1", [F, 2, 2])
            zero = sb("zero", [2 * D, 2, F])
            w2 = sb("w2", [F, 2, 2, D])
            hid = sb("hid", [F, 2, 2, GT])
            part = sb("part", [NT, 2, 2, GS, D])
            bH = ps("bH", [128, 2, 2, 512])
            bY = ps("bY", [128, 2, 512])
            landed = [sem("landed0"), sem("landed1")]
            zero_set, own, split_ready, h_made, hid_ready, y_made, y_taken, parted = (
                sem(n) for n in ("zero_set", "own", "split_ready", "h_made", "hid_ready", "y_made", "y_taken", "parted"))
            sem.start()
            block = ctx.enter_context(nc.Block())
            PAIRS = E // 2
            NP = PAIRS // 2
            NL = NG // 2

            @block.sync
            def _(sp):
                def load(slot, p):
                    for to, w in ((w1[0:D, slot].rearrange("p e f -> p (e f)"), aps[f"{name}_w1"]),
                                  (w1[D:2 * D, slot].rearrange("p e f -> p (e f)"), aps[f"{name}_w1"]), (b1[:, slot, :], aps[f"{name}_b1"]),
                                  (w2[:, slot, :, :].rearrange("p e f -> p (e f)"), aps[f"{name}_w2"])):
                        src = w[p, :, :] if isinstance(p, int) else w[bass.ds(p, 1), :, :].squeeze(0)
                        sp.dma_start(to, src).then_inc(landed[slot], 16)

                for slot in range(2):
                    load(slot, slot)
                with sp.Fori(0, NP - 1) as i:
                    for slot in range(2):
                        sp.wait_ge(y_made, START + i * (4 * NL) + 2 * NL * (slot + 1))
                        load(slot, (i + 1) * 2 + slot)

            @block.gpsimd
            def _(pool):
                OWN = 5
                nc.gpsimd.memset(zero[:, :, :], 0.0).then_inc(zero_set, 1)
                pool.wait_ge(zero_set, START + 1)
                rounded = lambda to, x: nc.gpsimd.tensor_tensor(to, x, zero[0:x.shape[0]], ALU.add)
                with pool.Fori(0, NP) as i:
                    for slot in range(2):
                        own_done = InOrder(pool, own, (i * 2 + slot) * OWN)
                        w, a, b = w1[:, slot], w12[:, slot], w13[:, slot]
                        pool.wait_ge(landed[slot], i * 64 + 64)
                        pool.wait_ge(split_ready, START + i * 2 + slot)
                        own_done(rounded(b, w))
                        own_done(nc.gpsimd.tensor_tensor(w, w, b, ALU.subtract))
                        own_done(rounded(a, w))
                        own_done(nc.gpsimd.tensor_tensor(w, w, a, ALU.subtract))
                        own_done(rounded(a[0:D], b[0:D]))
                        nc.gpsimd.tensor_tensor(b[D:2 * D], w[D:2 * D], zero[D:2 * D], ALU.add).then_inc(split_ready, 1)
                        assert own_done.n == OWN

            @block.tensor
            def _(pe):
                with pe.Fori(0, NP) as i:
                    for slot in range(2):
                        with pe.Fori(0, NL) as j:
                            pe.wait_ge(split_ready, START + i * 2 + (slot + 1))
                            t = (i * 2 + slot) * NL + j
                            for u in range(2):
                                pe.wait_ge(hid_ready, START + t * 4)
                                for e in range(2):
                                    for n, w in enumerate((w13, w12, w12)):
                                        mm = nc.tensor.matmul(bH[0:F, u, e, 0:GT], w[:, slot, e, :],
                                                              parts[2 - n][:, bass.ds((j * 2 + u) * GT, GT)],
                                                              start=(n == 0), stop=(n == 2))
                                    mm.then_inc(h_made, 1)
                            for u in range(2):
                                pe.wait_ge(y_taken, START + t * 2)
                                for e in range(2):
                                    pe.wait_ge(hid_ready, START + t * 4 + (2 * u + e + 1))
                                    for s in range(GS):
                                        c = (e * GS + s) * D
                                        mm = nc.tensor.matmul(bY[0:NT, u, c:c + D], hid[:, u, e, s * NT:(s + 1) * NT],
                                                              w2[:, slot, e, :], start=True, stop=True)
                                mm.then_inc(y_made, 1)

            @block.scalar
            def _(act):
                with act.Fori(0, NP) as i:
                    for slot in range(2):
                        with act.Fori(0, NL) as j:
                            act.wait_ge(landed[slot], i * 64 + 64)
                            t = (i * 2 + slot) * NL + j
                            for u in range(2):
                                act.wait_ge(y_made, START + t * 2)
                                for e in range(2):
                                    act.wait_ge(h_made, START + t * 4 + (2 * u + e + 1))
                                    nc.scalar.activation(hid[:, u, e, :], bH[0:F, u, e, 0:GT], ACT.Relu,
                                                         bias=b1[:, slot, e:e + 1]).then_inc(hid_ready, 1)

            @block.vector
            def _(dve):
                with dve.Fori(0, NP) as i:
                    for slot in range(2):
                        with dve.Fori(0, NL) as j:
                            t = (i * 2 + slot) * NL + j
                            for u in range(2):
                                g = j * 2 + u
                                dve.wait_ge(y_made, START + t * 2 + (u + 1))
                                wg = weight[:, bass.ds(g * GS, GS), bass.ds((i * 2 + slot) * 2, 2)]
                                nc.vector.tensor_tensor(part[:, u], bY[0:NT, u, :].rearrange("p (e s f) -> p e s f", e=2, s=GS),
                                                        bc(wg.rearrange("p s e -> p e s"), D, 3), ALU.mult).then_inc(y_taken, 1)
                                ag = acc[:, bass.ds(g * GS, GS), :]
                                for e in range(2):
                                    dve.wait_ge(y_taken, START + t * 2 + (u + 1))
                                    if e:
                                        dve.wait_ge(parted, START + t * 4 + (2 * u + e))
                                    nc.vector.tensor_tensor(ag, ag, part[:, u, e], ALU.add).then_inc(parted, 1)


def route(core, name, E, parts, weight, acc):
    nc, aps = core.nc, core.aps
    with ExitStack() as ctx:
        sem = Semaphores(nc, ctx, name)
        sb = lambda n, shape, dt=F32: ctx.enter_context(nc.sbuf_tensor(f"{name}_{n}", shape, dt))
        ps = lambda n, shape: ctx.enter_context(nc.psum_tensor(f"{name}_{n}", shape, F32))
        wr = sb("wr", [D, E])
        br = sb("br", [NT, E])
        b2 = sb("b2", [E, D])
        iota = sb("iota", [NT, E])
        xg = sb("xg", [NT, GS, 2, D])
        xgT = sb("xgT", [D, GT])
        part1, part2, part31 = (sb(n, [2 * D, GT], BF16) for n in ("part1", "part2", "part31"))
        rest = sb("rest", [2 * D, GT])
        logits = sb("logits", [NT, GS, E])
        top = sb("top", [NT, GS, 8])
        topi = sb("topi", [NT, GS, 8], U32)
        topf = sb("topf", [NT, GS, 2])
        idle = sb("idle", [NT, 1])
        carrier = lambda: nc.vector.memset(idle[:, :], 0.0)
        odds = sb("odds", [NT, GS])
        share = sb("share", [NT, 2, GS])
        second = sb("second", [NT, GS, E])
        wg = sb("wg", [NT, GS, E])
        wT = sb("wT", [E, GT])
        bX, bL, bW, bB = (ps(n, [128, 512]) for n in ("bX", "bL", "bW", "bB"))
        loaded, xg_ready, x_transposed, xT_ready, logits_made, gap_ready, odds_ready, wg_ready = (
            sem(n) for n in ("route_loaded", "xg_ready", "x_transposed", "xT_ready", "logits_made", "gap_ready",
                             "odds_ready", "wg_ready"))
        parts_ready, parts_kept = (sem(n) for n in ("parts_ready", "parts_kept"))
        w_transposed, wT_ready, bias_made, bias_taken, own = (
            sem(n) for n in ("w_transposed", "wT_ready", "bias_made", "bias_taken", "own"))
        sem.start()
        block = ctx.enter_context(nc.Block())
        OWN = 12

        @block.sync
        def _(sp):
            sp.dma_start(wr[:, :], aps[f"{name}_wr"]).then_inc(loaded, 16)
            sp.dma_start(br[:, :], aps[f"{name}_br"].partition_broadcast(NT)).then_inc(loaded, 16)
            sp.dma_start(b2[:, :], aps[f"{name}_b2"]).then_inc(loaded, 16)
            sp.dma_start(iota[:, :], aps[f"iota{E}"].partition_broadcast(NT)).then_inc(loaded, 16)

        @block.gpsimd
        def _(pool):
            with pool.Fori(0, NG) as g:
                pool.wait_ge(x_transposed, START + g)
                for c in range(2):
                    ins = nc.gpsimd.tensor_copy(xg[:, :, c, :], core.xn[:, bass.ds(g * GS, GS), :])
                ins.then_inc(xg_ready, 1)
                pool.wait_ge(parts_ready, START + g + 1)
                at = bass.ds(g * GT, GT)
                nc.gpsimd.tensor_copy(parts[0][:, at], part1[:, :])
                nc.gpsimd.tensor_copy(parts[1][:, at], part2[:, :])
                nc.gpsimd.tensor_copy(parts[2][:, at], part31[:, :]).then_inc(parts_kept, 1)

        @block.tensor
        def _(pe):
            pe.wait_ge(loaded, 64)
            with pe.Fori(0, NG) as g:
                pe.wait_ge(xT_ready, START + g)
                pe.wait_ge(parts_ready, START + g)
                pe.wait_ge(xg_ready, START + g + 1)
                for s in range(GS):
                    mm = nc.tensor.transpose(bX[:, s * NT:(s + 1) * NT], xg[:, s, :, :].rearrange("p c f -> p (c f)"),
                                             core.ident[0:NT, 0:NT])
                mm.then_inc(x_transposed, 1)
                pe.wait_ge(xT_ready, START + g + 1)
                pe.wait_ge(gap_ready, START + g)
                for s in range(GS):
                    mm = nc.tensor.matmul(bL[0:NT, s * E:(s + 1) * E], xgT[:, s * NT:(s + 1) * NT], wr[:, :],
                                          start=True, stop=True)
                mm.then_inc(logits_made, 1)
                pe.wait_ge(wT_ready, START + g)
                pe.wait_ge(wg_ready, START + g + 1)
                mm = transpose_each(core, bW, wg, E)
                mm.then_inc(w_transposed, 1)
                pe.wait_ge(wT_ready, START + g + 1)
                pe.wait_ge(bias_taken, START + g)
                for s in range(GS):
                    mm = nc.tensor.matmul(bB[0:NT, s * D:(s + 1) * D], wT[:, s * NT:(s + 1) * NT], b2[:, :],
                                          start=True, stop=True)
                mm.then_inc(bias_made, 1)

        @block.scalar
        def _(act):
            with act.Fori(0, NG) as g:
                act.wait_ge(x_transposed, START + g + 1)
                act.wait_ge(logits_made, START + g)
                act.wait_ge(parts_kept, START + g)
                nc.scalar.copy(part1[:, :], bX[:, 0:GT])
                nc.scalar.copy(part31[D:2 * D, :], bX[D:2 * D, 0:GT])
                nc.scalar.copy(xgT[:, :], bX[0:D, 0:GT]).then_inc(xT_ready, 1)
                act.wait_ge(gap_ready, START + g + 1)
                nc.scalar.activation(share[:, 1, :], odds[:, :], ACT.Exp).then_inc(odds_ready, 1)
                act.wait_ge(w_transposed, START + g + 1)
                act.wait_ge(bias_made, START + g)
                nc.scalar.copy(wT[:, :], bW[0:E, 0:GT]).then_inc(wT_ready, 1)

        @block.vector
        def _(dve):
            dve.wait_ge(loaded, 64)
            with dve.Fori(0, NG) as g:
                own_done = InOrder(dve, own, g * OWN)
                dve.wait_ge(xT_ready, START + g + 1)
                dve.wait_ge(parts_kept, START + g)
                own_done(nc.vector.tensor_tensor(rest[:, :], bX[:, 0:GT], part1[:, :], ALU.subtract))
                own_done(nc.vector.tensor_copy(part2[:, :], rest[:, :]))
                nc.vector.tensor_tensor(part31[0:D, :], rest[0:D, :], part2[0:D, :], ALU.subtract).then_inc(parts_ready, 1)
                dve.wait_ge(logits_made, START + g + 1)
                own_done(nc.vector.tensor_tensor(logits[:, :, :], bL[0:NT, 0:GS * E].rearrange("p (s e) -> p s e", s=GS),
                                                 bc(br[:, :], GS, 1), ALU.add), carrier)
                for s in range(GS):
                    ins = nc.vector.max(top[:, s, :], logits[:, s, :])
                own_done(ins, carrier)
                for s in range(GS):
                    ins = nc.vector.max_index(topi[:, s, :], top[:, s, :], logits[:, s, :])
                own_done(ins)
                own_done(nc.vector.tensor_copy(topf[:, :, :], topi[:, :, 0:2]))
                nc.vector.tensor_tensor(odds[:, :], top[:, :, 1], top[:, :, 0], ALU.subtract).then_inc(gap_ready, 1)
                dve.wait_ge(odds_ready, START + g + 1)
                own_done(nc.vector.tensor_scalar(share[:, 0, :], share[:, 1, :], 1.0, None, ALU.add))
                own_done(nc.vector.reciprocal(share[:, 0, :], share[:, 0, :]))
                own_done(nc.vector.tensor_tensor(share[:, 1, :], share[:, 1, :], share[:, 0, :], ALU.mult))
                dve.wait_ge(w_transposed, START + g)
                each = lambda t: bc(t, E, 2)
                at = bc(iota[:, :], GS, 1)
                own_done(nc.vector.tensor_tensor(wg[:, :, :], at, each(topf[:, :, 0]), ALU.is_equal))
                nc.vector.tensor_tensor(second[:, :, :], at, each(topf[:, :, 1]), ALU.is_equal)
                own_done(nc.vector.tensor_tensor(wg[:, :, :], wg[:, :, :], each(share[:, 0, :]), ALU.mult))
                own_done(nc.vector.tensor_tensor(second[:, :, :], second[:, :, :], each(share[:, 1, :]), ALU.mult))
                nc.vector.tensor_tensor(wg[:, :, :], wg[:, :, :], second[:, :, :], ALU.add).then_inc(wg_ready, 1)
                dve.wait_ge(wg_ready, START + g + 1)
                nc.vector.tensor_copy(weight[:, bass.ds(g * GS, GS), :], wg[:, :, :])
                dve.wait_ge(bias_made, START + g + 1)
                dve.wait_ge(x_transposed, START + g + 1)
                ag = acc[:, bass.ds(g * GS, GS), :]
                nc.vector.tensor_tensor(ag, ag, bB[0:NT, 0:GS * D].rearrange("p (s f) -> p s f", s=GS),
                                        ALU.add).then_inc(bias_taken, 1)
                assert own_done.n == OWN, own_done.n


def add_normed(core, name):
    nc, aps = core.nc, core.aps
    CH = 4
    W = NB // CH
    with ExitStack() as ctx:
        sem = Semaphores(nc, ctx, name)
        sb = lambda n, shape: ctx.enter_context(nc.sbuf_tensor(f"{name}_{n}", shape, F32))
        affine = sb("affine", [NT, 2, D])
        sq = sb("sq", [NT, CH, W, D])
        mean = sb("mean", [NT, CH, W])
        var, root = sb("var", [NT, CH, W]), sb("root", [NT, CH, W])
        loaded, centered, squared, summed, rooted, own = (
            sem(n) for n in ("affine_loaded", "centered", "squared", "summed", "rooted", "own"))
        sem.start()
        block = ctx.enter_context(nc.Block())

        @block.sync
        def _(sp):
            sp.dma_start(affine[:, :, :], aps[f"{name}_affine"].partition_broadcast(NT)).then_inc(loaded, 16)

        @block.vector
        def _(dve):
            own_done = InOrder(dve, own)
            for c in range(CH):
                xc = core.xn[:, c * W:(c + 1) * W, :]
                own_done(nc.vector.tensor_reduce(mean[:, c, :], xc, AX, ALU.add))
                own_done(nc.vector.tensor_scalar(mean[:, c, :], mean[:, c, :], 1.0 / D, None, ALU.mult))
                nc.vector.tensor_tensor(xc, xc, bc(mean[:, c, :], D, 2), ALU.subtract).then_inc(centered, 1)
            for c in range(CH):
                dve.wait_ge(squared, START + c + 1)
                own_done(nc.vector.tensor_reduce(var[:, c, :], sq[:, c], AX, ALU.add))
                nc.vector.tensor_scalar(var[:, c, :], var[:, c, :], 1.0 / D, 1e-5, ALU.mult, ALU.add).then_inc(summed, 1)
            dve.wait_ge(loaded, 16)
            for c in range(CH):
                xc = core.xn[:, c * W:(c + 1) * W, :]
                hc = core.h[:, c * W:(c + 1) * W, :]
                dve.wait_ge(rooted, START + c + 1)
                inverse_root(nc, own_done, var[:, c, :], root[:, c, :])
                own_done(nc.vector.tensor_tensor(xc, xc, bc(root[:, c, :], D, 2), ALU.mult))
                own_done(nc.vector.tensor_tensor(xc, xc, bc(affine[:, 0, :], W, 1), ALU.mult))
                own_done(nc.vector.tensor_tensor(xc, xc, bc(affine[:, 1, :], W, 1), ALU.add))
                nc.vector.tensor_tensor(hc, hc, xc, ALU.add)

        @block.scalar
        def _(act):
            for c in range(CH):
                act.wait_ge(centered, START + c + 1)
                nc.scalar.activation(sq[:, c], core.xn[:, c * W:(c + 1) * W, :], ACT.Square).then_inc(squared, 1)
            for c in range(CH):
                act.wait_ge(summed, START + c + 1)
                nc.scalar.activation(root[:, c, :], var[:, c, :], ACT.Sqrt).then_inc(rooted, 1)


def lattice_attention(core, name):
    nc, aps = core.nc, core.aps
    NH, HD = 8, 64
    NL = NH * HD
    PHI = (1.0 + math.sqrt(5.0)) / 2.0
    C1 = PHI * math.sqrt(2.0) * 51.85
    C2 = math.pi / PHI
    ROUND = 1.5 * 2.0 ** 23
    TURN = 6.283184
    WIDTH = NH * NT
    with ExitStack() as ctx:
        sem = Semaphores(nc, ctx, name)
        sb = lambda n, shape: ctx.enter_context(nc.sbuf_tensor(f"{name}_{n}", shape, F32))
        ps = lambda n, shape: ctx.enter_context(nc.psum_tensor(f"{name}_{n}", shape, F32))
        wqkv = sb("wqkv", [65, 3 * NL])
        wo = sb("wo", [128, 4, D])
        bo = sb("bo", [1, D])
        ones = sb("ones", [1, NT])
        halfpi = sb("halfpi", [NT, 1])
        xg = sb("xg", [NT, GS, D])
        xT = sb("xT", [65, GT])
        qkT = sb("qkT", [128, 8, GT])
        v = sb("v", [NT, GS, NL])
        fold = sb("fold", [NT, GS, WIDTH])
        work = sb("work", [NT, GS, WIDTH])
        low = sb("low", [NT, GS, WIDTH])
        probs = sb("probs", [NT, GS, WIDTH])
        probsT = sb("probsT", [NT, 2, WIDTH])
        negmax = sb("negmax", [NT, GS, NH])
        sums = sb("sums", [NT, GS, NH])
        oT = sb("oT", [128, GS, 4, NT])
        bAB = ps("bAB", [128, 2, 512])
        bS = ps("bS", [128, 2, 2, 512])
        bP = ps("bP", [128, 2, 512])
        loaded, set_up = sem("loaded"), sem("set_up")
        xg_ready, x_transposed, xT_ready, qk_made, qk_taken, v_made, v_taken = (
            sem(n) for n in ("xg_ready", "x_transposed", "xT_ready", "qk_made", "qk_taken", "v_made", "v_taken"))
        scores_made, folded, filtered, exp_done, normed, falloff_ready, phase_ready, waves_ready, damped = (
            sem(n) for n in ("scores_made", "folded", "filtered", "exp_done", "normed", "falloff_ready",
                             "phase_ready", "waves_ready", "damped"))
        pT_made, pT_taken, o_made, o_taken, y_made, y_taken, own, own_act = (
            sem(n) for n in ("pT_made", "pT_taken", "o_made", "o_taken", "y_made", "y_taken", "own", "act_own"))
        sem.start()
        block = ctx.enter_context(nc.Block())
        NQK = 8
        FIRST = 0
        OWN, OWN_ACT = 10 * GS, GS

        @block.sync
        def _(sp):
            sp.dma_start(wqkv[:, :], aps[f"{name}_wqkv"]).then_inc(loaded, 16)
            sp.dma_start(wo[:, :, :], aps[f"{name}_wo"].rearrange("(j p) n -> p j n", p=128)).then_inc(loaded, 16)
            sp.dma_start(bo[:, :], aps[f"{name}_bo"]).then_inc(loaded, 16)

        @block.gpsimd
        def _(pool):
            nc.gpsimd.memset(xT[D:D + 1, :], 1.0).then_inc(set_up, 1)
            nc.gpsimd.memset(ones[:, :], 1.0).then_inc(set_up, 1)
            pool.wait_ge(set_up, START + 2)
            nc.gpsimd.memset(halfpi[:, :], math.pi / 2).then_inc(set_up, 1)
            pool.wait_ge(set_up, START + 3)
            with pool.Fori(0, NG) as g:
                pool.wait_ge(x_transposed, START + g)
                nc.gpsimd.tensor_copy(xg[:, :, :], core.xn[:, bass.ds(g * GS, GS), :]).then_inc(xg_ready, 1)

        @block.tensor
        def _(pe):
            pe.wait_ge(loaded, 48)
            pe.wait_ge(set_up, START + 3)

            def queries_and_keys(g):
                pe.wait_ge(xg_ready, START + g + 1)
                transpose_each(core, bAB[:, 0, :], xg, D).then_inc(x_transposed, 1)
                pe.wait_ge(xT_ready, START + g + 1)
                for n in range(NQK):
                    if n >= 2:
                        pe.wait_ge(qk_taken, START + NQK * g + n - 1)
                    nc.tensor.matmul(bAB[:, n % 2, 0:GT], wqkv[:, n * 128:(n + 1) * 128], xT[:, :],
                                     start=True, stop=True).then_inc(qk_made, 1)

            def scores(g, s):
                if g is not FIRST or s:
                    pe.wait_ge(filtered, START + GS * g + s - 1)
                for j in range(4):
                    for half in range(2):
                        rows = slice(half * HD, (half + 1) * HD)
                        mm = nc.tensor.matmul(bS[0:NT, s % 2, half, j * NT:(j + 1) * NT],
                                              qkT[rows, j, s * NT:(s + 1) * NT],
                                              qkT[rows, 4 + j, s * NT:(s + 1) * NT], start=True, stop=True)
                mm.then_inc(scores_made, 1)

            def first_scores(g):
                pe.wait_ge(qk_taken, START + NQK * (g + 1))
                scores(g, 0)
                scores(g, 1)

            def turn_of(g, more):
                scores(g, 2)
                scores(g, 3)
                pe.wait_ge(y_taken, START + g)
                for s in range(GS):
                    if s >= 2:
                        pe.wait_ge(v_taken, START + GS * g + s - 1)
                    nc.tensor.matmul(bAB[0:NT, s % 2, :], xT[:, s * NT:(s + 1) * NT], wqkv[:, 2 * NL:3 * NL],
                                     start=True, stop=True).then_inc(v_made, 1)

                pe.wait_ge(v_taken, START + GS * (g + 1))
                if more:
                    queries_and_keys(g + 1)
                    first_scores(g + 1)

                def turn(s):
                    pe.wait_ge(damped, START + GS * g + s + 1)
                    pe.wait_ge(pT_taken, START + GS * g + s)
                    for n in range(NH):
                        mm = nc.tensor.transpose(bP[0:NT, n // 4, (n % 4) * NT:(n % 4 + 1) * NT],
                                                 probs[:, s, n * NT:(n + 1) * NT], core.ident[0:NT, 0:NT])
                    mm.then_inc(pT_made, 1)

                def weigh(s):
                    pe.wait_ge(pT_taken, START + GS * g + s + 1)
                    pe.wait_ge(o_taken, START + GS * g + s)
                    for j in range(4):
                        for half in range(2):
                            h = 2 * j + half
                            mm = nc.tensor.matmul(bAB[half * HD:(half + 1) * HD, 1, j * NT:(j + 1) * NT],
                                                  v[:, s, h * HD:(h + 1) * HD],
                                                  probsT[:, s % 2, (half * 4 + j) * NT:(half * 4 + j + 1) * NT],
                                                  start=True, stop=True)
                    mm.then_inc(o_made, 1)

                turn(0)
                for s in range(GS):
                    if s + 1 < GS:
                        turn(s + 1)
                    weigh(s)
                pe.wait_ge(o_taken, START + GS * (g + 1))
                for s in range(GS):
                    to = bAB[0:NT, 0, s * D:(s + 1) * D]
                    nc.tensor.matmul(to, ones[:, :], bo[:, :], start=True, stop=False)
                    for j in range(4):
                        mm = nc.tensor.matmul(to, oT[:, s, j, :], wo[:, j, :], start=False, stop=(j == 3))
                mm.then_inc(y_made, 1)

            queries_and_keys(FIRST)
            first_scores(FIRST)
            with pe.Fori(0, NG - 1) as g:
                turn_of(g, True)
            turn_of(NG - 1, False)

        @block.scalar
        def _(act):
            act.wait_ge(set_up, START + 3)

            def take_x(g):
                act.wait_ge(x_transposed, START + g + 1)
                nc.scalar.copy(xT[0:D, :], bAB[0:D, 0, 0:GT]).then_inc(xT_ready, 1)

            def take_queries_and_keys(g, first, last):
                for n in range(first, last):
                    act.wait_ge(qk_made, START + NQK * g + n + 1)
                    nc.scalar.copy(qkT[:, n, :], bAB[:, n % 2, 0:GT]).then_inc(qk_taken, 1)

            def turn(g, more):
                own_done = InOrder(act, own_act, g * OWN_ACT)
                def magnitude(s):
                    act.wait_ge(scores_made, START + GS * g + s + 1)
                    for half in range(2):
                        ins = nc.scalar.activation(fold[:, s, half * GT:(half + 1) * GT], bS[0:NT, s % 2, half, 0:GT],
                                                   ACT.Abs, scale=1618.0 / 8 / 3)
                    ins.then_inc(folded, 1)

                def exponentials(s):
                    act.wait_ge(filtered, START + GS * g + s + 1)
                    for n in range(NH):
                        p = probs[:, s, n * NT:(n + 1) * NT]
                        ins = nc.scalar.activation(p, p, ACT.Exp, bias=negmax[:, s, n:n + 1],
                                                   accum_out=sums[:, s, n:n + 1])
                    ins.then_inc(exp_done, 1)

                magnitude(0)
                magnitude(1)
                for s in range(GS):
                    exponentials(s)
                    if s + 2 < GS:
                        magnitude(s + 2)
                for s in range(GS):
                    act.wait_ge(v_made, START + GS * g + s + 1)
                    nc.scalar.copy(v[:, s, :], bAB[0:NT, s % 2, :]).then_inc(v_taken, 1)
                if more:
                    take_x(g + 1)
                for s in range(GS):
                    act.wait_ge(normed, START + GS * g + s + 1)
                    nc.scalar.activation(fold[:, s, :], probs[:, s, :], ACT.Copy, scale=C1 / (2 * math.pi))
                    own_done(nc.scalar.activation(low[:, s, :], probs[:, s, :], ACT.Square))
                    nc.scalar.activation(low[:, s, :], low[:, s, :], ACT.Exp, scale=-1.0 / PHI).then_inc(falloff_ready, 1)
                    if more:
                        take_queries_and_keys(g + 1, 2 * s, 2 * s + 2)
                for s in range(GS):
                    act.wait_ge(phase_ready, START + GS * g + s + 1)
                    nc.scalar.activation(fold[:, s, :], fold[:, s, :], ACT.Sin, scale=TURN)
                    nc.scalar.activation(work[:, s, :], probs[:, s, :], ACT.Sin, bias=halfpi[:, :],
                                         scale=-C2).then_inc(waves_ready, 1)
                for s in range(GS):
                    act.wait_ge(pT_made, START + GS * g + s + 1)
                    for half in range(2):
                        ins = nc.scalar.copy(probsT[:, s % 2, half * GT:(half + 1) * GT], bP[0:NT, half, 0:GT])
                    ins.then_inc(pT_taken, 1)
                    act.wait_ge(o_made, START + GS * g + s + 1)
                    nc.scalar.copy(oT[:, s, :, :].rearrange("p j t -> p (j t)"), bAB[:, 1, 0:GT]).then_inc(o_taken, 1)

            take_x(0)
            take_queries_and_keys(0, 0, NQK)
            with act.Fori(0, NG - 1) as g:
                turn(g, True)
            turn(NG - 1, False)

        @block.vector
        def _(dve):
            def residual(g):
                dve.wait_ge(y_made, START + g + 1)
                hg = core.h[:, bass.ds(g * GS, GS), :]
                nc.vector.tensor_tensor(hg, hg, bAB[0:NT, 0, 0:GS * D].rearrange("p (s f) -> p s f", s=GS),
                                        ALU.add).then_inc(y_taken, 1)

            def turn(g):
                own_done = InOrder(dve, own, g * OWN)
                for s in range(GS):
                    if s == 2 and g is not FIRST:
                        residual(g - 1)
                    f, w, l, p = fold[:, s, :], work[:, s, :], low[:, s, :], probs[:, s, :]
                    dve.wait_ge(folded, START + GS * g + s + 1)
                    own_done(nc.vector.tensor_scalar(w, f, ROUND, ROUND, ALU.add, ALU.subtract))
                    own_done(nc.vector.tensor_tensor(f, f, w, ALU.subtract))
                    own_done(nc.vector.tensor_scalar(w, f, 0.0, None, ALU.is_ge))
                    own_done(nc.vector.scalar_tensor_tensor(out=w, in0=f, scalar=1.0 / 3, in1=w, op0=ALU.is_lt, op1=ALU.mult))
                    own_done(nc.vector.tensor_scalar(w, w, (1.0 / PHI - 1.0) / 8, 1.0 / 8, ALU.mult, ALU.add))
                    for half in range(2):
                        ins = nc.vector.tensor_tensor(probs[:, s, half * GT:(half + 1) * GT],
                                                      bS[0:NT, s % 2, half, 0:GT], work[:, s, half * GT:(half + 1) * GT],
                                                      ALU.mult)
                    own_done(ins)
                    nc.vector.tensor_reduce(negmax[:, s, :], p.rearrange("p (n m) -> p n m", n=NH), AX, ALU.max,
                                            negate=True).then_inc(filtered, 1)
                for s in range(GS):
                    dve.wait_ge(exp_done, START + GS * g + s + 1)
                    p3 = probs[:, s, :].rearrange("p (n m) -> p n m", n=NH)
                    own_done(nc.vector.reciprocal(sums[:, s, :], sums[:, s, :]))
                    nc.vector.tensor_tensor(p3, p3, bc(sums[:, s, :], NT, 2), ALU.mult).then_inc(normed, 1)
                for s in range(GS):
                    f, w = fold[:, s, :], work[:, s, :]
                    dve.wait_ge(falloff_ready, START + GS * g + s + 1)
                    own_done(nc.vector.tensor_scalar(w, f, ROUND, ROUND, ALU.add, ALU.subtract))
                    nc.vector.tensor_tensor(f, f, w, ALU.subtract).then_inc(phase_ready, 1)
                for s in range(GS):
                    f, w, l, p = fold[:, s, :], work[:, s, :], low[:, s, :], probs[:, s, :]
                    dve.wait_ge(waves_ready, START + GS * g + s + 1)
                    own_done(nc.vector.tensor_tensor(f, f, l, ALU.mult))
                    own_done(nc.vector.tensor_tensor(f, f, w, ALU.add))
                    nc.vector.tensor_tensor(p, p, f, ALU.mult).then_inc(damped, 1)
                assert own_done.n == OWN, own_done.n

            turn(FIRST)
            with dve.Fori(1, NG) as g:
                turn(g)
            residual(NG - 1)


def tree_experts(core, name):
    nc, aps = core.nc, core.aps
    LEVELS = 8
    SLOTS = 2 ** LEVELS
    WIDE = 8
    PAIRS = SLOTS // (2 * WIDE)
    RW = 2 * WIDE
    ROWS = LEVELS - 3
    with ExitStack() as ctx:
        sem = Semaphores(nc, ctx, name)
        sb = lambda n, shape: ctx.enter_context(nc.sbuf_tensor(f"{name}_{n}", shape, F32))
        ps = lambda n, shape: ctx.enter_context(nc.psum_tensor(f"{name}_{n}", shape, F32))
        w1 = sb("w1", [65, SLOTS])
        half_precision = lambda n, shape: ctx.enter_context(nc.sbuf_tensor(f"{name}_{n}", shape, BF16))
        w12 = half_precision("w12", [2 * D, SLOTS * D])
        w13 = half_precision("w13", [2 * D, SLOTS * D])
        b2 = sb("b2", [128, 2, D])
        xg = sb("xg", [NT, GS, 2, D])
        part11, part22, part31 = (half_precision(n, [2 * D, GT]) for n in ("part11", "part22", "part31"))
        x1T = sb("x1T", [65, GT])
        score = sb("score", [NT, GS, SLOTS])
        size = sb("size", [NT, GS, SLOTS])
        right = sb("right", [NT, GS, SLOTS])
        here = sb("here", [NT, GS, SLOTS])
        row_share = sb("row_share", [NT, GS, ROWS, RW])
        shareT = sb("shareT", [128, GS, 2, NT])
        rest = shareT[:, 0:GS // 2, :, :].rearrange("p s c t -> p (s c t)")
        chosen = sb("chosen", [128, GS, ROWS * RW, D])
        idle = sb("idle", [NT, 2, PAIRS])
        total = sb("total", [NT, GS, D])
        total_before = right[:, :, 0:D]
        bX = ps("bX", [128, 512])
        bL = ps("bL", [128, 2, 512])
        bY = ps("bY", [128, 2, 2, 512])
        bZ = ps("bZ", [128, 512])
        loaded, set_up = sem("loaded"), sem("set_up")
        landed = [sem("landed0"), sem("landed1")]
        part1_made, rest_made, part2_made, split = (
            sem(n) for n in ("part1_made", "rest_made", "part2_made", "split"))
        parts_ready = sem("parts_ready")
        xg_ready, x_transposed, xT_ready, scores_made, scores_taken, size_ready = (
            sem(n) for n in ("xg_ready", "x_transposed", "xT_ready", "scores_made", "scores_taken", "size_ready"))
        share_ready, share_transposed, shareT_ready, bias_made, bias_taken, y_made, y_taken, own = (
            sem(n) for n in ("share_ready", "share_transposed", "shareT_ready", "bias_made", "bias_taken",
                             "y_made", "y_taken", "own"))
        weighed, path_shared = sem("weighed"), sem("path_shared")
        sem.start()
        block = ctx.enter_context(nc.Block())
        OWN = 2 + 1 + 2 * (LEVELS - 1) + 1 + 2 * GS + 2
        NPIECE = 4
        PIECE = SLOTS * D // NPIECE
        piece = lambda t, n: t[:, n * PIECE:(n + 1) * PIECE]
        all_chosen = chosen[:, :, :, :].rearrange("p s k f -> p (s k f)")
        staged = lambda n: all_chosen[:, n % 2 * PIECE:(n % 2 + 1) * PIECE]

        def weigh_path(eng, s, first, last):
            rows = chosen[0:NT, s, first * RW:last * RW, :]
            return eng.tensor_tensor(rows, rows, bc(row_share[:, s, first:last, :].rearrange("p r k -> p (r k)"), D, 2),
                                     ALU.mult)

        HALF = PAIRS // 2

        def copies(s, pairs):
            return s // 2 * 2 * PAIRS + 2 * (pairs - 1) + s % 2 + 1

        @block.sync
        def _(sp):
            sp.dma_start(w1[:, :], aps[f"{name}_w1"]).then_inc(loaded, 16)
            sp.dma_start(b2[:, :, :], aps[f"{name}_b2"].rearrange("(c p) n -> p c n", p=128)).then_inc(loaded, 16)
            for n in range(NPIECE):
                if n >= 2:
                    sp.wait_ge(split, START + 2 * (n - 1))
                for half in range(2):
                    sp.dma_start(staged(n)[half * D:(half + 1) * D, :], piece(aps[f"{name}_w2"], n)).then_inc(landed[n % 2], 16)

        @block.gpsimd
        def _(pool):
            nc.gpsimd.memset(x1T[D:D + 1, :], 1.0).then_inc(set_up, 1)
            pool.wait_ge(set_up, START + 1)
            nc.gpsimd.memset(all_chosen[:, 2 * PIECE:], 0.0).then_inc(set_up, 1)
            pool.wait_ge(set_up, START + 2)
            nc.gpsimd.memset(here[:, :, 0:1], 0.0).then_inc(set_up, 1)
            nc.gpsimd.memset(here[:, :, 1:2], 1.0).then_inc(set_up, 1)
            pool.wait_ge(set_up, START + 4)

            def copy_x(g):
                for c in range(2):
                    ins = nc.gpsimd.tensor_copy(xg[:, :, c, :], core.xn[:, bass.ds(g * GS, GS), :])
                ins.then_inc(xg_ready, 1)

            def weigh(g, s):
                pool.wait_ge(y_taken, START + GS * PAIRS * g + copies(s, HALF))
                weigh_path(nc.gpsimd, s, 0, ROWS - 1).then_inc(weighed, 1)
                pool.wait_ge(weighed, START + GS * g + s + 1)
                rows = chosen[0:NT, s, 0:(ROWS - 1) * RW, :].rearrange("p (r k) f -> p r (k f)", k=RW)
                nc.gpsimd.tensor_tensor(rows[:, :, 0:WIDE * D], rows[:, :, 0:WIDE * D],
                                        rows[:, :, WIDE * D:RW * D], ALU.add).then_inc(path_shared, 1)

            def turn(g, more):
                weigh(g, 0)
                weigh(g, 1)
                if more:
                    pool.wait_ge(x_transposed, START + g + 1)
                    copy_x(g + 1)
                weigh(g, 2)
                weigh(g, 3)

            copy_x(0)
            with pool.Fori(0, NG - 1) as g:
                turn(g, True)
            turn(NG - 1, False)

        @block.tensor
        def _(pe):
            pe.wait_ge(loaded, 32)
            pe.wait_ge(set_up, START + 4)
            pe.wait_ge(split, START + 2 * NPIECE)
            with pe.Fori(0, NG) as g:
                pe.wait_ge(parts_ready, START + g)
                pe.wait_ge(xg_ready, START + g + 1)
                for s in range(GS):
                    mm = nc.tensor.transpose(bX[:, s * NT:(s + 1) * NT], xg[:, s, :, :].rearrange("p c f -> p (c f)"),
                                             core.ident[0:NT, 0:NT])
                mm.then_inc(x_transposed, 1)
                pe.wait_ge(xT_ready, START + g + 1)
                pe.wait_ge(shareT_ready, START + g)
                for s in range(GS):
                    mm = nc.tensor.matmul(bL[0:NT, s // 2, (s % 2) * SLOTS:(s % 2 + 1) * SLOTS],
                                          x1T[:, s * NT:(s + 1) * NT], w1[:, :], start=True, stop=True)
                mm.then_inc(scores_made, 1)
                def turn_shares():
                    pe.wait_ge(share_ready, START + g + 1)
                    for s in range(GS):
                        for c in range(2):
                            mm = nc.tensor.transpose(bL[:, s // 2, ((s % 2) * 2 + c) * NT:((s % 2) * 2 + c + 1) * NT],
                                                     size[:, s, c * 128:(c + 1) * 128], core.ident[0:NT, 0:NT])
                    mm.then_inc(share_transposed, 1)

                def biases():
                    pe.wait_ge(shareT_ready, START + g + 1)
                    pe.wait_ge(bias_taken, START + g)
                    for s in range(GS):
                        for c in range(2):
                            mm = nc.tensor.matmul(bZ[0:NT, s * D:(s + 1) * D], shareT[:, s, c, :], b2[:, c, :],
                                                  start=(c == 0), stop=(c == 1))
                    mm.then_inc(bias_made, 1)

                for n in range(GS * PAIRS):
                        if n == 4:
                            turn_shares()
                        if n == 8:
                            biases()
                        s = n // (2 * PAIRS) * 2 + n % 2
                        p = n // 2 % PAIRS
                        pe.wait_ge(y_taken, START + GS * PAIRS * g + max(n - 1, 0))
                        if n == 0:
                            pe.wait_ge(parts_ready, START + g + 1)
                        for half in range(2):
                            cols = slice((2 * p + half) * WIDE * D, (2 * p + half + 1) * WIDE * D)
                            for m, (x, w) in enumerate(((part31, w13), (part22, w12), (part11, w12))):
                                mm = nc.tensor.matmul(bY[0:NT, s % 2, half, :], x[:, s * NT:(s + 1) * NT], w[:, cols],
                                                      start=(m == 0), stop=(m == 2))
                        mm.then_inc(y_made, 1)

        @block.scalar
        def _(act):
            for n in range(NPIECE):
                act.wait_ge(landed[n % 2], 32 * (n // 2 + 1))
                nc.scalar.copy(piece(w13, n), staged(n)).then_inc(part1_made, 1)
                act.wait_ge(rest_made, START + n + 1)
                nc.scalar.copy(piece(w12, n), staged(n)).then_inc(part2_made, 1)
                act.wait_ge(part2_made, START + n + 1)
                nc.scalar.copy(piece(w12, n)[0:D, :], piece(w13, n)[0:D, :]).then_inc(split, 1)
            with act.Fori(0, NG) as g:
                act.wait_ge(x_transposed, START + g + 1)
                act.wait_ge(bias_made, START + g)
                nc.scalar.copy(part11[:, :], bX[:, 0:GT])
                nc.scalar.copy(part31[D:2 * D, :], bX[D:2 * D, 0:GT])
                nc.scalar.copy(x1T[0:D, :], bX[0:D, 0:GT]).then_inc(xT_ready, 1)
                act.wait_ge(scores_made, START + g + 1)
                act.wait_ge(share_ready, START + g)
                nc.scalar.copy(score[:, :, :].rearrange("p (b s) k -> p b (s k)", b=2), bL[0:NT, :, :]).then_inc(scores_taken, 1)
                act.wait_ge(scores_taken, START + g + 1)
                act.wait_ge(share_transposed, START + g)
                nc.scalar.activation(size[:, :, :], score[:, :, :], ACT.Abs).then_inc(size_ready, 1)
                act.wait_ge(size_ready, START + 2 * g + 1)
                nc.scalar.activation(size[:, :, :], size[:, :, :], ACT.Gelu).then_inc(size_ready, 1)
                act.wait_ge(share_transposed, START + g + 1)
                act.wait_ge(bias_made, START + g)
                for b in range(2):
                    ins = nc.scalar.copy(shareT[:, 2 * b:2 * b + 2, :, :].rearrange("p s c t -> p (s c t)"),
                                         bL[:, b, 0:4 * NT])
                ins.then_inc(shareT_ready, 1)

        @block.vector
        def _(dve):
            dve.wait_ge(set_up, START + 4)
            for n in range(NPIECE):
                dve.wait_ge(part1_made, START + n + 1)
                nc.vector.tensor_tensor(staged(n), staged(n), piece(w13, n), ALU.subtract).then_inc(rest_made, 1)
                dve.wait_ge(part2_made, START + n + 1)
                nc.vector.tensor_tensor(piece(w13, n)[D:2 * D, :], staged(n)[D:2 * D, :], piece(w12, n)[D:2 * D, :],
                                        ALU.subtract).then_inc(split, 1)
            with dve.Fori(0, NG) as g:
                own_done = InOrder(dve, own, g * OWN)
                dve.wait_ge(xT_ready, START + g + 1)
                own_done(nc.vector.tensor_tensor(rest, bX[:, 0:GT], part11[:, :], ALU.subtract))
                own_done(nc.vector.tensor_copy(part22[:, :], rest))
                nc.vector.tensor_tensor(part31[0:D, :], rest[0:D], part22[0:D, :], ALU.subtract).then_inc(parts_ready, 1)
                dve.wait_ge(scores_taken, START + g + 1)
                own_done(nc.vector.tensor_scalar(right[:, :, :], score[:, :, :], 0.0, None, ALU.is_gt))
                for l in range(LEVELS - 1):
                    a, b = 2 ** l, 2 ** (l + 1)
                    children = here[:, :, 2 * a:2 * b].rearrange("p s (k c) -> p s k c", c=2)
                    own_done(nc.vector.tensor_tensor(children[:, :, :, 1], here[:, :, a:b], right[:, :, a:b], ALU.mult))
                    own_done(nc.vector.tensor_tensor(children[:, :, :, 0], here[:, :, a:b], children[:, :, :, 1],
                                                     ALU.subtract))
                dve.wait_ge(size_ready, START + 2 * g + 2)
                dve.wait_ge(share_transposed, START + g)
                own_done(nc.vector.tensor_tensor(size[:, :, :], size[:, :, :], here[:, :, :], ALU.mult))
                ins = nc.vector.tensor_copy(row_share[:, :, 0, :], size[:, :, 0:RW])
                for r in range(1, ROWS):
                    a = 2 ** (r + 3)
                    for s in range(GS):
                        ins = nc.vector.tensor_reduce(row_share[:, s, r, :],
                                                      size[:, s, a:2 * a].rearrange("p (c k) -> p k c", k=RW),
                                                      AX, ALU.add)
                ins.then_inc(share_ready, 1)

                def sum_path(s):
                    dve.wait_ge(y_taken, START + GS * PAIRS * g + copies(s, PAIRS))
                    own_done(weigh_path(nc.vector, s, ROWS - 1, ROWS))
                    nc.vector.tensor_reduce(total[:, s, :], chosen[0:NT, s, (ROWS - 1) * RW:, :]
                                            .rearrange("p k f -> p f k"), AX, ALU.add)
                    dve.wait_ge(path_shared, START + GS * g + s + 1)
                    rows = chosen[0:NT, s, 0:(ROWS - 1) * RW, :].rearrange("p (r k) f -> p f r k", k=RW)
                    own_done(nc.vector.tensor_reduce(total_before[:, s, :], rows[:, :, :, 0:WIDE], XY, ALU.add))

                for s0 in range(0, GS, 2):
                    for p in range(PAIRS):
                        for s in (s0, s0 + 1):
                            n = (s0 * PAIRS) + 2 * p + s - s0
                            dve.wait_ge(y_made, START + GS * PAIRS * g + n + 1)
                            dve.wait_ge(y_taken, START + GS * PAIRS * g + max(n - 1, 0))
                            nc.vector.memset(idle[:, s % 2, p:p + 1], 0.0)
                            row = p.bit_length()
                            nc.vector.copy_predicated(
                                chosen[0:NT, s, row * RW:(row + 1) * RW, :],
                                bc(here[:, s, p * RW:(p + 1) * RW].bitcast(U32), D, 2),
                                bY[0:NT, s % 2, :, :].rearrange("p b (k f) -> p (b k) f", k=WIDE)).then_inc(y_taken, 1)
                        if p == 3 and s0:
                            sum_path(0)
                            sum_path(1)
                sum_path(2)
                sum_path(3)
                hg = core.h[:, bass.ds(g * GS, GS), :]
                own_done(nc.vector.tensor_tensor(total[:, :, :], total[:, :, :], total_before, ALU.add))
                own_done(nc.vector.tensor_tensor(total[:, :, :], total[:, :, :], hg, ALU.add))
                dve.wait_ge(bias_made, START + g + 1)
                nc.vector.tensor_tensor(hg, total[:, :, :], bZ[0:NT, 0:GS * D].rearrange("p (s f) -> p s f", s=GS),
                                        ALU.add).then_inc(bias_taken, 1)
                assert own_done.n == OWN, own_done.n


def phase_attention(core, name):
    nc, aps = core.nc, core.aps
    K = 32
    ROUND = 1.5 * 2.0 ** 23
    TURN = 6.283184
    HALF = TURN / 2
    with ExitStack() as ctx:
        sem = Semaphores(nc, ctx, name)
        sb = lambda n, shape: ctx.enter_context(nc.sbuf_tensor(f"{name}_{n}", shape, F32))
        ps = lambda n: ctx.enter_context(nc.psum_tensor(f"{name}_{n}", [128, 512], F32))
        wkq1 = sb("wkq1", [65, 2 * D])
        wv = sb("wv", [65, 2 * D])
        wg1 = sb("wg1", [65, 16])
        w2 = sb("w2", [2 * D, 2, 2 * K])
        b2 = sb("b2", [2 * K, 2])
        wg2 = sb("wg2", [17, 2])
        wo = sb("wo", [65, D])
        affine = sb("affine", [NT, 2, D])
        upto = sb("upto", [NT, NT])
        scale = sb("scale", [NT, 2])
        wave = sb("wave", [NT, 2, D])
        turns = sb("turns", [NT, 2, D])
        halfpi = sb("halfpi", [128, 1])
        xg = sb("xg", [NT, GS, D])
        xT = sb("xT", [65, GT])
        hid = sb("hid", [2 * D, GT])
        ph = sb("ph", [2 * K, 2, GT])
        feat = sb("feat", [2 * K, 2, GT])
        vv = sb("vv", [NT, GS, 2, D])
        gT = sb("gT", [17, GT])
        gate = sb("gate", [NT, GS, 2])
        gsum = sb("gsum", [NT, GS])
        turned = sb("turned", [NT, GS, 2, D])
        mix = sb("mix", [NT, GS, 2, D])
        causal = sb("causal", [NT, GS, NT])
        both = sb("both", [NT, GS, D])
        sq = sb("sq", [NT, GS, D])
        mean = sb("mean", [NT, GS])
        var = sb("var", [NT, GS])
        nT = sb("nT", [65, GT])
        bX, bH, bV, bG, bK, bQ, bC, bR = (ps(n) for n in ("bX", "bH", "bV", "bG", "bK", "bQ", "bC", "bR"))
        loaded, set_up, phase_turned, wave_ready = (sem(n) for n in ("loaded", "set_up", "phase_turned", "wave_ready"))
        xg_ready, x_transposed, xT_ready, hid_made, hid_ready, v_made, v_taken, g1_made, g1_taken = (
            sem(n) for n in ("xg_ready", "x_transposed", "xT_ready", "hid_made", "hid_ready", "v_made", "v_taken",
                             "g1_made", "g1_taken"))
        g2_made, gate_centered, gate_exp, phases_made, feat_ready, a_made, a_taken, content_made = (
            sem(n) for n in ("g2_made", "gate_centered", "gate_exp", "phases_made", "feat_ready", "a_made", "a_taken",
                             "content_made"))
        turned_ready, run_made, centered, squared, summed, rooted, normed, n_transposed, nT_ready, y_made, y_taken = (
            sem(n) for n in ("turned_ready", "run_made", "centered", "squared", "summed", "rooted", "normed",
                             "n_transposed", "nT_ready", "y_made", "y_taken"))
        own, own_act = sem("own"), sem("act_own")
        sem.start()
        block = ctx.enter_context(nc.Block())
        OWN, OWN_ACT = 17, 2
        NLOAD = 11

        @block.sync
        def _(sp):
            for to, what in ((wkq1, "wkq1"), (wv, "wv"), (wg1, "wg1"), (w2, "w2"), (b2, "b2"), (wg2, "wg2"), (wo, "wo")):
                sp.dma_start(to[:], aps[f"{name}_{what}"]).then_inc(loaded, 16)
            sp.dma_start(affine[:, :, :], aps[f"{name}_affine"].partition_broadcast(NT)).then_inc(loaded, 16)
            sp.dma_start(upto[:, :], aps["upto"]).then_inc(loaded, 16)
            sp.dma_start(scale[:, :], aps["position_scale"]).then_inc(loaded, 16)
            sp.dma_start(turns[:, 1, :], aps[f"{name}_base_phases"]).then_inc(loaded, 16)

        @block.gpsimd
        def _(pool):
            for n, to in enumerate((xT[D:D + 1, :], nT[D:D + 1, :], gT[:, :])):
                nc.gpsimd.memset(to, 1.0).then_inc(set_up, 1)
                pool.wait_ge(set_up, START + n + 1)
            nc.gpsimd.memset(halfpi[:, :], math.pi / 2).then_inc(set_up, 1)
            pool.wait_ge(set_up, START + 4)
            with pool.Fori(0, NG) as g:
                pool.wait_ge(x_transposed, START + g)
                nc.gpsimd.tensor_copy(xg[:, :, :], core.xn[:, bass.ds(g * GS, GS), :]).then_inc(xg_ready, 1)

        @block.tensor
        def _(pe):
            pe.wait_ge(loaded, 16 * NLOAD)
            pe.wait_ge(set_up, START + 4)
            of = lambda s: slice(s * NT, (s + 1) * NT)
            with pe.Fori(0, NG) as g:
                pe.wait_ge(xg_ready, START + g + 1)
                transpose_each(core, bX, xg, D).then_inc(x_transposed, 1)
                pe.wait_ge(xT_ready, START + g + 1)
                nc.tensor.matmul(bH[:, 0:GT], wkq1[:, :], xT[:, :], start=True, stop=True).then_inc(hid_made, 1)
                for s in range(GS):
                    mm = nc.tensor.matmul(bV[0:NT, s * 2 * D:(s + 1) * 2 * D], xT[:, of(s)], wv[:, :], start=True, stop=True)
                mm.then_inc(v_made, 1)
                pe.wait_ge(gate_centered, START + g)
                nc.tensor.matmul(bG[0:16, 0:GT], wg1[:, :], xT[:, :], start=True, stop=True).then_inc(g1_made, 1)
                pe.wait_ge(hid_ready, START + g + 1)
                pe.wait_ge(a_taken, START + g)
                pe.wait_ge(nT_ready, START + g)
                nc.tensor.matmul(bK[0:2 * K, 0:GT], w2[:, 0, :], hid[:, :], start=True, stop=True)
                nc.tensor.matmul(bQ[0:2 * K, 0:GT], w2[:, 1, :], hid[:, :], start=True, stop=True).then_inc(phases_made, 1)
                pe.wait_ge(g1_taken, START + g + 1)
                for s in range(GS):
                    mm = nc.tensor.matmul(bG[0:NT, 2 * s:2 * s + 2], gT[:, of(s)], wg2[:, :], start=True, stop=True)
                mm.then_inc(g2_made, 1)
                pe.wait_ge(feat_ready, START + g + 1)
                for s in range(GS):
                    mm = nc.tensor.matmul(bK[0:NT, of(s)], feat[:, 0, of(s)], feat[:, 1, of(s)], start=True, stop=True)
                mm.then_inc(a_made, 1)
                pe.wait_ge(turned_ready, START + g + 1)
                nc.tensor.matmul(bR[0:NT, :], upto[:, :], turned[:, :, :, :].rearrange("p s c f -> p (s c f)"),
                                 start=True, stop=True).then_inc(run_made, 1)
                pe.wait_ge(a_taken, START + g + 1)
                pe.wait_ge(y_taken, START + g)
                for s in range(GS):
                    mm = nc.tensor.matmul(bC[0:NT, s * D:(s + 1) * D], causal[:, s, :], vv[:, s, 0, :], start=True, stop=True)
                mm.then_inc(content_made, 1)
                pe.wait_ge(normed, START + g + 1)
                transpose_each(core, bQ, both, D).then_inc(n_transposed, 1)
                pe.wait_ge(nT_ready, START + g + 1)
                for s in range(GS):
                    mm = nc.tensor.matmul(bC[0:NT, s * D:(s + 1) * D], nT[:, of(s)], wo[:, :], start=True, stop=True)
                mm.then_inc(y_made, 1)

        @block.scalar
        def _(act):
            act.wait_ge(loaded, 16 * NLOAD)
            act.wait_ge(set_up, START + 4)
            act.wait_ge(phase_turned, START + 1)
            nc.scalar.activation(wave[:, 0, :], turns[:, 0, :], ACT.Sin, bias=halfpi[0:NT, :], scale=-TURN)
            nc.scalar.activation(wave[:, 1, :], turns[:, 1, :], ACT.Sin, scale=TURN).then_inc(wave_ready, 1)
            with act.Fori(0, NG) as g:
                own_done = InOrder(act, own_act, g * OWN_ACT)
                act.wait_ge(x_transposed, START + g + 1)
                nc.scalar.copy(xT[0:D, :], bX[0:D, 0:GT]).then_inc(xT_ready, 1)
                act.wait_ge(hid_made, START + g + 1)
                nc.scalar.activation(hid[:, :], bH[:, 0:GT], ACT.Tanh).then_inc(hid_ready, 1)
                act.wait_ge(v_made, START + g + 1)
                act.wait_ge(content_made, START + g)
                act.wait_ge(turned_ready, START + g)
                nc.scalar.copy(vv[:, :, :, :].rearrange("p s c f -> p (s c f)"), bV[0:NT, :]).then_inc(v_taken, 1)
                act.wait_ge(g1_made, START + g + 1)
                nc.scalar.activation(gT[0:16, :], bG[0:16, 0:GT], ACT.Relu).then_inc(g1_taken, 1)
                act.wait_ge(phases_made, START + g + 1)
                nc.scalar.activation(ph[:, 0, :], bK[0:2 * K, 0:GT], ACT.Tanh, bias=b2[:, 0:1])
                own_done(nc.scalar.activation(ph[:, 1, :], bQ[0:2 * K, 0:GT], ACT.Tanh, bias=b2[:, 1:2]))
                own_done(nc.scalar.activation(ph[0:K, :, :], ph[0:K, :, :], ACT.Abs))
                nc.scalar.activation(feat[0:K, :, :], ph[0:K, :, :], ACT.Sin, bias=halfpi[0:K, :], scale=-HALF)
                nc.scalar.activation(feat[K:2 * K, :, :], ph[K:2 * K, :, :], ACT.Sin, scale=HALF).then_inc(feat_ready, 1)
                act.wait_ge(gate_centered, START + g + 1)
                nc.scalar.activation(gate[:, :, :], gate[:, :, :], ACT.Exp).then_inc(gate_exp, 1)
                act.wait_ge(centered, START + g + 1)
                nc.scalar.activation(sq[:, :, :], both[:, :, :], ACT.Square).then_inc(squared, 1)
                act.wait_ge(summed, START + g + 1)
                nc.scalar.activation(var[:, :], var[:, :], ACT.Sqrt, bias=core.eps[0:NT, 0:1], scale=1.0 / D).then_inc(rooted, 1)
                act.wait_ge(n_transposed, START + g + 1)
                nc.scalar.copy(nT[0:D, :], bQ[0:D, 0:GT]).then_inc(nT_ready, 1)

        @block.vector
        def _(dve):
            dve.wait_ge(loaded, 16 * NLOAD)
            first = InOrder(dve, own)
            first(nc.vector.tensor_scalar(turns[:, 1, :], turns[:, 1, :], 1 / (2 * math.pi), None, ALU.mult))
            first(nc.vector.tensor_scalar(turns[:, 0, :], turns[:, 1, :], ROUND, ROUND, ALU.add, ALU.subtract))
            first(nc.vector.tensor_tensor(turns[:, 1, :], turns[:, 1, :], turns[:, 0, :], ALU.subtract))
            first(nc.vector.tensor_scalar(turns[:, 0, :], turns[:, 1, :], -1.0, None, ALU.mult))
            nc.vector.tensor_tensor(turns[:, 0, :], turns[:, 0, :], turns[:, 1, :], ALU.max).then_inc(phase_turned, 1)
            dve.wait_ge(wave_ready, START + 1)
            with dve.Fori(0, NG) as g:
                own_done = InOrder(dve, own, g * OWN + 4)
                dve.wait_ge(v_taken, START + g + 1)
                dve.wait_ge(run_made, START + g)
                for c in range(2):
                    ins = nc.vector.tensor_tensor(turned[:, :, c, :], vv[:, :, 1, :], bc(wave[:, c, :], GS, 1), ALU.mult)
                ins.then_inc(turned_ready, 1)
                dve.wait_ge(g2_made, START + g + 1)
                own_done(nc.vector.tensor_copy(gate[:, :, :], bG[0:NT, 0:2 * GS].rearrange("p (s c) -> p s c", c=2)))
                own_done(nc.vector.tensor_tensor(gsum[:, :], gate[:, :, 0], gate[:, :, 1], ALU.max))
                nc.vector.tensor_tensor(gate[:, :, :], gate[:, :, :], bc(gsum[:, :], 2, 2), ALU.subtract).then_inc(gate_centered, 1)
                dve.wait_ge(a_made, START + g + 1)
                dve.wait_ge(content_made, START + g)
                nc.vector.tensor_tensor(causal[:, :, :], bK[0:NT, 0:GT].rearrange("p (s t) -> p s t", s=GS),
                                        bc(upto[:, :], GS, 1), ALU.mult).then_inc(a_taken, 1)
                dve.wait_ge(gate_exp, START + g + 1)
                own_done(nc.vector.tensor_tensor(gsum[:, :], gate[:, :, 0], gate[:, :, 1], ALU.add))
                own_done(nc.vector.reciprocal(gsum[:, :], gsum[:, :]))
                own_done(nc.vector.tensor_tensor(gate[:, :, :], gate[:, :, :], bc(gsum[:, :], 2, 2), ALU.mult))
                own_done(nc.vector.tensor_tensor(gate[:, :, :], gate[:, :, :], bc(scale[:, :], GS, 1), ALU.mult))
                dve.wait_ge(run_made, START + g + 1)
                own_done(nc.vector.tensor_tensor(mix[:, :, :, :].rearrange("p s c f -> p s (c f)"),
                                                 bR[0:NT, :].rearrange("p (s x) -> p s x", s=GS),
                                                 bc(wave[:, :, :].rearrange("p c f -> p (c f)"), GS, 1), ALU.mult))
                own_done(nc.vector.tensor_tensor(both[:, :, :], mix[:, :, 0, :], mix[:, :, 1, :], ALU.add))
                own_done(nc.vector.tensor_tensor(both[:, :, :], both[:, :, :], bc(gate[:, :, 0], D, 2), ALU.mult))
                dve.wait_ge(content_made, START + g + 1)
                own_done(nc.vector.tensor_tensor(mix[:, :, 0, :], bC[0:NT, 0:GS * D].rearrange("p (s f) -> p s f", s=GS),
                                                 bc(gate[:, :, 1], D, 2), ALU.mult))
                own_done(nc.vector.tensor_tensor(both[:, :, :], both[:, :, :], mix[:, :, 0, :], ALU.add))
                own_done(nc.vector.tensor_reduce(mean[:, :], both[:, :, :], AX, ALU.add))
                own_done(nc.vector.tensor_scalar(mean[:, :], mean[:, :], 1.0 / D, None, ALU.mult))
                nc.vector.tensor_tensor(both[:, :, :], both[:, :, :], bc(mean[:, :], D, 2), ALU.subtract).then_inc(centered, 1)
                dve.wait_ge(squared, START + g + 1)
                nc.vector.tensor_reduce(var[:, :], sq[:, :, :], AX, ALU.add).then_inc(summed, 1)
                dve.wait_ge(rooted, START + g + 1)
                own_done(nc.vector.reciprocal(var[:, :], var[:, :]))
                own_done(nc.vector.tensor_tensor(both[:, :, :], both[:, :, :], bc(var[:, :], D, 2), ALU.mult))
                own_done(nc.vector.tensor_tensor(both[:, :, :], both[:, :, :], bc(affine[:, 0, :], GS, 1), ALU.mult))
                nc.vector.tensor_tensor(both[:, :, :], both[:, :, :], bc(affine[:, 1, :], GS, 1), ALU.add).then_inc(normed, 1)
                hg = core.h[:, bass.ds(g * GS, GS), :]
                own_done(nc.vector.tensor_tensor(hg, hg, core.xn[:, bass.ds(g * GS, GS), :], ALU.add))
                dve.wait_ge(y_made, START + g + 1)
                nc.vector.tensor_tensor(hg, hg, bC[0:NT, 0:GS * D].rearrange("p (s f) -> p s f", s=GS),
                                        ALU.add).then_inc(y_taken, 1)
                assert own_done.n == OWN, own_done.n


def expert_heads(core, name):
    nc, aps = core.nc, core.aps
    NH, NE, HD = 4, 4, 16
    NEG = -3.0e38
    with ExitStack() as ctx:
        sem = Semaphores(nc, ctx, name)
        sb = lambda n, shape: ctx.enter_context(nc.sbuf_tensor(f"{name}_{n}", shape, F32))
        ps = lambda n, shape: ctx.enter_context(nc.psum_tensor(f"{name}_{n}", shape, F32))
        whl = sb("whl", [65, D])
        wqk = sb("wqk", [D, NE + 1, D])
        wv = sb("wv", [D, D])
        wgate = sb("wgate", [128, 2, NH * NE])
        bgate = sb("bgate", [NT, NH * NE])
        wfc1 = sb("wfc1", [65, D])
        wfc2 = sb("wfc2", [65, D])
        wfg = sb("wfg", [D, NH])
        affine = sb("affine", [NT, 4, HD])
        headmask = sb("headmask", [D, NH])
        future = sb("future", [NT, NT])
        resid = sb("resid", [NT, NH, HD])
        xg = sb("xg", [NT, GS, D])
        xT = sb("xT", [65, GT])
        sT = sb("sT", [D, GT])
        qkT = sb("qkT", [D, NE + 1, GT])
        kmask = sb("kmask", [D, GS, NH, NT])
        v = sb("v", [NT, GS, NH, 32])
        present = sb("present", [NT, GS, D])
        probs = sb("probs", [NT, 2, 2, NH, NT])
        probsT = sb("probsT", [NT, 2, NH, NE, NT])
        negmax = sb("negmax", [NT, 2, 2 * NH])
        sums = sb("sums", [NT, GS, NE, NH])
        oT = sb("oT", [128, NE, NT])
        outs = sb("outs", [NT, GS, NH, NE, HD])
        outsT = sb("outsT", [128, GS, 2, NT])
        gate = sb("gate", [NT, GS * NH, NE])
        fold = sb("fold", [NT, GS * NH])
        mixed = sb("mixed", [NT, GS, NH * HD])
        fx = sb("fx", [NT, GS, D])
        kept = sb("kept", [NT, GS, D])
        fT = sb("fT", [65, GT])
        keptT = sb("keptT", [D, GT])
        hT = sb("hT", [65, GT])
        sq = sb("sq", [NT, GS, D])
        var = sb("var", [NT, GS * NH])
        headgate = sb("headgate", [NT, GS, NH])
        headsum = sb("headsum", [NT, GS])
        bAB = ps("bAB", [128, 2, 512])
        bS = ps("bS", [128, 2, 2, 512])
        bP = ps("bP", [128, 2, 512])
        bA, bB = bAB[:, 0, :], bAB[:, 1, :]

        loaded, set_up, own, own_act = sem("loaded"), sem("set_up"), sem("own"), sem("act_own")
        pre_x, pre_xT, pre_s, pre_taken = (sem(n) for n in ("pre_x", "pre_xT", "pre_s", "pre_taken"))
        xg_ready, x_transposed, xT_ready, proj_made, proj_taken, sx_made, sx_taken, kmask_ready = (
            sem(n) for n in ("xg_ready", "x_transposed", "xT_ready", "proj_made", "proj_taken", "sx_made",
                             "sx_taken", "kmask_ready"))
        scores_made, masked, exp_done, pT_made, pT_taken, o_made, o_taken, o_turned, outs_ready = (
            sem(n) for n in ("scores_made", "masked", "exp_done", "pT_made", "pT_taken", "o_made", "o_taken",
                             "o_turned", "outs_ready"))
        outs_turned, outsT_ready, gate_made, gate_centered, gate_exp, f_ready, f_turned, fT_ready = (
            sem(n) for n in ("outs_turned", "outsT_ready", "gate_made", "gate_centered", "gate_exp", "f_ready",
                             "f_turned", "fT_ready"))
        fc1_made, h_ready, fc2_made, fout_ready, fout_turned, foutT_ready, hg_made, hg_centered, hg_exp = (
            sem(n) for n in ("fc1_made", "h_ready", "fc2_made", "fout_ready", "fout_turned", "foutT_ready",
                             "hg_made", "hg_centered", "hg_exp"))
        norm_sems = [[sem(f"{w}{n}") for w in ("centered", "squared", "summed", "rooted")] for n in range(2)]
        done = sem("done")
        sem.start()
        block = ctx.enter_context(nc.Block())
        NLOAD = 11
        PAIRS = (0, 2, 3)
        NPROJ = len(PAIRS) + 2
        NU = 2 * GS
        OWN, OWN_ACT = 43, 2
        of = lambda s: slice(s * NT, (s + 1) * NT)

        @block.sync
        def _(sp):
            for to, what in ((whl, "whl"), (wqk, "wqk"), (wv, "wv"), (wgate, "wgate"), (wfc1, "wfc1"), (wfc2, "wfc2"),
                             (wfg, "wfg")):
                sp.dma_start(to[:], aps[f"{name}_{what}"]).then_inc(loaded, 16)
            sp.dma_start(bgate[:, :], aps[f"{name}_bgate"].partition_broadcast(NT)).then_inc(loaded, 16)
            sp.dma_start(affine[:, :, :], aps[f"{name}_affine"].partition_broadcast(NT)).then_inc(loaded, 16)
            sp.dma_start(headmask[:, :], aps["headmask4"]).then_inc(loaded, 16)
            sp.dma_start(future[:, :], aps["future"]).then_inc(loaded, 16)

        @block.gpsimd
        def _(pool):
            for n, (to, value) in enumerate(((xT[D:D + 1, :], 1.0), (fT[D:D + 1, :], 1.0), (hT[D:D + 1, :], 1.0),
                                             (v[:, :, :, :], 0.0))):
                nc.gpsimd.memset(to, value).then_inc(set_up, 1)
                pool.wait_ge(set_up, START + n + 1)
            with pool.Fori(0, NG) as g:
                pool.wait_ge(x_transposed, START + g)
                nc.gpsimd.tensor_copy(xg[:, :, :], core.xn[:, bass.ds(g * GS, GS), :]).then_inc(xg_ready, 1)

        @block.tensor
        def _(pe):
            pe.wait_ge(loaded, 16 * NLOAD)
            pe.wait_ge(set_up, START + 4)
            for s in range(GS):
                mm = nc.tensor.transpose(bA[0:D, of(s)], core.xn[:, s, :], core.ident[0:NT, 0:NT])
            mm.then_inc(pre_x, 1)
            pe.wait_ge(pre_xT, START + 1)
            for s in range(GS):
                mm = nc.tensor.matmul(bB[0:NT, s * D:(s + 1) * D], xT[:, of(s)], whl[:, :], start=True, stop=True)
            mm.then_inc(pre_s, 1)
            pe.wait_ge(pre_taken, START + 1)
            with pe.Fori(0, NG) as g:
                pe.wait_ge(done, START + g)
                pe.wait_ge(xg_ready, START + g + 1)
                transpose_each(core, bA, xg, D).then_inc(x_transposed, 1)
                pe.wait_ge(xT_ready, START + g + 1)
                for n in range(NPROJ):
                    bank = bAB[:, n % 2, :]
                    if n == 1:
                        pe.wait_ge(proj_taken, START + NPROJ * g + 1)
                    elif n > 1:
                        pe.wait_ge(proj_taken, START + NPROJ * g + n - 1)
                    if n == 0:
                        mm = nc.tensor.matmul(bank[0:D, 0:GT], whl[:, :], xT[:, :], start=True, stop=True)
                    elif n <= len(PAIRS):
                        first = PAIRS[n - 1]
                        mm = nc.tensor.matmul(bank[:, 0:GT], wqk[:, first:first + 2, :].rearrange("p e f -> p (e f)"),
                                              sT[:, :], start=True, stop=True)
                    else:
                        for s in range(GS):
                            mm = nc.tensor.matmul(bank[0:NT, s * D:(s + 1) * D], sT[:, of(s)], wv[:, :], start=True, stop=True)
                    mm.then_inc(proj_made, 1)
                pe.wait_ge(proj_taken, START + NPROJ * g + NPROJ - 1)
                for s in range(GS):
                    mm = nc.tensor.matmul(bB[0:NT, s * D:(s + 1) * D], xT[:, of(s)], whl[:, :], start=True, stop=True)
                mm.then_inc(sx_made, 1)

                def scores(u):
                    s, pair = u // 2, u % 2
                    pe.wait_ge(kmask_ready, START + GS * g + s + 1)
                    pe.wait_ge(masked, START + NU * g + max(u - 1, 0))
                    for e in range(2):
                        mm = nc.tensor.matmul(bS[0:NT, u % 2, e, 0:GT], qkT[:, 2 * pair + e, of(s)],
                                              kmask[:, s, :, :].rearrange("p n t -> p (n t)"), start=True, stop=True)
                    mm.then_inc(scores_made, 1)

                def turn(u):
                    pe.wait_ge(exp_done, START + NU * g + u + 1)
                    pe.wait_ge(pT_taken, START + NU * g + u)
                    for n in range(NH):
                        for e in range(2):
                            mm = nc.tensor.transpose(bP[0:NT, n // 2, of(n % 2 * 2 + e)], probs[:, u % 2, e, n, :],
                                                     core.ident[0:NT, 0:NT])
                    mm.then_inc(pT_made, 1)

                def weigh(s):
                    pe.wait_ge(pT_taken, START + NU * g + 2 * s + 2)
                    pe.wait_ge(proj_taken, START + NPROJ * (g + 1))
                    for n in range(NH):
                        mm = nc.tensor.matmul(bA[32 * n:32 * n + 32, 0:GT], v[:, s, n, :],
                                              probsT[:, s % 2, n, :, :].rearrange("p e t -> p (e t)"),
                                              start=True, stop=True, tile_position=(0, 32 * n))
                    mm.then_inc(o_made, 1)
                    pe.wait_ge(o_taken, START + GS * g + s + 1)
                    pe.wait_ge(sx_taken, START + g + 1)
                    pe.wait_ge(outs_ready, START + GS * g + s)
                    for e in range(NE):
                        mm = nc.tensor.transpose(bB[0:NT, e * 128:(e + 1) * 128], oT[:, e, :], core.ident[:, :])
                    mm.then_inc(o_turned, 1)

                scores(0)
                for u in range(NU):
                    if u + 1 < NU:
                        scores(u + 1)
                    turn(u)
                    if u % 2 == 0 and u:
                        weigh(u // 2 - 1)
                weigh(GS - 1)
                pe.wait_ge(outs_ready, START + GS * (g + 1))
                for s in range(GS):
                    for c in range(2):
                        mm = nc.tensor.transpose(bAB[:, s // 2, of(s % 2 * 2 + c)],
                                                 outs[:, s, 2 * c:2 * c + 2, :, :].rearrange("p n e f -> p (n e f)"),
                                                 core.ident[0:NT, 0:NT])
                mm.then_inc(outs_turned, 1)
                pe.wait_ge(outsT_ready, START + g + 1)
                for s in range(GS):
                    for c in range(2):
                        mm = nc.tensor.matmul(bA[0:NT, s * 16:(s + 1) * 16], outsT[:, s, c, :], wgate[:, c, :],
                                              start=(c == 0), stop=(c == 1))
                mm.then_inc(gate_made, 1)
                pe.wait_ge(f_ready, START + g + 1)
                transpose_each(core, bB, fx, D).then_inc(f_turned, 1)
                pe.wait_ge(fT_ready, START + g + 1)
                nc.tensor.matmul(bA[0:D, 0:GT], wfc1[:, :], fT[:, :], start=True, stop=True).then_inc(fc1_made, 1)
                pe.wait_ge(h_ready, START + g + 1)
                for s in range(GS):
                    mm = nc.tensor.matmul(bB[0:NT, s * D:(s + 1) * D], hT[:, of(s)], wfc2[:, :], start=True, stop=True)
                mm.then_inc(fc2_made, 1)
                pe.wait_ge(fout_ready, START + g + 1)
                transpose_each(core, bA, fx, D).then_inc(fout_turned, 1)
                pe.wait_ge(foutT_ready, START + g + 1)
                for s in range(GS):
                    mm = nc.tensor.matmul(bB[0:NT, s * NH:(s + 1) * NH], fT[0:D, of(s)], wfg[:, :], start=True, stop=True)
                mm.then_inc(hg_made, 1)

        @block.scalar
        def _(act):
            act.wait_ge(loaded, 16 * NLOAD)
            act.wait_ge(set_up, START + 4)
            act.wait_ge(pre_x, START + 1)
            nc.scalar.copy(xT[0:D, :], bA[0:D, 0:GT]).then_inc(pre_xT, 1)
            with act.Fori(0, NG) as g:
                act.wait_ge(x_transposed, START + g + 1)
                nc.scalar.copy(xT[0:D, :], bA[0:D, 0:GT]).then_inc(xT_ready, 1)
                for n in range(NPROJ):
                    act.wait_ge(proj_made, START + NPROJ * g + n + 1)
                    bank = bAB[:, n % 2, :]
                    if n == 0:
                        ins = nc.scalar.copy(sT[:, :], bank[0:D, 0:GT])
                    elif n <= len(PAIRS):
                        for m in range(2):
                            e = PAIRS[n - 1] + m
                            if (e, n) != (3, 3):
                                ins = nc.scalar.activation(qkT[:, e, :], bank[m * D:(m + 1) * D, 0:GT], ACT.Copy,
                                                           scale=float(HD) ** 0.5 if e < NE else 1.0)
                    else:
                        ins = nc.scalar.copy(v[:, :, :, 0:HD].rearrange("p s n f -> p (s n) f"),
                                             bank[0:NT, 0:GS * D].rearrange("p (x f) -> p x f", f=HD))
                    ins.then_inc(proj_taken, 1)

                def exponentials(u):
                    s, pair = u // 2, u % 2
                    act.wait_ge(masked, START + NU * g + u + 1)
                    for e in range(2):
                        for n in range(NH):
                            p = probs[:, u % 2, e, n, :]
                            ins = nc.scalar.activation(p, p, ACT.Exp, bias=negmax[:, u % 2, e * NH + n:e * NH + n + 1],
                                                       accum_out=sums[:, s, 2 * pair + e, n:n + 1])
                    ins.then_inc(exp_done, 1)

                def take_context(s):
                    act.wait_ge(o_made, START + GS * g + s + 1)
                    act.wait_ge(o_turned, START + GS * g + s)
                    nc.scalar.copy(oT[:, :, :].rearrange("p e t -> p (e t)"), bA[:, 0:GT]).then_inc(o_taken, 1)

                for u in range(NU):
                    exponentials(u)
                    act.wait_ge(pT_made, START + NU * g + u + 1)
                    act.wait_ge(o_made, START + GS * g + max(u // 2 - 1, 0))
                    pair = u % 2
                    for b in range(2):
                        ins = nc.scalar.copy(probsT[:, u // 2 % 2, 2 * b:2 * b + 2, 2 * pair:2 * pair + 2, :]
                                             .rearrange("p n e t -> p n (e t)"),
                                             bP[0:NT, b, 0:GT].rearrange("p (n x) -> p n x", n=2))
                    ins.then_inc(pT_taken, 1)
                    if u % 2 == 0 and u:
                        take_context(u // 2 - 1)
                take_context(GS - 1)
                act.wait_ge(outs_turned, START + g + 1)
                for b in range(2):
                    ins = nc.scalar.copy(outsT[:, 2 * b:2 * b + 2, :, :].rearrange("p s c t -> p (s c t)"),
                                         bAB[:, b, 0:4 * NT])
                ins.then_inc(outsT_ready, 1)
                act.wait_ge(gate_centered, START + g + 1)
                nc.scalar.activation(gate[:, :, :], gate[:, :, :], ACT.Exp).then_inc(gate_exp, 1)

                def norm(n):
                    centered, squared, summed, rooted = norm_sems[n]
                    act.wait_ge(centered, START + g + 1)
                    nc.scalar.activation(sq[:, :, :], mixed[:, :, :], ACT.Square).then_inc(squared, 1)
                    act.wait_ge(summed, START + g + 1)
                    nc.scalar.activation(var[:, :], var[:, :], ACT.Sqrt, bias=core.eps[0:NT, 1:2],
                                         scale=1.0 / HD).then_inc(rooted, 1)

                norm(0)
                act.wait_ge(f_turned, START + g + 1)
                nc.scalar.copy(fT[0:D, :], bB[0:D, 0:GT]).then_inc(fT_ready, 1)
                norm(1)
                act.wait_ge(fout_turned, START + g + 1)
                nc.scalar.copy(fT[0:D, :], bA[0:D, 0:GT]).then_inc(foutT_ready, 1)
                act.wait_ge(hg_centered, START + g + 1)
                nc.scalar.activation(headgate[:, :, :], headgate[:, :, :], ACT.Exp).then_inc(hg_exp, 1)

        @block.vector
        def _(dve):
            dve.wait_ge(loaded, 16 * NLOAD)
            dve.wait_ge(pre_s, START + 1)
            for n in range(NH):
                ins = nc.vector.tensor_copy(resid[:, n, :], bB[0:NT, n * D + n * HD:n * D + (n + 1) * HD])
            ins.then_inc(pre_taken, 1)
            dve.wait_ge(pre_taken, START + 1)
            heads = lambda t: t.rearrange("p s (n f) -> p (s n) f", n=NH)
            with dve.Fori(0, NG) as g:
                own_done = InOrder(dve, own, g * OWN)
                dve.wait_ge(proj_taken, START + NPROJ * g + NPROJ - 1)
                for s in range(GS):
                    ins = nc.vector.tensor_tensor(kmask[:, s, :, :], bc(qkT[:, NE, of(s)], NH, 1),
                                                  bc(headmask[:, :], NT, 2), ALU.mult).then_inc(kmask_ready, 1)
                dve.wait_ge(sx_made, START + g + 1)
                nc.vector.tensor_scalar(present[:, :, :].rearrange("p s f -> p (s f)"), bB[0:NT, 0:GS * D], 0.0, None,
                                        ALU.not_equal).then_inc(sx_taken, 1)

                def mask(u):
                    dve.wait_ge(scores_made, START + NU * g + u + 1)
                    dve.wait_ge(pT_made, START + NU * g + max(u - 1, 0))
                    for e in range(2):
                        ins = nc.vector.tensor_tensor(probs[:, u % 2, e, :, :],
                                                      bS[0:NT, u % 2, e, 0:GT].rearrange("p (n t) -> p n t", n=NH),
                                                      bc(future[:, :], NH, 1), ALU.add)
                    own_done(ins)
                    nc.vector.tensor_reduce(negmax[:, u % 2, :], probs[:, u % 2, :, :, :].rearrange("p e n t -> p (e n) t"),
                                            AX, ALU.max, negate=True).then_inc(masked, 1)

                def contexts(s):
                    dve.wait_ge(o_turned, START + GS * g + s + 1)
                    own_done(nc.vector.reciprocal(sums[:, s, :, :], sums[:, s, :, :]))
                    for n in range(NH):
                        ins = nc.vector.tensor_tensor(
                            outs[:, s, n, :, :],
                            bB[0:NT, :].rearrange("p (e n f) -> p n e f", e=NE, n=NH)[:, n, :, 0:HD],
                            bc(sums[:, s, :, n], HD, 2), ALU.mult)
                    own_done(ins)
                    nc.vector.tensor_tensor(outs[:, s, :, :, :], outs[:, s, :, :, :],
                                            bc(present[:, s, :].rearrange("p (n f) -> p n f", n=NH), NE, 2),
                                            ALU.mult).then_inc(outs_ready, 1)

                mask(0)
                for u in range(NU):
                    if u + 1 < NU:
                        mask(u + 1)
                    if u % 2 == 0 and u:
                        contexts(u // 2 - 1)
                contexts(GS - 1)
                dve.wait_ge(gate_made, START + g + 1)
                own_done(nc.vector.tensor_tensor(gate[:, :, :].rearrange("p (s n) e -> p s (n e)", s=GS),
                                                 bA[0:NT, 0:GS * 16].rearrange("p (s x) -> p s x", s=GS),
                                                 bc(bgate[:, :], GS, 1), ALU.add))
                own_done(nc.vector.tensor_reduce(fold[:, :], gate[:, :, :], AX, ALU.max))
                nc.vector.tensor_tensor(gate[:, :, :], gate[:, :, :], bc(fold[:, :], NE, 2), ALU.subtract).then_inc(gate_centered, 1)
                dve.wait_ge(gate_exp, START + g + 1)
                own_done(nc.vector.tensor_reduce(fold[:, :], gate[:, :, :], AX, ALU.add))
                own_done(nc.vector.reciprocal(fold[:, :], fold[:, :]))
                own_done(nc.vector.tensor_tensor(gate[:, :, :], gate[:, :, :], bc(fold[:, :], NE, 2), ALU.mult))
                flat = outs[:, :, :, :, :].rearrange("p s n e f -> p (s n e) f")
                own_done(nc.vector.tensor_tensor(flat, flat, bc(gate[:, :, :].rearrange("p x e -> p (x e)"), HD, 2), ALU.mult))
                own_done(nc.vector.tensor_reduce(heads(mixed[:, :, :]), outs[:, :, :, :, :].rearrange("p s n e f -> p (s n) f e"),
                                                 AX, ALU.add))
                own_done(nc.vector.tensor_tensor(mixed[:, :, :], mixed[:, :, :],
                                                 bc(resid[:, :, :].rearrange("p n f -> p (n f)"), GS, 1), ALU.add))

                def norm(n, to, ready):
                    centered, squared, summed, rooted = norm_sems[n]
                    own_done(nc.vector.tensor_reduce(fold[:, :], heads(mixed[:, :, :]), AX, ALU.add))
                    own_done(nc.vector.tensor_scalar(fold[:, :], fold[:, :], 1.0 / HD, None, ALU.mult))
                    nc.vector.tensor_tensor(heads(mixed[:, :, :]), heads(mixed[:, :, :]), bc(fold[:, :], HD, 2),
                                            ALU.subtract).then_inc(centered, 1)
                    dve.wait_ge(squared, START + g + 1)
                    nc.vector.tensor_reduce(var[:, :], heads(sq[:, :, :]), AX, ALU.add).then_inc(summed, 1)
                    dve.wait_ge(rooted, START + g + 1)
                    own_done(nc.vector.reciprocal(var[:, :], var[:, :]))
                    own_done(nc.vector.tensor_tensor(heads(mixed[:, :, :]), heads(mixed[:, :, :]), bc(var[:, :], HD, 2), ALU.mult))
                    own_done(nc.vector.tensor_tensor(heads(mixed[:, :, :]), heads(mixed[:, :, :]),
                                                     bc(affine[:, 2 * n, :], GS * NH, 1), ALU.mult))
                    nc.vector.tensor_tensor(heads(to), heads(mixed[:, :, :]), bc(affine[:, 2 * n + 1, :], GS * NH, 1),
                                            ALU.add).then_inc(ready, 1)

                norm(0, fx[:, :, :], f_ready)
                dve.wait_ge(fT_ready, START + g + 1)
                nc.vector.tensor_scalar(kept[:, :, :], fx[:, :, :], 0.0, None, ALU.not_equal)
                own_done(nc.vector.tensor_scalar(keptT[:, :], fT[0:D, :], 0.0, None, ALU.not_equal))
                dve.wait_ge(fc1_made, START + g + 1)
                nc.vector.scalar_tensor_tensor(out=hT[0:D, :], in0=bA[0:D, 0:GT], scalar=0.0, in1=keptT[:, :],
                                               op0=ALU.max, op1=ALU.mult).then_inc(h_ready, 1)
                dve.wait_ge(fc2_made, START + g + 1)
                own_done(nc.vector.tensor_tensor(mixed[:, :, :], bB[0:NT, 0:GS * D].rearrange("p (s f) -> p s f", s=GS),
                                                 kept[:, :, :], ALU.mult))
                own_done(nc.vector.tensor_tensor(mixed[:, :, :], mixed[:, :, :], fx[:, :, :], ALU.add))
                norm(1, fx[:, :, :], fout_ready)
                dve.wait_ge(hg_made, START + g + 1)
                own_done(nc.vector.tensor_copy(headgate[:, :, :], bB[0:NT, 0:GS * NH].rearrange("p (s n) -> p s n", s=GS)))
                own_done(nc.vector.tensor_reduce(headsum[:, :], headgate[:, :, :], AX, ALU.max))
                nc.vector.tensor_tensor(headgate[:, :, :], headgate[:, :, :], bc(headsum[:, :], NH, 2),
                                        ALU.subtract).then_inc(hg_centered, 1)
                dve.wait_ge(hg_exp, START + g + 1)
                own_done(nc.vector.tensor_reduce(headsum[:, :], headgate[:, :, :], AX, ALU.add))
                own_done(nc.vector.reciprocal(headsum[:, :], headsum[:, :]))
                own_done(nc.vector.tensor_tensor(headgate[:, :, :], headgate[:, :, :], bc(headsum[:, :], NH, 2), ALU.mult))
                own_done(nc.vector.tensor_tensor(heads(fx[:, :, :]), heads(fx[:, :, :]),
                                                 bc(headgate[:, :, :].rearrange("p s n -> p (s n)"), HD, 2), ALU.mult))
                hg = core.h[:, bass.ds(g * GS, GS), :]
                nc.vector.tensor_tensor(hg, hg, fx[:, :, :], ALU.add).then_inc(done, 1)
                assert own_done.n == OWN, own_done.n


def window_encoder(core, name):
    nc, aps = core.nc, core.aps
    K, NH, HD, NI = 10, 4, 16, 34
    NF = NT + K - 1
    ON_POOL = (8, 9)
    CHUNKS = ((0, 4), (4, 8), (8, 10))
    NC = len(CHUNKS)
    BANK = 512 // D
    first_pair = lambda q: q * (q + 1) // 2
    PAIRS = first_pair(K)
    with ExitStack() as ctx:
        sem = Semaphores(nc, ctx, name)
        sb = lambda n, shape: ctx.enter_context(nc.sbuf_tensor(f"{name}_{n}", shape, F32))
        frames = sb("frames", [NI, NB, NF])
        xw = sb("xw", [NI, NF])
        win = sb("win", [NI, K, D])
        wqkv, wqkv2 = sb("wqkv", [65, 3 * D]), sb("wqkv2", [65, 3 * D])
        wo, w1, w2 = sb("wo", [65, D]), sb("w1", [D, 2, 128]), sb("w2", [128, 2, D])
        b1, b2 = sb("b1", [128, 2]), sb("b2", [NT, D])
        affine = sb("affine", [D, 3, 2])
        h0, hb = sb("h0", [NT, 2, K, D]), sb("hb", [NT, K, D])
        x1, x2, x3, sq = sb("x1", [NT, K, D]), sb("x2", [NT, K, D]), sb("x3", [NT, K, D]), sb("sq", [NT, 2, K, D])
        mean, var = sb("mean", [NT, 3, K]), sb("var", [NT, 3, K])
        xT, oT, x2T, x3T = (sb(n, [65, K * NT]) for n in ("xT", "oT", "x2T", "x3T"))
        qkv = sb("qkv", [NT, 2, K, 3 * D])
        kv2, q2 = sb("kv2", [NT, K, 2 * D]), sb("q2", [NT, D])
        prod = sb("prod", [NT, PAIRS * D])
        score, e = sb("score", [NT, K, NH, K]), sb("e", [NT, K, NH, K])
        maxima, sums = sb("maxima", [NT, K, NH]), sb("sums", [NT, K, NH])
        o = sb("o", [NT, K, D])
        prod2 = sb("prod2", [NT, K * D])
        score2, maxima2, sums2, o2 = sb("score2", [NT, NH, K]), sb("maxima2", [NT, NH]), sb("sums2", [NT, NH]), sb("o2", [NT, D])
        hidden = sb("hidden", [128, 2, 2, GT])
        ps = lambda n, shape: ctx.enter_context(nc.psum_tensor(f"{name}_{n}", shape, F32))
        bT, bQ, bH, bO = ps("bT", [128, 2, 512]), ps("bQ", [128, 2, 512]), ps("bH", [128, 2, 512]), ps("bO", [128, 2, 512])

        loaded, set_up = sem("loaded"), sem("set_up")
        xw_ready, h0_made, h0_ready, x1_ready, x1_turned, x1_taken, qkv_made, qkv_taken = (
            sem(n) for n in ("xw_ready", "h0_made", "h0_ready", "x1_ready", "x1_turned", "x1_taken", "qkv_made",
                             "qkv_taken"))
        pool_scores, centered, exp_done, pool_values, o_ready, o_turned, o_taken, wo_made, wo_taken = (
            sem(n) for n in ("pool_scores", "centered", "exp_done", "pool_values", "o_ready", "o_turned", "o_taken",
                             "wo_made", "wo_taken"))
        x2_ready, x2_turned, x2_taken, b2_added = (
            sem(n) for n in ("x2_ready", "x2_turned", "x2_taken", "b2_added"))
        hidden_made, hidden_ready, w2_made, w2_taken, x3_ready, x3_turned, x3_taken = (
            sem(n) for n in ("hidden_made", "hidden_ready", "w2_made", "w2_taken", "x3_ready", "x3_turned", "x3_taken"))
        kv_made, kv_taken, centered2, exp2_done = (
            sem(n) for n in ("kv_made", "kv_taken", "centered2", "exp2_done"))
        start_own, front_own, back_own, last_own = (
            sem(n) for n in ("start_own", "front_own", "back_own", "last_own"))
        norm_sems = [[sem(f"{w}{n}") for w in ("norm_centered", "norm_squared", "norm_summed", "norm_rooted")]
                     for n in range(3)]
        x2_centered, x3_centered = norm_sems[1][0], norm_sems[2][0]
        sem.start()
        block = ctx.enter_context(nc.Block())
        NLOAD = 10
        OWN_START, OWN_FRONT, OWN_BACK, OWN_LAST = 3, 9, 4, 6
        TURNS = NB // 2 - 2
        FIRST = 0
        units = lambda c: range(*CHUNKS[c])
        cols = lambda c: slice(CHUNKS[c][0] * NT, CHUNKS[c][1] * NT)
        of = lambda k: slice(k * NT, (k + 1) * NT)
        wide_of = lambda c: (CHUNKS[c][1] - CHUNKS[c][0]) * NT
        at = lambda k: bO[0:NT, k // BANK, k % BANK * D:(k % BANK + 1) * D]

        def query_products(eng, q, u):
            to = prod[:, first_pair(q) * D:first_pair(q + 1) * D].rearrange("p (k f) -> p k f", f=D)
            return eng.tensor_tensor(to, qkv[:, u, 0:q + 1, D:2 * D], bc(qkv[:, u, q, 0:D], q + 1, 1), ALU.mult)

        def value_products(eng, q, u):
            to = prod[:, first_pair(q) * D:first_pair(q + 1) * D].rearrange("p (h f k) -> p h f k", h=NH, f=HD)
            return eng.tensor_tensor(to, qkv[:, u, 0:q + 1, 2 * D:3 * D].rearrange("p k (h f) -> p h f k", h=NH),
                                     bc(e[:, q, :, 0:q + 1], HD, 2), ALU.mult)

        def sequence(t, b):
            return t[:, b, :] if isinstance(b, int) else t[:, bass.ds(b, 1), :].rearrange("p o f -> p (o f)")

        @block.sync
        def _(sp):
            for to, what in ((frames, "frames"), (win, "win"), (wqkv, "wqkv"), (wqkv2, "wqkv2"), (wo, "wo"), (w1, "w1"),
                             (w2, "w2"), (b1, "b1"), (affine, "affine")):
                sp.dma_start(to[:], aps[f"{name}_{what}"]).then_inc(loaded, 16)
            sp.dma_start(b2[:, :], aps[f"{name}_b2"].partition_broadcast(NT)).then_inc(loaded, 16)

        @block.gpsimd
        def _(pool):
            for n, (to, value) in enumerate(((xT[D:D + 1, :], 1.0), (oT[D:D + 1, :], 1.0), (x3T[D:D + 1, :], 1.0),
                                             (score[:, :, :, :], -3.0e38))):
                nc.gpsimd.memset(to, value).then_inc(set_up, 1)
                pool.wait_ge(set_up, START + n + 1)
            pool.wait_ge(loaded, 16 * NLOAD)

            def take_frames(f):
                if f is not FIRST:
                    pool.wait_ge(h0_made, START + f)
                nc.gpsimd.tensor_copy(xw[:, :], sequence(frames, f)).then_inc(xw_ready, 1)

            def front(f, u):
                pool.wait_ge(qkv_taken, START + 5 * f + 5)
                for q in ON_POOL:
                    ins = query_products(nc.gpsimd, q, u)
                ins.then_inc(pool_scores, 1)
                pool.wait_ge(exp_done, START + f + 1)
                for q in ON_POOL:
                    ins = value_products(nc.gpsimd, q, u)
                ins.then_inc(pool_values, 1)
                pool.wait_ge(x2_centered, START + f + 1)
                nc.gpsimd.tensor_tensor(hb[:, :, :], hb[:, :, :], bc(b2[:, :], K, 1), ALU.add).then_inc(b2_added, 1)

            take_frames(FIRST)
            take_frames(1)
            for f in range(2):
                take_frames(f + 2)
                front(f, f)
            with pool.Fori(0, TURNS) as i:
                for f, u in ((i * 2 + 2, 0), (i * 2 + 3, 1)):
                    take_frames(f + 2)
                    front(f, u)
            for u in range(2):
                front(NB - 2 + u, u)

        @block.tensor
        def _(pe):
            pe.wait_ge(loaded, 16 * NLOAD)
            pe.wait_ge(set_up, START + 4)

            def turn(src, c, signal):
                for k in units(c):
                    wide = src[:, k:k + 2, :].rearrange("p s f -> p (s f)") if k == CHUNKS[c][0] else src[:, k, :]
                    j = k - CHUNKS[c][0]
                    mm = nc.tensor.transpose(bT[0:wide.shape[1], c % 2, of(j)], wide, core.ident[0:NT, 0:NT])
                mm.then_inc(signal, 1)

            def embed(f):
                pe.wait_ge(xw_ready, START + f + 1)
                if f is not FIRST:
                    pe.wait_ge(wo_taken, START + f - 1)
                for k in range(K):
                    mm = nc.tensor.matmul(at(k), xw[:, k:k + NT], win[:, k, :], start=True, stop=True)
                mm.then_inc(h0_made, 1)

            def project(f):
                pe.wait_ge(x1_ready, START + f + 1)
                if f is not FIRST:
                    pe.wait_ge(x2_taken, START + NC * (f - 1))
                for c in range(NC):
                    if c == 2:
                        pe.wait_ge(x1_taken, START + NC * f + 1)
                    turn(x1, c, x1_turned)
                for j in range(K // 2):
                    pe.wait_ge(x1_taken, START + NC * f + 2 * j // 4 + 1)
                    if j >= 2:
                        pe.wait_ge(qkv_taken, START + 5 * f + j - 1)
                    for u in range(2):
                        mm = nc.tensor.matmul(bQ[0:NT, j % 2, u * 3 * D:(u + 1) * 3 * D], xT[:, of(2 * j + u)], wqkv[:, :],
                                              start=True, stop=True)
                    mm.then_inc(qkv_made, 1)

            def context_out(f):
                pe.wait_ge(o_ready, START + f + 1)
                for c in range(NC):
                    if c == 2:
                        pe.wait_ge(o_taken, START + NC * f + 1)
                    turn(o, c, o_turned)
                pe.wait_ge(w2_taken, START + f)
                for c in range(NC):
                    pe.wait_ge(o_taken, START + NC * f + c + 1)
                    for k in units(c):
                        mm = nc.tensor.matmul(at(k), oT[:, of(k)], wo[:, :], start=True, stop=True)
                mm.then_inc(wo_made, 1)

            def turn_x2(f):
                pe.wait_ge(x2_ready, START + f + 1)
                for c in range(NC):
                    if c == 2:
                        pe.wait_ge(x2_taken, START + NC * f + 1)
                    turn(x2, c, x2_turned)

            def mlp(b):
                def first(c):
                    pe.wait_ge(x2_taken, START + NC * b + c + 1)
                    for m in range(2):
                        if c:
                            pe.wait_ge(hidden_ready, START + 2 * NC * b + 2 * (c - 1) + m + 1)
                        nc.tensor.matmul(bH[:, m, 0:wide_of(c)], w1[:, m, :], x2T[0:D, cols(c)],
                                         start=True, stop=True).then_inc(hidden_made, 1)

                def second(c):
                    pe.wait_ge(hidden_ready, START + 2 * NC * b + 2 * c + 2)
                    for j, k in enumerate(units(c)):
                        for m in range(2):
                            mm = nc.tensor.matmul(at(k), hidden[:, c % 2, m, of(j)], w2[:, m, :],
                                                  start=(m == 0), stop=(m == 1))
                    mm.then_inc(w2_made, 1)

                first(0)
                for c in range(NC):
                    if c + 1 < NC:
                        first(c + 1)
                    second(c)

            def project_again(b):
                pe.wait_ge(x3_ready, START + b + 1)
                for c in range(NC):
                    if c == 2:
                        pe.wait_ge(x3_taken, START + NC * b + 1)
                    turn(x3, c, x3_turned)
                for c in range(NC):
                    pe.wait_ge(x3_taken, START + NC * b + c + 1)
                    if c == 2:
                        pe.wait_ge(kv_taken, START + NC * b + 1)
                    for j, k in enumerate(units(c)):
                        mm = nc.tensor.matmul(bQ[0:NT, c % 2, j * 2 * D:(j + 1) * 2 * D], x3T[:, of(k)], wqkv2[:, D:3 * D],
                                              start=True, stop=True)
                    if c == 2:
                        mm = nc.tensor.matmul(bQ[0:NT, 0, 4 * D:5 * D], x3T[:, of(K - 1)], wqkv2[:, 0:D],
                                              start=True, stop=True)
                    mm.then_inc(kv_made, 1)

            def turn_of(f, back=True, start=True, embedding=True):
                if start:
                    project(f + 1)
                if back:
                    mlp(f - 1)
                context_out(f)
                if embedding:
                    embed(f + 2)
                if back:
                    project_again(f - 1)
                turn_x2(f)

            embed(FIRST)
            project(FIRST)
            embed(1)
            turn_of(0, back=False)
            turn_of(1)
            with pe.Fori(0, TURNS) as i:
                for f in (i * 2 + 2, i * 2 + 3):
                    turn_of(f)
            turn_of(NB - 2, embedding=False)
            turn_of(NB - 1, start=False, embedding=False)
            mlp(NB - 1)
            project_again(NB - 1)

        @block.scalar
        def _(act):
            act.wait_ge(loaded, 16 * NLOAD)
            act.wait_ge(set_up, START + 4)

            def squares(n, x, i):
                was_centered, was_squared, _, _ = norm_sems[n]
                act.wait_ge(was_centered, START + i + 1)
                nc.scalar.activation(sq[:, n % 2, :, :], x[:, :, :], ACT.Square).then_inc(was_squared, 1)

            def roots(n, i):
                _, _, was_summed, was_rooted = norm_sems[n]
                act.wait_ge(was_summed, START + i + 1)
                nc.scalar.activation(var[:, n, :], var[:, n, :], ACT.Sqrt, bias=core.eps[0:NT, 0:1],
                                     scale=1.0 / D).then_inc(was_rooted, 1)

            def take_turned(to, turned, taken, i, norm=None):
                for c in range(NC):
                    act.wait_ge(turned, START + NC * i + c + 1)
                    src = bT[0:D, c % 2, 0:wide_of(c)]
                    if norm is None:
                        ins = nc.scalar.copy(to[0:D, cols(c)], src)
                    else:
                        ins = nc.scalar.activation(to[0:D, cols(c)], src, ACT.Identity, bias=affine[:, norm, 1:2],
                                                   scale=affine[:, norm, 0:1])
                    ins.then_inc(taken, 1)

            def embedded(f, u):
                act.wait_ge(h0_made, START + f + 1)
                for b, (n0, n1) in enumerate(((0, BANK), (BANK, K))):
                    ins = nc.scalar.copy(h0[:, u, n0:n1, :].rearrange("p k f -> p (k f)"), bO[0:NT, b, 0:(n1 - n0) * D])
                ins.then_inc(h0_ready, 1)

            def projected(f, u):
                take_turned(xT, x1_turned, x1_taken, f, 0)
                for j in range(K // 2):
                    act.wait_ge(qkv_made, START + 5 * f + j + 1)
                    nc.scalar.copy(qkv[:, u, 2 * j:2 * j + 2, :].rearrange("p k f -> p (k f)"),
                                   bQ[0:NT, j % 2, 0:6 * D]).then_inc(qkv_taken, 1)

            def exponentials(f):
                act.wait_ge(centered, START + f + 1)
                nc.scalar.activation(e[:, :, :, :], e[:, :, :, :], ACT.Exp, scale=float(HD) ** -0.5).then_inc(exp_done, 1)

            def gelu(b, c):
                for m in range(2):
                    act.wait_ge(hidden_made, START + 2 * NC * b + 2 * c + m + 1)
                    if m == 0 and c == 0:
                        act.wait_ge(w2_made, START + NC * b)
                    if m == 0 and c == 2:
                        act.wait_ge(w2_made, START + NC * b + 1)
                    nc.scalar.activation(hidden[:, c % 2, m, 0:wide_of(c)], bH[:, m, 0:wide_of(c)], ACT.Gelu,
                                         bias=b1[:, m:m + 1]).then_inc(hidden_ready, 1)

            def keys_again(b):
                for c in range(NC):
                    act.wait_ge(kv_made, START + NC * b + c + 1)
                    n = len(units(c))
                    if c == 2:
                        nc.scalar.copy(q2[:, :], bQ[0:NT, 0, 4 * D:5 * D])
                    nc.scalar.copy(kv2[:, CHUNKS[c][0]:CHUNKS[c][1], :].rearrange("p k f -> p (k f)"),
                                   bQ[0:NT, c % 2, 0:n * 2 * D]).then_inc(kv_taken, 1)

            def exponentials_again(b):
                act.wait_ge(centered2, START + b + 1)
                nc.scalar.activation(score2[:, :, :], score2[:, :, :], ACT.Exp, scale=float(HD) ** -0.5).then_inc(exp2_done, 1)

            def turn(f, u, last=True, back=True, start=True, embedding=True):
                if start:
                    projected(f + 1, 1 - u)
                exponentials(f)
                if last:
                    exponentials_again(f - 2)
                if back:
                    for c in range(NC):
                        gelu(f - 1, c)
                take_turned(oT, o_turned, o_taken, f)
                if back:
                    squares(2, x3, f - 1)
                squares(1, x2, f)
                if back:
                    roots(2, f - 1)
                roots(1, f)
                if embedding:
                    embedded(f + 2, u)
                if back:
                    take_turned(x3T, x3_turned, x3_taken, f - 1, 2)
                if embedding:
                    squares(0, x1, f + 2)
                    roots(0, f + 2)
                if back:
                    keys_again(f - 1)
                take_turned(x2T, x2_turned, x2_taken, f, 1)

            embedded(0, 0)
            squares(0, x1, 0)
            roots(0, 0)
            projected(0, 0)
            embedded(1, 1)
            squares(0, x1, 1)
            roots(0, 1)
            turn(0, 0, last=False, back=False)
            turn(1, 1, last=False)
            with act.Fori(0, TURNS) as i:
                for f, u in ((i * 2 + 2, 0), (i * 2 + 3, 1)):
                    turn(f, u)
            turn(NB - 2, 0, embedding=False)
            turn(NB - 1, 1, start=False, embedding=False)
            exponentials_again(NB - 2)
            for c in range(NC):
                gelu(NB - 1, c)
            squares(2, x3, NB - 1)
            roots(2, NB - 1)
            take_turned(x3T, x3_turned, x3_taken, NB - 1, 2)
            keys_again(NB - 1)
            exponentials_again(NB - 1)

        @block.vector
        def _(dve):
            def center(n, own_done, src, to):
                own_done(nc.vector.tensor_reduce(mean[:, n, :], src, AX, ALU.add))
                own_done(nc.vector.tensor_scalar(mean[:, n, :], mean[:, n, :], 1.0 / D, None, ALU.mult))
                nc.vector.tensor_tensor(to[:, :, :], src, bc(mean[:, n, :], D, 2), ALU.subtract).then_inc(
                    norm_sems[n][0], 1)

            def sum_squares(n, i):
                _, was_squared, was_summed, _ = norm_sems[n]
                dve.wait_ge(was_squared, START + i + 1)
                nc.vector.tensor_reduce(var[:, n, :], sq[:, n % 2, :, :], AX, ALU.add).then_inc(was_summed, 1)

            def scale(n, own_done, to, i, ready):
                _, _, _, was_rooted = norm_sems[n]
                dve.wait_ge(was_rooted, START + i + 1)
                own_done(nc.vector.reciprocal(var[:, n, :], var[:, n, :]))
                nc.vector.tensor_tensor(to[:, :, :], to[:, :, :], bc(var[:, n, :], D, 2), ALU.mult).then_inc(ready, 1)

            def add_banks(to, src, taken):
                for b, (n0, n1) in enumerate(((0, BANK), (BANK, K))):
                    flat = lambda t: t[:, n0:n1, :].rearrange("p k f -> p (k f)")
                    ins = nc.vector.tensor_tensor(flat(to), flat(src), bO[0:NT, b, 0:(n1 - n0) * D], ALU.add)
                ins.then_inc(taken, 1)

            def attention_scores(f, u, own_done):
                dve.wait_ge(qkv_taken, START + 5 * f + 5)
                for q in range(K):
                    if q not in ON_POOL:
                        ins = query_products(nc.vector, q, u)
                own_done(ins)
                dve.wait_ge(pool_scores, START + f + 1)
                for q in range(K):
                    ins = nc.vector.tensor_reduce(
                        score[:, q, :, 0:q + 1].rearrange("p h k -> p k h"),
                        prod[:, first_pair(q) * D:first_pair(q + 1) * D].rearrange("p (k h f) -> p k h f", h=NH, f=HD),
                        AX, ALU.add)
                own_done(ins)
                own_done(nc.vector.tensor_reduce(maxima[:, :, :], score[:, :, :, :], AX, ALU.max))
                nc.vector.tensor_tensor(e[:, :, :, :], score[:, :, :, :], bc(maxima[:, :, :], K, 3), ALU.subtract).then_inc(
                    centered, 1)

            def attention_values(f, u, own_done):
                dve.wait_ge(exp_done, START + f + 1)
                for q in range(K):
                    if q not in ON_POOL:
                        value_products(nc.vector, q, u)
                own_done(nc.vector.tensor_reduce(sums[:, :, :], e[:, :, :, :], AX, ALU.add))
                own_done(nc.vector.reciprocal(sums[:, :, :], sums[:, :, :]))
                dve.wait_ge(pool_values, START + f + 1)
                dve.wait_ge(o_turned, START + NC * f)
                for q in range(K):
                    ins = nc.vector.tensor_reduce(
                        o[:, q, :],
                        prod[:, first_pair(q) * D:first_pair(q + 1) * D].rearrange("p (f k) -> p f k", f=D),
                        AX, ALU.add)
                own_done(ins)
                heads = o[:, :, :].rearrange("p k (h f) -> p (k h) f", h=NH)
                nc.vector.tensor_tensor(heads, heads, bc(sums[:, :, :].rearrange("p k h -> p (k h)"), HD, 2),
                                        ALU.mult).then_inc(o_ready, 1)

            def residual(f, u, own_done):
                dve.wait_ge(x3_centered, START + f)
                dve.wait_ge(x2_turned, START + NC * f)
                dve.wait_ge(wo_made, START + f + 1)
                add_banks(hb[:, :, :], h0[:, u, :, :], wo_taken)
                dve.wait_ge(wo_taken, START + f + 1)
                center(1, own_done, hb[:, :, :], x2)

            def mlp_residual(b, own_done):
                dve.wait_ge(w2_made, START + NC * b + NC)
                dve.wait_ge(b2_added, START + b + 1)
                own_done(nc.vector.tensor_tensor(sequence(core.h, b), hb[:, K - 1, :], at(K - 1), ALU.add))
                add_banks(hb[:, :, :], hb[:, :, :], w2_taken)
                dve.wait_ge(w2_taken, START + b + 1)
                center(2, own_done, hb[:, :, :], x3)

            def last_scores(b, own_done):
                dve.wait_ge(kv_taken, START + NC * b + NC)
                keyed = prod2[:, :].rearrange("p (k f) -> p k f", f=D)
                own_done(nc.vector.tensor_tensor(keyed, kv2[:, :, 0:D], bc(q2[:, :], K, 1), ALU.mult))
                own_done(nc.vector.tensor_reduce(score2[:, :, :].rearrange("p h k -> p k h"),
                                                 prod2[:, :].rearrange("p (k h f) -> p k h f", h=NH, f=HD), AX, ALU.add))
                own_done(nc.vector.tensor_reduce(maxima2[:, :], score2[:, :, :], AX, ALU.max))
                nc.vector.tensor_tensor(score2[:, :, :], score2[:, :, :], bc(maxima2[:, :], K, 2),
                                        ALU.subtract).then_inc(centered2, 1)

            def last_values(b, own_done):
                dve.wait_ge(exp2_done, START + b + 1)
                nc.vector.tensor_tensor(prod2[:, :].rearrange("p (h f k) -> p h f k", h=NH, f=HD),
                                        kv2[:, :, D:2 * D].rearrange("p k (h f) -> p h f k", h=NH),
                                        bc(score2[:, :, :], HD, 2), ALU.mult)
                own_done(nc.vector.tensor_reduce(sums2[:, :], score2[:, :, :], AX, ALU.add))
                own_done(nc.vector.reciprocal(sums2[:, :], sums2[:, :]))
                own_done(nc.vector.tensor_reduce(o2[:, :], prod2[:, :].rearrange("p (f k) -> p f k", f=D), AX, ALU.add))
                nc.vector.tensor_tensor(sequence(core.xn, b).rearrange("p (h f) -> p h f", h=NH),
                                        o2[:, :].rearrange("p (h f) -> p h f", h=NH), bc(sums2[:, :], HD, 2), ALU.mult)

            dve.wait_ge(loaded, 16 * NLOAD)
            dve.wait_ge(set_up, START + 4)

            def start(f, u):
                own_start = InOrder(dve, start_own, f * OWN_START)
                dve.wait_ge(h0_ready, START + f + 1)
                if f is not FIRST:
                    dve.wait_ge(x1_turned, START + NC * f)
                center(0, own_start, h0[:, u, :, :], x1)
                sum_squares(0, f)
                scale(0, own_start, x1, f, x1_ready)
                assert own_start.n == OWN_START, own_start.n

            def last_attention(b):
                own_last = InOrder(dve, last_own, b * OWN_LAST)
                last_scores(b, own_last)
                last_values(b, own_last)
                assert own_last.n == OWN_LAST, own_last.n

            def turn(f, u, last=True, back=True, starting=True):
                own_front = InOrder(dve, front_own, f * OWN_FRONT)
                own_back = InOrder(dve, back_own, (f - 1) * OWN_BACK if back else 0)
                own_last = InOrder(dve, last_own, (f - 2) * OWN_LAST if last else 0)
                if starting:
                    start(f + 1, 1 - u)
                attention_scores(f, u, own_front)
                if last:
                    last_scores(f - 2, own_last)
                attention_values(f, u, own_front)
                if last:
                    last_values(f - 2, own_last)
                    assert own_last.n == OWN_LAST, own_last.n
                if back:
                    mlp_residual(f - 1, own_back)
                residual(f, u, own_front)
                if back:
                    sum_squares(2, f - 1)
                sum_squares(1, f)
                if back:
                    scale(2, own_back, x3, f - 1, x3_ready)
                    assert own_back.n == OWN_BACK, own_back.n
                scale(1, own_front, x2, f, x2_ready)
                assert own_front.n == OWN_FRONT, own_front.n

            start(FIRST, 0)
            turn(0, 0, last=False, back=False)
            turn(1, 1, last=False)
            with dve.Fori(0, TURNS) as i:
                for f, u in ((i * 2 + 2, 0), (i * 2 + 3, 1)):
                    turn(f, u)
            turn(NB - 2, 0)
            turn(NB - 1, 1, starting=False)
            last_attention(NB - 2)
            own_back = InOrder(dve, back_own, (NB - 1) * OWN_BACK)
            mlp_residual(NB - 1, own_back)
            sum_squares(2, NB - 1)
            scale(2, own_back, x3, NB - 1, x3_ready)
            last_attention(NB - 1)


def last_slot(core, name):
    nc, aps = core.nc, core.aps
    with ExitStack() as ctx:
        sem = Semaphores(nc, ctx, name)
        sb = lambda n, shape: ctx.enter_context(nc.sbuf_tensor(f"{name}_{n}", shape, F32))
        wo, w1, w2, wout = sb("wo", [65, D]), sb("w1", [D, 2, 128]), sb("w2", [128, 2, D]), sb("wout", [65, D])
        b1, b2, affine = sb("b1", [128, 2]), sb("b2", [NT, D]), sb("affine", [D, 2])
        xg, hs, x, sq = ([sb(f"{n}{u}", [NT, GS, D]) for u in range(2)] for n in ("xg", "hs", "x", "sq"))
        mean, var, carrier = ([sb(f"{n}{u}", [NT, GS]) for u in range(2)] for n in ("mean", "var", "carrier"))
        xT, x2T = ([sb(f"{n}{u}", [rows, GT]) for u in range(2)] for n, rows in (("xT", 65), ("x2T", D)))
        hidden = [sb(f"hidden{u}", [128, 2, GT]) for u in range(2)]
        ps = lambda n, shape: ctx.enter_context(nc.psum_tensor(f"{name}_{n}", shape, F32))
        bA, bB = ([ps(f"{n}{u}", [128, 512]) for u in range(2)] for n in ("bA", "bB"))
        bH = [ps(f"bH{u}", [128, 2, 512]) for u in range(2)]
        loaded, set_up, own, inverted = (sem(n) for n in ("loaded", "set_up", "own", "inverted"))
        (xg_ready, o_turned, o_taken, wo_made, centered, squared, summed, rooted, x_ready, x_turned, x_taken) = (
            sem(n) for n in ("xg_ready", "o_turned", "o_taken", "wo_made", "centered", "squared", "summed", "rooted",
                             "x_ready", "x_turned", "x_taken"))
        hidden_made, hidden_ready, w2_made, h_ready, h_turned, h_taken, z_made, z_taken = (
            sem(n) for n in ("hidden_made", "hidden_ready", "w2_made", "h_ready", "h_turned", "h_taken", "z_made",
                             "z_taken"))
        sem.start()
        block = ctx.enter_context(nc.Block())
        NLOAD = 7
        OWN = 4
        of = lambda s: slice(s * NT, (s + 1) * NT)

        @block.sync
        def _(sp):
            for to, what in ((wo, "wo"), (w1, "w1"), (w2, "w2"), (wout, "wout"), (b1, "b1"), (affine, "affine")):
                sp.dma_start(to[:], aps[f"{name}_{what}"]).then_inc(loaded, 16)
            sp.dma_start(b2[:, :], aps[f"{name}_b2"].partition_broadcast(NT)).then_inc(loaded, 16)

        @block.gpsimd
        def _(pool):
            for u in range(2):
                nc.gpsimd.memset(xT[u][D:D + 1, :], 1.0).then_inc(set_up, 1)
                pool.wait_ge(set_up, START + u + 1)

            def copy_context(g, u):
                pool.wait_ge(o_turned, START + g - u)
                nc.gpsimd.tensor_copy(xg[u][:, :, :], core.xn[:, bass.ds(g * GS, GS), :]).then_inc(xg_ready, 1)

            with pool.Fori(0, NG // 2) as i:
                for step in (copy_context,):
                    for u in range(2):
                        step(i * 2 + u, u)

        @block.tensor
        def _(pe):
            pe.wait_ge(loaded, 16 * NLOAD)
            pe.wait_ge(set_up, START + 2)

            def turn_context(g, u):
                pe.wait_ge(xg_ready, START + g + 1)
                transpose_each(core, bA[u], xg[u], D).then_inc(o_turned, 1)

            def context_out(g, u):
                pe.wait_ge(o_taken, START + g + 1)
                pe.wait_ge(z_taken, START + g - u)
                for s in range(GS):
                    mm = nc.tensor.matmul(bB[u][0:NT, s * D:(s + 1) * D], xT[u][:, of(s)], wo[:, :], start=True, stop=True)
                mm.then_inc(wo_made, 1)

            def turn_normed(g, u):
                pe.wait_ge(x_ready, START + g + 1)
                transpose_each(core, bA[u], x[u], D).then_inc(x_turned, 1)

            def first_matrix(g, u):
                pe.wait_ge(x_taken, START + g + 1)
                for m in range(2):
                    nc.tensor.matmul(bH[u][:, m, 0:GT], w1[:, m, :], x2T[u][:, :], start=True, stop=True).then_inc(hidden_made, 1)

            def second_matrix(g, u):
                pe.wait_ge(hidden_ready, START + 2 * g + 2)
                for s in range(GS):
                    for m in range(2):
                        mm = nc.tensor.matmul(bB[u][0:NT, s * D:(s + 1) * D], hidden[u][:, m, of(s)], w2[:, m, :],
                                              start=(m == 0), stop=(m == 1))
                mm.then_inc(w2_made, 1)

            def turn_h(g, u):
                pe.wait_ge(h_ready, START + g + 1)
                transpose_each(core, bA[u], x[u], D).then_inc(h_turned, 1)

            def project_out(g, u):
                pe.wait_ge(h_taken, START + g + 1)
                for s in range(GS):
                    mm = nc.tensor.matmul(bB[u][0:NT, s * D:(s + 1) * D], xT[u][:, of(s)], wout[:, :], start=True, stop=True)
                mm.then_inc(z_made, 1)

            with pe.Fori(0, NG // 2) as i:
                for step in (turn_context, context_out, turn_normed, first_matrix, second_matrix, turn_h, project_out):
                    for u in range(2):
                        step(i * 2 + u, u)

        @block.scalar
        def _(act):
            act.wait_ge(loaded, 16 * NLOAD)
            act.wait_ge(set_up, START + 2)

            def take_context(g, u):
                act.wait_ge(o_turned, START + g + 1)
                nc.scalar.copy(xT[u][0:D, :], bA[u][0:D, 0:GT]).then_inc(o_taken, 1)

            def squares(g, u):
                act.wait_ge(centered, START + g + 1)
                nc.scalar.activation(sq[u][:, :, :], x[u][:, :, :], ACT.Square).then_inc(squared, 1)

            def roots(g, u):
                act.wait_ge(summed, START + g + 1)
                nc.scalar.activation(var[u][:, :], var[u][:, :], ACT.Sqrt, bias=core.eps[0:NT, 0:1],
                                     scale=1.0 / D).then_inc(rooted, 1)

            def take_normed(g, u):
                act.wait_ge(x_turned, START + g + 1)
                nc.scalar.activation(x2T[u][:, :], bA[u][0:D, 0:GT], ACT.Identity, bias=affine[:, 1:2],
                                     scale=affine[:, 0:1]).then_inc(x_taken, 1)

            def gelu(g, u):
                for m in range(2):
                    act.wait_ge(hidden_made, START + 2 * g + m + 1)
                    nc.scalar.activation(hidden[u][:, m, :], bH[u][:, m, 0:GT], ACT.Gelu, bias=b1[:, m:m + 1]).then_inc(hidden_ready, 1)

            def take_h(g, u):
                act.wait_ge(h_turned, START + g + 1)
                nc.scalar.copy(xT[u][0:D, :], bA[u][0:D, 0:GT]).then_inc(h_taken, 1)

            with act.Fori(0, NG // 2) as i:
                for step in (take_context, squares, roots, take_normed, gelu, take_h):
                    for u in range(2):
                        step(i * 2 + u, u)

        @block.vector
        def _(dve):
            dve.wait_ge(loaded, 16 * NLOAD)
            group = lambda g: core.h[:, bass.ds(g * GS, GS), :]
            made = lambda u: bB[u][0:NT, 0:GS * D].rearrange("p (s f) -> p s f", s=GS)

            def center(g, u):
                own_done = InOrder(dve, own, g * OWN)
                dve.wait_ge(wo_made, START + g + 1)
                own_done(nc.vector.tensor_tensor(hs[u][:, :, :], group(g), made(u), ALU.add))
                own_done(nc.vector.tensor_reduce(mean[u][:, :], hs[u][:, :, :], AX, ALU.add))
                own_done(nc.vector.tensor_scalar(mean[u][:, :], mean[u][:, :], 1.0 / D, None, ALU.mult))
                nc.vector.tensor_tensor(x[u][:, :, :], hs[u][:, :, :], bc(mean[u][:, :], D, 2), ALU.subtract).then_inc(centered, 1)
                own_done(nc.vector.tensor_tensor(hs[u][:, :, :], hs[u][:, :, :], bc(b2[:, :], GS, 1), ALU.add))
                assert own_done.n == OWN, own_done.n

            def sum_squares(g, u):
                dve.wait_ge(squared, START + g + 1)
                nc.vector.tensor_reduce(var[u][:, :], sq[u][:, :, :], AX, ALU.add).then_inc(summed, 1)

            def scale(g, u):
                dve.wait_ge(rooted, START + g + 1)
                nc.vector.reciprocal(var[u][:, :], var[u][:, :]).then_inc(inverted, 1)
                dve.wait_ge(inverted, START + g + 1)
                nc.vector.tensor_tensor(x[u][:, :, :], x[u][:, :, :], bc(var[u][:, :], D, 2), ALU.mult).then_inc(x_ready, 1)

            def residual(g, u):
                dve.wait_ge(w2_made, START + g + 1)
                nc.vector.tensor_tensor(x[u][:, :, :], hs[u][:, :, :], made(u), ALU.add).then_inc(h_ready, 1)

            def keep(g, u):
                dve.wait_ge(z_made, START + g + 1)
                nc.vector.memset(carrier[u][0:1, 0:1], 0.0)
                nc.vector.tensor_copy(group(g), made(u)).then_inc(z_taken, 1)

            with dve.Fori(0, NG // 2) as i:
                for step in (center, sum_squares, scale, residual, keep):
                    for u in range(2):
                        step(i * 2 + u, u)


def program(nc, aps, out):
    with ExitStack() as ctx:
        core = Core(nc, ctx, aps)
        constants(core)
        window_encoder(core, "L0t")
        last_slot(core, "L0z")
        layer_norm(core, "L0a_ln")
        window_attention(core, "L0a", True)
        layer_norm(core, "L0f_ln")
        experts(core, "L0f", 16, 128, True)
        add_normed(core, "L0f")
        layer_norm(core, "L1a_ln")
        window_attention(core, "L1a", False)
        layer_norm(core, "L1f_ln")
        experts(core, "L1f", 64, 128, False)
        layer_norm(core, "L2a_ln")
        phase_attention(core, "L2a")
        layer_norm(core, "L2f_ln")
        expert_heads(core, "L2f")
        layer_norm(core, "L3a_ln")
        lattice_attention(core, "L3a")
        layer_norm(core, "L3f_ln")
        tree_experts(core, "L3f")
        sem = Semaphores(nc, ctx, "out")
        stored = sem("stored")
        sem.start()
        block = ctx.enter_context(nc.Block())

        @block.sync
        def _(sp):
            sp.dma_start(out.rearrange("b t d -> t b d"), core.h[:, :, :]).then_inc(stored, 16)
            sp.wait_ge(stored, 16)


def laid_out(inputs):
    a = {k: np.asarray(v) for k, v in inputs.items()}
    out = {}
    f = np.float32
    tok = np.arange(NT)
    out["headmask8"] = (np.arange(D)[:, None] // 8 == np.arange(8)[None, :]).astype(f)
    out["onehot7"] = np.tile((tok[None, :] % 7 == np.arange(7)[:, None]).astype(f), (1, GS))
    rel = (tok[None, :] - tok[:, None]).astype(f)
    out["posrel"] = np.stack([rel, np.zeros_like(rel), rel * rel], axis=1)

    def under(w, b):
        return np.concatenate([w, b[None, :]], axis=0)

    t = {k: a[f"L0_tok_{k}"] for k in ("w_in", "b_in", "wqkv", "bqkv", "wo", "bo", "w1", "b1", "w2", "b2", "ln1_g",
                                       "ln1_b", "ln2_g", "ln2_b", "w_out", "b_out")}
    K = 10
    frames = np.ones((34, NB, NT + K - 1), f)
    frames[:32, :, :K - 1] = 0
    frames[:32, :, K - 1:] = a["x"][:, :NT].transpose(2, 0, 1)
    out["L0t_frames"] = frames
    angle = np.arange(K)[:, None] * np.exp(np.arange(0, D, 2) * (-math.log(10000.0) / D))
    slots_pe = np.stack([np.sin(angle), np.cos(angle)], axis=-1).reshape(K, D).astype(f)
    out["L0t_win"] = np.concatenate([np.broadcast_to(under(t["w_in"], t["b_in"])[:, None, :], (33, K, D)), slots_pe[None]])
    affine = lambda *names: np.stack([np.stack([t[f"{n}_g"][l], t[f"{n}_b"][l]], axis=-1) for n, l in names], axis=1)
    out["L0t_wqkv"], out["L0t_wqkv2"] = (under(t["wqkv"][l], t["bqkv"][l]) for l in range(2))
    out["L0t_affine"] = affine(("ln1", 0), ("ln2", 0), ("ln1", 1))
    out["L0z_affine"] = affine(("ln2", 1))[:, 0]
    out["L0z_wout"] = under(t["w_out"], t["b_out"])
    for l, name in enumerate(("L0t", "L0z")):
        out[f"{name}_wo"] = under(t["wo"][l], t["bo"][l])
        out[f"{name}_w1"] = t["w1"][l].reshape(D, 2, 128)
        out[f"{name}_b1"] = t["b1"][l].reshape(2, 128).T
        out[f"{name}_w2"] = t["w2"][l].reshape(2, 128, D).transpose(1, 0, 2)
        out[f"{name}_b2"] = t["b2"][l]
    out["L0a_wqkv"] = under(a["L0_attn_qkv_w"].T, a["L0_attn_qkv_b"])
    out["L0a_wproj"] = under(a["L0_attn_proj_w"].T, a["L0_attn_proj_b"])
    bias = a["L0_attn_bias_table"][np.arange(7)[:, None] - (tok % 7)[None, :] + 6]
    out["L0a_bias7"] = np.repeat(bias[:, None, :], 8, axis=1)
    out["L1a_wqkv"] = under(np.concatenate([a["L1_attn_Wqk"], a["L1_attn_Wv"]], axis=0).T, np.zeros(3 * D, f))
    out["L1a_wproj"] = under(a["L1_attn_Wproj"].T, a["L1_attn_bproj"])
    out["L1a_wpos"] = a["L1_attn_Wpos"].T
    out["L1a_bpos"] = a["L1_attn_bpos"]
    out["L1a_gating"] = a["L1_attn_gating"]

    def mixture(name, wr, br, w1, b1, w2, b2):
        E, _, F = w1.shape
        out[f"{name}_wr"], out[f"{name}_br"], out[f"{name}_b2"] = wr, br, b2
        out[f"{name}_w1"] = w1.reshape(E // 2, 2, D, F).transpose(0, 2, 1, 3).reshape(E // 2, D, 2 * F)
        out[f"{name}_b1"] = b1.reshape(E // 2, 2, F).transpose(0, 2, 1)
        out[f"{name}_w2"] = w2.reshape(E // 2, 2, F, D).transpose(0, 2, 1, 3).reshape(E // 2, F, 2 * D)
        out[f"iota{E}"] = np.arange(E, dtype=f)

    mixture("L0f", *(a[f"L0_ffn_{k}"] for k in ("gate_w", "gate_b", "w1", "b1", "w2", "b2")))
    mixture("L1f", *(a[f"L1_ffn_{k}"] for k in ("Wr", "br", "W1", "b1", "W2", "b2")))
    out["L0f_affine"] = np.stack([a["L0_ffn_gamma"], a["L0_ffn_beta"]])
    out["L3a_wqkv"] = under(np.concatenate([a[f"L3_attn_W{k}"] for k in "qkv"], axis=1),
                            np.concatenate([a[f"L3_attn_b{k}"] for k in "qkv"]))
    out["L3a_wo"], out["L3a_bo"] = a["L3_attn_Wo"], a["L3_attn_bo"][None, :]
    def slots(w):
        return np.concatenate([np.zeros_like(w[:1]), w], axis=0)

    out["L3f_w1"] = under(slots(a["L3_ffn_w1s"]).T, slots(a["L3_ffn_b1s"]))
    out["L3f_w2"] = slots(a["L3_ffn_w2s"]).transpose(1, 0, 2).reshape(D, 256 * D)
    out["L3f_b2"] = slots(a["L3_ffn_b2s"])
    p = {k: a[f"L2_attn_{k}"] for k in ("Wk1", "bk1", "Wk2", "bk2", "Wq1", "bq1", "Wq2", "bq2", "Wvc", "bvc", "Wvp",
                                        "bvp", "Wg1", "bg1", "Wg2", "bg2", "ln_g", "ln_b", "Wo", "bo")}
    side = lambda *w: np.concatenate(w, axis=-1)
    out["L2a_wkq1"] = under(side(p["Wk1"], p["Wq1"]), side(p["bk1"], p["bq1"]))
    out["L2a_wv"] = under(side(p["Wvc"], p["Wvp"]), side(p["bvc"], p["bvp"]))
    out["L2a_wg1"], out["L2a_wg2"] = under(p["Wg1"], p["bg1"]), under(p["Wg2"], p["bg2"])
    out["L2a_wo"] = under(p["Wo"], p["bo"])
    k2, q2 = side(p["Wk2"], p["Wk2"]), side(p["Wq2"], p["Wq2"])
    out["L2a_w2"] = np.stack([np.concatenate([k2, np.zeros_like(k2)]), np.concatenate([np.zeros_like(q2), q2])], axis=1)
    out["L2a_b2"] = np.stack([side(p["bk2"], p["bk2"]), side(p["bq2"], p["bq2"])], axis=1)
    out["L2a_affine"] = np.stack([p["ln_g"], p["ln_b"]])
    out["L2a_base_phases"] = a["L2_attn_base_phases"][:NT]
    out["upto"] = np.triu(np.ones((NT, NT), f))
    out["position_scale"] = np.stack([1 / np.sqrt(tok + 1.0), 1 / np.sqrt((tok + 1.0) * 32)], axis=1).astype(f)
    p = {k: a[f"L2_ffn_{k}"] for k in ("hl_w", "hl_b", "wq", "wk", "wv", "gate_w", "gate_b", "ln_g", "ln_b", "fc1_w",
                                       "fc1_b", "fc2_w", "fc2_b", "fnorm_g", "fnorm_b", "fgate_w")}

    def diagonal(blocks):
        n, r, c = blocks.shape
        m = np.zeros((n, r, n, c), blocks.dtype)
        for k in range(n):
            m[k, :, k, :] = blocks[k]
        return m.reshape(n * r, n * c)

    out["L2f_whl"] = under(p["hl_w"].reshape(D, D).T, p["hl_b"].reshape(D))
    out["L2f_wqk"] = np.stack([diagonal(p["wq"][:, e].transpose(0, 2, 1)) for e in range(4)]
                              + [diagonal(p["wk"].transpose(0, 2, 1))], axis=1)
    out["L2f_wv"] = diagonal(p["wv"].transpose(0, 2, 1))
    out["L2f_wgate"] = diagonal(p["gate_w"].transpose(0, 2, 1)).reshape(2, 128, 16).transpose(1, 0, 2)
    out["L2f_bgate"] = p["gate_b"].reshape(16)
    out["L2f_wfc1"] = under(diagonal(np.stack([p["fc1_w"].T] * 4)), np.tile(p["fc1_b"], 4))
    out["L2f_wfc2"] = under(diagonal(np.stack([p["fc2_w"].T] * 4)), np.tile(p["fc2_b"], 4))
    out["L2f_wfg"] = p["fgate_w"].T
    out["L2f_affine"] = np.stack([p["ln_g"], p["ln_b"], p["fnorm_g"], p["fnorm_b"]])
    out["headmask4"] = (np.arange(D)[:, None] // 16 == np.arange(4)[None, :]).astype(f)
    out["future"] = np.where(tok[None, :] > tok[:, None], f(-3.0e38), f(0))
    return {k: np.ascontiguousarray(v) for k, v in out.items()}


def kernel(**inputs):
    import concourse.bacc as _bacc
    from concourse.bass_utils import run_bass_kernel_spmd as _run

    nc = _bacc.Bacc("TRN2", target_bir_lowering=False, num_devices=1)
    arrays = laid_out(inputs)
    aps = {n: nc.dram_tensor(f"in_{n}", v.shape, mybir.dt.from_np(v.dtype), kind="ExternalInput").ap()
           for n, v in arrays.items()}
    out = nc.dram_tensor("out_0", (NB, NT, D), F32, kind="ExternalOutput").ap()
    program(nc, aps, out)
    r = _run(nc, [{f"in_{n}": v for n, v in arrays.items()}], core_ids=[0])
    return r.results[0]["out_0"]
```
